# Optimizing a Trainium2 kernel written in Bass

```python
import numpy as np
import jax
import jax.numpy as jnp

def _softmax(x, axis=-1):
    return jax.nn.softmax(x, axis=axis)

def _gelu(x):
    return jax.nn.gelu(x, approximate=True)

def _silu(x):
    return jax.nn.silu(x)

def _sigmoid(x):
    return jax.nn.sigmoid(x)

def _layernorm(x, axis=-1, eps=1e-05):
    m = jnp.mean(x, axis=axis, keepdims=True)
    v = jnp.var(x, axis=axis, keepdims=True)
    return (x - m) / jnp.sqrt(v + eps)

def _scatter_add(tgt, idx, src, axis=0):
    return tgt.at[idx].add(src)

def _segment_sum(src, seg, n):
    return jax.ops.segment_sum(src, seg, n)
kernel_name = 'mk_perceiver_d1_seqx_r4_b1bd10'

def setup_inputs(seed: int=0):
    np.random.seed(seed)
    _w = jnp.asarray

    def _rec_inputs():
        import jax
        import jax.numpy as jnp
        _rk = jax.random.key(seed)
        x = 0.001912 + 0.9994 * jax.random.normal(jax.random.fold_in(_rk, 1), (32, 64, 256), jnp.float32)
        _lenS = 64 - jax.random.randint(jax.random.fold_in(_rk, 7), (32,), 0, max(1, 64 // 4) + 1, jnp.int32)
        _lenS2 = 1601 - jax.random.randint(jax.random.fold_in(_rk, 8), (32,), 0, max(1, 1601 // 4) + 1, jnp.int32)
        _ctx_1024P = jax.random.normal(jax.random.fold_in(_rk, 11), (32, 16, 256), jnp.float32)
        _ctx_1024c = jax.random.dirichlet(jax.random.fold_in(_rk, 511), 0.3 * jnp.ones((16,), jnp.float32), (32, 1601))
        _ctx_1024t = jnp.einsum('bsk,bkd->bsd', _ctx_1024c, _ctx_1024P)
        _ctx_1024t = _ctx_1024t * jax.lax.rsqrt(jnp.mean(jnp.square(_ctx_1024t)) + 1e-12) * 0.953939
        ctx_1024 = -0.000392918 + 0.999932 * (_ctx_1024t + 0.3 * jax.random.normal(jax.random.fold_in(_rk, 611), (32, 1601, 256), jnp.float32))
        return (x, ctx_1024)
    x, ctx_1024 = _rec_inputs()

    def _L0_xattn_setup():
        import jax, jax.numpy as jnp
        import numpy as np
        DIM = 256
        MEMORY_SIZE = 64
        MEMORY_DIM = 256
        SUMMARY_LEN = 16
        STRIDE = 8
        EPS = 1.1920929e-07

        def _rmsnorm2d(x, w):
            ms = jnp.mean(jnp.square(x), axis=(-2, -1), keepdims=True)
            return x * jax.lax.rsqrt(ms + EPS) * w
        key = jax.random.key(seed)
        ks = jax.random.split(key, 11)
        s = lambda k, shape, scale: jax.random.normal(k, shape, dtype=jnp.float32) * scale
        return {'x': s(ks[0], (4, 1024, DIM), 1.0), 'h': s(ks[1], (4, MEMORY_SIZE, MEMORY_DIM), 1.0), 'ws_w': s(ks[2], (MEMORY_DIM, DIM * SUMMARY_LEN), 0.008), 'sa_wq': s(ks[3], (MEMORY_DIM, MEMORY_DIM), 0.03), 'sa_wk': s(ks[4], (MEMORY_DIM, MEMORY_DIM), 0.03), 'sa_wv': s(ks[5], (MEMORY_DIM, MEMORY_DIM), 0.03), 'qa_q': s(ks[6], (MEMORY_SIZE, MEMORY_DIM), 1.0), 'qa_wk': s(ks[7], (MEMORY_DIM, MEMORY_DIM), 0.03), 'qa_wv': s(ks[8], (MEMORY_DIM, MEMORY_DIM), 0.03), 'mn_w': s(ks[9], (MEMORY_SIZE, MEMORY_DIM), 1.0), 'hn_w': s(ks[10], (MEMORY_SIZE, MEMORY_DIM), 1.0)}
    _L0_xattn_all = _L0_xattn_setup()
    _L0_xattn_in = {k: v for k, v in _L0_xattn_all.items() if k in ('ws_w', 'sa_wq', 'sa_wk', 'sa_wv', 'qa_q', 'qa_wk', 'qa_wv', 'mn_w', 'hn_w')}
    del _L0_xattn_all

    def _L0_attn_setup():
        import jax, jax.numpy as jnp
        import numpy as np
        B, N, C, H = (4, 1024, 256, 16)
        D = C // H
        LN_EPS = 1e-05
        key = jax.random.key(seed)
        ks = jax.random.split(key, 20)
        s = 0.02
        inp = {'x': jax.random.normal(ks[0], (B, N, C), jnp.float32)}
        for i, nm in enumerate(['q', 'k1', 'k2', 'v1', 'v2']):
            inp[f'W{nm}'] = jax.random.normal(ks[1 + i], (C, C), jnp.float32) * s
            inp[f'b{nm}'] = jnp.zeros((C,), jnp.float32)
        for i in range(4):
            inp[f'g{i + 1}'] = jax.random.normal(ks[10 + i], (H,), jnp.float32) * 0.5
        inp['ln_g'] = jnp.ones((C,), jnp.float32)
        inp['ln_b'] = jnp.zeros((C,), jnp.float32)
        inp['Wo'] = jax.random.normal(ks[14], (C, C), jnp.float32) * s
        inp['bo'] = jnp.zeros((C,), jnp.float32)
        return inp
    _L0_attn_all = _L0_attn_setup()
    _L0_attn_in = {k: v for k, v in _L0_attn_all.items() if k in ('Wq', 'bq', 'Wk1', 'bk1', 'Wk2', 'bk2', 'Wv1', 'bv1', 'Wv2', 'bv2', 'g1', 'g2', 'g3', 'g4', 'ln_g', 'ln_b', 'Wo', 'bo')}
    del _L0_attn_all

    def _L0_ffn_setup():
        import jax, jax.numpy as jnp
        import numpy as np
        SWIGLU_ALPHA = 1.702
        SWIGLU_LIMIT = 7.0
        TOP_K = 4
        key = jax.random.key(seed)
        k = jax.random.split(key, 5)
        B, S, D, E, I = (2, 256, 256, 8, 512)
        return {'hidden_states': jax.random.normal(k[0], (B, S, D), dtype=jnp.float32), 'router_weight': jax.random.normal(k[1], (E, D), dtype=jnp.float32) * 0.02, 'router_bias': jnp.zeros((E,), dtype=jnp.float32), 'gate_up_proj': jax.random.normal(k[2], (E, 2 * I, D), dtype=jnp.float32) * 0.02, 'gate_up_proj_bias': jnp.zeros((E, 2 * I), dtype=jnp.float32), 'down_proj': jax.random.normal(k[3], (E, D, I), dtype=jnp.float32) * 0.02, 'down_proj_bias': jnp.zeros((E, D), dtype=jnp.float32)}
    _L0_ffn_all = _L0_ffn_setup()
    _L0_ffn_in = {k: v for k, v in _L0_ffn_all.items() if k in ('router_weight', 'router_bias', 'gate_up_proj', 'gate_up_proj_bias', 'down_proj', 'down_proj_bias')}
    del _L0_ffn_all
    return {'x': x, 'ctx_1024': ctx_1024, 'L0_xattn_ws_w': _L0_xattn_in['ws_w'], 'L0_xattn_sa_wq': _L0_xattn_in['sa_wq'], 'L0_xattn_sa_wk': _L0_xattn_in['sa_wk'], 'L0_xattn_sa_wv': _L0_xattn_in['sa_wv'], 'L0_xattn_qa_q': _L0_xattn_in['qa_q'], 'L0_xattn_qa_wk': _L0_xattn_in['qa_wk'], 'L0_xattn_qa_wv': _L0_xattn_in['qa_wv'], 'L0_xattn_mn_w': _L0_xattn_in['mn_w'], 'L0_xattn_hn_w': _L0_xattn_in['hn_w'], 'L0_attn_Wq': _L0_attn_in['Wq'], 'L0_attn_bq': _L0_attn_in['bq'], 'L0_attn_Wk1': _L0_attn_in['Wk1'], 'L0_attn_bk1': _L0_attn_in['bk1'], 'L0_attn_Wk2': _L0_attn_in['Wk2'], 'L0_attn_bk2': _L0_attn_in['bk2'], 'L0_attn_Wv1': _L0_attn_in['Wv1'], 'L0_attn_bv1': _L0_attn_in['bv1'], 'L0_attn_Wv2': _L0_attn_in['Wv2'], 'L0_attn_bv2': _L0_attn_in['bv2'], 'L0_attn_g1': _L0_attn_in['g1'], 'L0_attn_g2': _L0_attn_in['g2'], 'L0_attn_g3': _L0_attn_in['g3'], 'L0_attn_g4': _L0_attn_in['g4'], 'L0_attn_ln_g': _L0_attn_in['ln_g'], 'L0_attn_ln_b': _L0_attn_in['ln_b'], 'L0_attn_Wo': _L0_attn_in['Wo'], 'L0_attn_bo': _L0_attn_in['bo'], 'L0_ffn_router_weight': _L0_ffn_in['router_weight'], 'L0_ffn_router_bias': _L0_ffn_in['router_bias'], 'L0_ffn_gate_up_proj': _L0_ffn_in['gate_up_proj'], 'L0_ffn_gate_up_proj_bias': _L0_ffn_in['gate_up_proj_bias'], 'L0_ffn_down_proj': _L0_ffn_in['down_proj'], 'L0_ffn_down_proj_bias': _L0_ffn_in['down_proj_bias']}

def reference(x, ctx_1024, L0_xattn_ws_w, L0_xattn_sa_wq, L0_xattn_sa_wk, L0_xattn_sa_wv, L0_xattn_qa_q, L0_xattn_qa_wk, L0_xattn_qa_wv, L0_xattn_mn_w, L0_xattn_hn_w, L0_attn_Wq, L0_attn_bq, L0_attn_Wk1, L0_attn_bk1, L0_attn_Wk2, L0_attn_bk2, L0_attn_Wv1, L0_attn_bv1, L0_attn_Wv2, L0_attn_bv2, L0_attn_g1, L0_attn_g2, L0_attn_g3, L0_attn_g4, L0_attn_ln_g, L0_attn_ln_b, L0_attn_Wo, L0_attn_bo, L0_ffn_router_weight, L0_ffn_router_bias, L0_ffn_gate_up_proj, L0_ffn_gate_up_proj_bias, L0_ffn_down_proj, L0_ffn_down_proj_bias):
    import jax
    import jax.numpy as jnp

    def _L0_xattn_ref(x, h, ws_w, sa_wq, sa_wk, sa_wv, qa_q, qa_wk, qa_wv, mn_w, hn_w):
        import jax, jax.numpy as jnp
        import numpy as np
        DIM = 256
        MEMORY_SIZE = 64
        MEMORY_DIM = 256
        SUMMARY_LEN = 16
        STRIDE = 8
        EPS = 1.1920929e-07

        def _rmsnorm2d(x, w):
            ms = jnp.mean(jnp.square(x), axis=(-2, -1), keepdims=True)
            return x * jax.lax.rsqrt(ms + EPS) * w
        bsz, seqlen, dim = x.shape
        conv_seqlen = seqlen + STRIDE - (seqlen - SUMMARY_LEN) % STRIDE
        nwin = (conv_seqlen - SUMMARY_LEN) // STRIDE + 1
        seq = jnp.pad(x, ((0, 0), (0, conv_seqlen - seqlen), (0, 0)))
        idx = jnp.arange(nwin)[:, None] * STRIDE + jnp.arange(SUMMARY_LEN)[None, :]
        windows = seq[:, idx, :]
        summary = windows.reshape(bsz, nwin, dim * SUMMARY_LEN)
        summary = jnp.einsum('bnf,mf->bnm', summary, ws_w)
        scale = 1.0 / jnp.sqrt(jnp.float32(MEMORY_DIM))
        xq = jnp.einsum('bnm,hm->bnh', summary, sa_wq)
        xk = jnp.einsum('bnm,hm->bnh', summary, sa_wk)
        xv = jnp.einsum('bnm,hm->bnh', summary, sa_wv)
        sa_scores = jax.nn.softmax(jnp.einsum('bnh,bkh->bnk', xq, xk) * scale, axis=-1)
        att_summary = jnp.einsum('bnk,bkh->bnh', sa_scores, xv)
        qk = jnp.einsum('bnm,hm->bnh', summary, qa_wk)
        qv = jnp.einsum('bnm,hm->bnh', summary, qa_wv)
        q_scores = jax.nn.softmax(jnp.einsum('qh,bnh->bqn', qa_q, qk) * scale, axis=-1)
        memory = jnp.einsum('bqn,bnh->bqh', q_scores, qv)
        h = h + _rmsnorm2d(memory, mn_w)
        return _rmsnorm2d(h, hn_w)

    def _L0_attn_ref(x, Wq, bq, Wk1, bk1, Wk2, bk2, Wv1, bv1, Wv2, bv2, g1, g2, g3, g4, ln_g, ln_b, Wo, bo):
        import jax, jax.numpy as jnp
        import numpy as np
        B, N, C, H = (4, 1024, 256, 16)
        D = C // H
        LN_EPS = 1e-05
        b, n, c = x.shape
        h, d = (H, c // H)

        def proj_heads(W, bb):
            z = x + x @ W.T + bb
            return z.reshape(b, n, h, d).transpose(0, 2, 1, 3)
        q = proj_heads(Wq, bq).astype(jnp.float32)
        k1 = proj_heads(Wk1, bk1).astype(jnp.float32)
        k2 = proj_heads(Wk2, bk2).astype(jnp.float32)
        v1 = proj_heads(Wv1, bv1).astype(jnp.float32)
        v2 = proj_heads(Wv2, bv2).astype(jnp.float32)
        S1 = jnp.einsum('bhnd,bhne->bhde', k1, v1) / n
        S2 = jnp.einsum('bhnd,bhne->bhde', k2, v2) / n
        v1m = v1.mean(axis=2, keepdims=True)
        v2m = v2.mean(axis=2, keepdims=True)
        S12 = S1 * S2
        y1 = q @ S1 * v2m
        y2 = S12.sum(axis=2, keepdims=True)
        y3 = q @ S2 * v1m
        y4 = q @ S12
        gr = lambda g: g.reshape(1, h, 1, 1)
        out = y1 * gr(g1) + y2 * gr(g2) + y3 * gr(g3) + y4 * gr(g4)
        out = out.transpose(0, 2, 1, 3).reshape(b, n, c)
        mu = out.mean(axis=-1, keepdims=True)
        var = jnp.mean((out - mu) ** 2, axis=-1, keepdims=True)
        out = (out - mu) * jax.lax.rsqrt(var + LN_EPS) * ln_g + ln_b
        return out @ Wo.T + bo

    def _L0_ffn_ref(hidden_states, router_weight, router_bias, gate_up_proj, gate_up_proj_bias, down_proj, down_proj_bias):
        import jax, jax.numpy as jnp
        import numpy as np
        SWIGLU_ALPHA = 1.702
        SWIGLU_LIMIT = 7.0
        TOP_K = 4
        B, S, D = hidden_states.shape
        E = router_weight.shape[0]
        x = hidden_states.reshape(-1, D)
        N = x.shape[0]
        logits = x @ router_weight.T + router_bias
        topk_logits, topk_idx = jax.lax.top_k(logits, TOP_K)
        topk_w = jax.nn.softmax(topk_logits.astype(jnp.float32), axis=-1)
        combine = jnp.zeros((N, E), dtype=jnp.float32)
        combine = combine.at[jnp.arange(N)[:, None], topk_idx].set(topk_w)
        gate_up = jnp.einsum('nd,ejd->nej', x, gate_up_proj) + gate_up_proj_bias
        gate, up = jnp.split(gate_up, 2, axis=-1)
        gate = jnp.minimum(gate, SWIGLU_LIMIT)
        up = jnp.clip(up, -SWIGLU_LIMIT, SWIGLU_LIMIT)
        act = (up + 1.0) * gate * jax.nn.sigmoid(SWIGLU_ALPHA * gate)
        out = jnp.einsum('nei,edi->ned', act, down_proj) + down_proj_bias
        y = jnp.einsum('ned,ne->nd', out, combine.astype(out.dtype))
        return y.reshape(B, S, D)
    x = x + _L0_xattn_ref(ctx_1024, _layernorm(x, axis=-1), L0_xattn_ws_w, L0_xattn_sa_wq, L0_xattn_sa_wk, L0_xattn_sa_wv, L0_xattn_qa_q, L0_xattn_qa_wk, L0_xattn_qa_wv, L0_xattn_mn_w, L0_xattn_hn_w)
    x = x + _L0_attn_ref(_layernorm(x, axis=-1), L0_attn_Wq, L0_attn_bq, L0_attn_Wk1, L0_attn_bk1, L0_attn_Wk2, L0_attn_bk2, L0_attn_Wv1, L0_attn_bv1, L0_attn_Wv2, L0_attn_bv2, L0_attn_g1, L0_attn_g2, L0_attn_g3, L0_attn_g4, L0_attn_ln_g, L0_attn_ln_b, L0_attn_Wo, L0_attn_bo)
    x = x + _L0_ffn_ref(_layernorm(x, axis=-1), L0_ffn_router_weight, L0_ffn_router_bias, L0_ffn_gate_up_proj, L0_ffn_gate_up_proj_bias, L0_ffn_down_proj, L0_ffn_down_proj_bias)
    return x

_drawn_inputs = setup_inputs


def setup_inputs(seed=0):
    import zlib

    import numpy as np

    out = dict(_drawn_inputs(seed))
    spreads = {'L0_attn_bq': (0.0, 0.707),
     'L0_attn_bk1': (0.0, 0.8),
     'L0_attn_bk2': (0.0, 0.8),
     'L0_attn_bv1': (0.0, 0.724),
     'L0_attn_bv2': (0.0, 0.645),
     'L0_attn_ln_g': (1.0, 0.2),
     'L0_attn_ln_b': (0.0, 0.375),
     'L0_attn_bo': (0.0, 0.1),
     'L0_ffn_router_bias': (0.0, 0.474),
     'L0_ffn_gate_up_proj_bias': (0.0, 0.8),
     'L0_ffn_down_proj_bias': (0.0, 0.1)}
    factors = {'L0_xattn_qa_q': 2.733,
     'L0_xattn_qa_wk': 2.728,
     'L0_attn_Wk1': 6.552,
     'L0_attn_Wk2': 6.451,
     'L0_attn_Wv1': 5.972,
     'L0_attn_Wv2': 5.697,
     'L0_attn_g3': 3.008}
    for name, (base, spread) in spreads.items():
        noise = np.random.default_rng([zlib.crc32(name.encode()), seed]).standard_normal(out[name].shape)
        drawn = base * np.exp(spread * noise) if base else spread * noise
        out[name] = jnp.asarray(drawn.astype(out[name].dtype))
    for name, factor in factors.items():
        out[name] = (out[name] * factor).astype(out[name].dtype)
    return out
```

```python
import concourse.bass as bass
from concourse import mybir
from contextlib import ExitStack

F32 = mybir.dt.float32
F32R = mybir.dt.float32r
ALU = mybir.AluOpType
ACT = mybir.ActivationFunctionType
AX = mybir.AxisListType

P = 128
B, S, D = 32, 64, 256
CTX = 1601
STRIDE, WIN = 8, 16
NWIN = (CTX + STRIDE - (CTX - WIN) % STRIDE - WIN) // STRIDE + 1
BF = STRIDE * D
NROW = 112
NREST = 96
NBLK = NROW + NREST
NT = 202
PAIRS = B // 2
CH = 4
CF = BF // CH
CT = CF // P
FT = WIN * D // P
DK = D // P
SCALE = 1.0 / D ** 0.5


def hi_lo_products(hi_a, lo_a, hi_b, lo_b):
    return ((hi_a, hi_b), (hi_a, lo_b), (lo_a, hi_b))


H = 16
HD = D // H
E = 8
ROWS = B * S
LN_EPS = 1e-5
RMS_EPS = 1.1920929e-07


def cross_attention(nc, io, rows, mean, rstd, ident):
    ctx = ExitStack()

    def sb(name, shape, dt=F32):
        return ctx.enter_context(nc.sbuf_tensor(name, shape, dt))

    def pb(name):
        return ctx.enter_context(nc.psum_tensor(name, [P, 512], F32))

    def sem(name):
        return ctx.enter_context(nc.semaphore(name))

    with ctx:
        t_raw = [sb(f"t_raw{i}", [P, CT, 2 * NT]) for i in range(2)]
        t_hi = [sb(f"t_hi{i}", [P, CT, 2 * NT], F32R) for i in range(2)]
        t_lo = [sb(f"t_lo{i}", [P, CT, 2 * NT], F32R) for i in range(2)]
        n_raw = [sb(f"n_raw{i}", [NROW, 2, 2, CF]) for i in range(2)]
        n_hi = [sb(f"n_hi{i}", [NROW, 2, CF], F32R) for i in range(2)]
        n_lo = [sb(f"n_lo{i}", [NROW, 2, CF], F32R) for i in range(2)]
        g_hi = sb("g_hi", [P, FT // 2, 2, S], F32R)
        g_lo = sb("g_lo", [P, FT // 2, 2, S], F32R)
        v_hi = sb("v_hi", [P, FT, D], F32R)
        v_lo = sb("v_lo", [P, FT, D], F32R)
        w_hi = [sb(f"w_hi{i}", [P, 2, CT, 2, S], F32R) for i in range(2)]
        w_lo = [sb(f"w_lo{i}", [P, 2, CT, 2, S], F32R) for i in range(2)]
        pt_hi = sb("pt_hi", [NROW, 2, 2, 2, S], F32R)
        pt_lo = sb("pt_lo", [NROW, 2, 2, 2, S], F32R)
        pw = [sb(f"pw{i}", [P, CF]) for i in range(2)]
        prob = sb("prob", [P, 1 + 2 * NROW])
        other = sb("other", [P, NWIN])
        score = sb("score", [P, NWIN])
        top = sb("top", [P, 1])
        ntop = sb("ntop", [P, 1])
        den = sb("den", [P, 1])
        a1 = sb("a1", [P, DK, S])
        mem = sb("mem", [P, D])
        rden = sb("rden", [P, PAIRS])
        rms_w = sb("rms_w", [P, 2, D])
        eps = sb("eps", [P, 2])
        same = sb("same", [P, P])
        square = sb("square", [P, D])
        ss = sb("ss", [P, 2])
        stat = sb("stat", [P, 6])
        mv = sb("mv", [P, 2])
        std = sb("std", [P, 4])
        inv = sb("inv", [P, 3])
        hn = sb("hn", [P, D])
        memw = sb("memw", [P, D])
        ws = rows[:, :, :].rearrange("p (s m x) d -> p s m (x d)", s=2, m=DK)
        qa_q = sb("qa_q_sb", [P, DK, S])
        qa_wk = sb("qa_wk_sb", [P, DK, D])
        qa_wv = sb("qa_wv_sb", [P, DK, D])

        ps_s = pb("ps_s")
        ps_w = [pb(f"ps_w{i}") for i in range(2)]
        ps_v = [pb(f"ps_v{i}") for i in range(2)]
        ps_fold = ps_w + ps_v
        ps_m = pb("ps_m")
        ps_p = pb("ps_p")
        ps_a = pb("ps_a")

        qa_landed = sem("qa_landed")
        ws_landed = [sem(f"ws_landed{i}") for i in range(2)]
        a1_ready = sem("a1_ready")
        a1_copied = sem("a1_copied")
        fold_ready = sem("fold_ready")
        fold_hi = sem("fold_hi")
        fold_lo = sem("fold_lo")
        zeroed = sem("zeroed")
        t_landed = [sem(f"t_landed{i}") for i in range(2)]
        n_landed = [sem(f"n_landed{i}") for i in range(2)]
        t_hi_done = sem("t_hi_done")
        t_lo_done = sem("t_lo_done")
        n_hi_done = sem("n_hi_done")
        n_lo_done = sem("n_lo_done")
        scores_done = sem("scores_done")
        pw_done = sem("pw_done")
        pw_copied = sem("pw_copied")
        turned = sem("turned")
        w_hi_done = sem("w_hi_done")
        w_lo_done = sem("w_lo_done")
        mem_done = sem("mem_done")
        mem_copied = sem("mem_copied")
        other_done = sem("other_done")
        added = sem("added")
        top_done = sem("top_done")
        ntop_done = sem("ntop_done")
        exp_done = sem("exp_done")
        rden_done = sem("rden_done")
        pt_ready = sem("pt_ready")
        pt_hi_done = sem("pt_hi_done")
        pt_lo_done = sem("pt_lo_done")
        x_landed = sem("x_landed")
        s = {n: sem("n_" + n) for n in (
            "sq1 gs1 sd1 st0 mv0 sd0 iv h mw hs sq2 gs2 sd2 iv2 gr x1 st1 mv1 sd3 mu rs").split()}
        block = ctx.enter_context(nc.Block())

        WCH = 4
        WF = WIN * D // WCH
        LAG = CH

        @block.sync
        def _(sp):
            sp.dma_start(qa_q[:, :, :], io["qa_qT"].rearrange("(k p) q -> p k q", p=P)).then_inc(qa_landed, 16)
            sp.dma_start(qa_wk[:, :, :], io["qa_wk"].rearrange("(k p) m -> p k m", p=P)).then_inc(qa_landed, 16)
            sp.dma_start(qa_wv[:, :, :], io["qa_wvT"].rearrange("(k p) h -> p k h", p=P)).then_inc(qa_landed, 16)
            for j in range(WCH):
                if j >= 2:
                    sp.wait_ge(fold_ready, 5 * (j - 1))
                sp.dma_start(ws[:, j % 2], io["ws_w"][:, j * WF:(j + 1) * WF].rearrange("(k p) f -> p k f", p=P))\
                  .then_inc(ws_landed[j % 2], 16)

            def load_t(t, c):
                sp.dma_start(t_raw[c % 2][:, :, :], io["ctxT"][bass.ds(t, 1), c].rearrange("o p k n -> p (o k) n"))\
                  .then_inc(t_landed[c % 2], 16)

            def load_n(t, c):
                for rows, kt in ((NROW, 0), (NREST, 1)):
                    sp.dma_start(n_raw[c % 2][0:rows, kt],
                                 io["ctxN"][bass.ds(2 * t, 2), kt * NROW:kt * NROW + rows, c * CF:(c + 1) * CF]
                                 .rearrange("b p f -> p b f")).then_inc(n_landed[c % 2], 16)

            for i, w in enumerate(("mn_w", "hn_w")):
                for b in range(2):
                    sp.dma_start(rms_w[b * S:(b + 1) * S, i, :], io[w]).then_inc(x_landed, 16)
            for c in range(CH):
                if c >= 2:
                    sp.wait_ge(t_lo_done, c - 1)
                load_t(0, c)
            sp.wait_ge(fold_ready, 20)
            sp.dma_start(rows[:, :, :], io["x"].rearrange("(t b) s d -> (b s) t d", b=2)).then_inc(x_landed, 16)
            sp.wait_ge(zeroed, 3)

            for c in range(CH):
                sp.wait_ge(t_lo_done, CH + c - 1)
                load_t(1, c)
                if c >= 2:
                    sp.wait_ge(n_lo_done, 2 * (c - 1))
                load_n(0, c)
            with sp.Fori(1, PAIRS - 1) as t:
                for c in range(CH):
                    sp.wait_ge(t_lo_done, CH * t + (CH + c - 1))
                    load_t(t + 1, c)
                    sp.wait_ge(n_lo_done, 2 * CH * t + 2 * (c - 1))
                    load_n(t, c)
            for c in range(CH):
                sp.wait_ge(n_lo_done, 2 * CH * (PAIRS - 1) + 2 * (c - 1))
                load_n(PAIRS - 1, c)

        @block.gpsimd
        def _(pool):
            tiles = [n_raw[0][NREST:NROW, 1, :, :], n_raw[1][NREST:NROW, 1, :, :], prob[:, :], ident[:, :]]
            for i, tile in enumerate(tiles):
                pool.memset(tile, 0.0).then_inc(zeroed, 1)
                pool.wait_ge(zeroed, i + 1)
            pool.affine_select(out=ident[:, :], in_=ident[:, :], compare_op=ALU.not_equal, fill=1.0, base=0,
                               pattern=[[-1, P]], channel_multiplier=1).then_inc(zeroed, 1)
            pool.wait_ge(zeroed, 5)
            consts = [(eps[:, 0:1], RMS_EPS), (eps[:, 1:2], LN_EPS), (same[:, :], 0.0), (same[0:S, 0:S], 1.0),
                      (same[S:P, S:P], 1.0)]
            for i, (tile, value) in enumerate(consts):
                pool.memset(tile, value).then_inc(zeroed, 1)
                pool.wait_ge(zeroed, 6 + i)

        def need(eng, name, t, back=0):
            if not (isinstance(t, int) and t < back):
                eng.wait_ge(s[name], t + 1 - back)

        def row(t):
            return rows[:, bass.ds(t, 1), :].rearrange("p o d -> p (o d)")

        def fold_targets(side, i):
            if side == "g":
                j, = i
                at = slice(8 * (j % 2), 8 * (j % 2) + 8)
                return [x[:, at, j // 2, :] for x in (g_hi, g_lo)]
            j, k = i
            return [x[:, 8 * j + 2 * k:8 * j + 2 * k + 2, :] for x in (v_hi, v_lo)]

        def fold_banks():
            n = 0
            for j in range(WCH):
                for side, i in [("g", (j,))] + [("v", (j, k)) for k in range(4)]:
                    yield n, j, side, i
                    n += 1

        def fold_src(n, side):
            return ps_fold[n % 4][:, :].rearrange("p (k q) -> p k q", q=S if side == "g" else D)

        @block.scalar
        def _(act):
            for n, j, side, i in fold_banks():
                act.wait_ge(fold_ready, n + 1)
                act.activation(fold_targets(side, i)[0], fold_src(n, side), ACT.Copy).then_inc(fold_hi, 1)

            def split_t(t, c):
                act.wait_ge(t_landed[c % 2], 16 * (2 * t + (c // 2 + 1)))
                if not (isinstance(t, int) and t == 0 and c < 2):
                    act.wait_ge(scores_done, CH * t + (c - 1))
                act.activation(t_hi[c % 2][:, :, :], t_raw[c % 2][:, :, :], ACT.Copy).then_inc(t_hi_done, 1)

            def split_n(t, c, b):
                if b == 0:
                    act.wait_ge(n_landed[c % 2], 32 * (2 * t + (c // 2 + 1)))
                if not (isinstance(t, int) and t == 0 and c == 0):
                    act.wait_ge(pw_done, 2 * CH * t + (2 * c + b - 1))
                act.activation(n_hi[b][:, :, :], n_raw[c % 2][:, :, b, :], ACT.Copy).then_inc(n_hi_done, 1)

            def copy_pw(t, c, b):
                act.wait_ge(pw_done, 2 * CH * t + (2 * c + b + 1))
                if not (isinstance(t, int) and t == 0 and c == 0):
                    act.wait_ge(turned, 2 * CH * t + (2 * c + b - 1))
                act.activation(pw[b][:, :], ps_w[b][:, :], ACT.Copy).then_inc(pw_copied, 1)

            def copy_w(t, c, b):
                act.wait_ge(turned, 2 * CH * t + (2 * c + b + 1))
                if b == 0 and not (isinstance(t, int) and t == 0 and c < 2):
                    act.wait_ge(mem_done, CH * t + (c - 1))
                act.activation(w_hi[c % 2][:, :, :, b, :].rearrange("p h k q -> p k h q"),
                               ps_v[b][:, :].rearrange("p (k h q) -> p k h q", k=CT, h=2),
                               ACT.Copy).then_inc(w_hi_done, 1)

            def softmax(t):
                act.wait_ge(scores_done, CH * t + CH)
                if not (isinstance(t, int) and t == 0):
                    act.wait_ge(added, 2 * t)
                act.activation(other[0:S, :], ps_s[S:P, 1:1 + NWIN], ACT.Copy).then_inc(other_done, 1)
                act.activation(other[S:P, :], ps_s[0:S, NT:NT + NWIN], ACT.Copy).then_inc(other_done, 1)

            def exponent(t):
                act.wait_ge(ntop_done, t + 1)
                if not (isinstance(t, int) and t == 0):
                    act.wait_ge(pt_ready, t)
                    act.wait_ge(rden_done, t)
                act.activation(prob[:, 1:1 + NWIN], score[:, :], ACT.Exp, bias=ntop[:, :], scale=SCALE,
                               accum_out=den[:, :]).then_inc(exp_done, 1)

            def copy_pt(t):
                act.wait_ge(pt_ready, t + 1)
                if not (isinstance(t, int) and t == 0):
                    act.wait_ge(pw_done, 2 * CH * t)
                act.activation(pt_hi[:, :, :, :, :].rearrange("p k b h q -> p (k b h q)"),
                               ps_p[0:NROW, :], ACT.Copy).then_inc(pt_hi_done, 1)

            def copy_mem(t):
                act.wait_ge(mem_done, CH * t + CH)
                act.wait_ge(rden_done, t + 1)
                need(act, "mw", t, back=1)
                act.activation(mem[:, :], ps_m[:, 0:D], ACT.Copy, scale=rden[:, bass.ds(t, 1)]).then_inc(mem_copied, 1)

            def root(src, dst, which, name, scale=1.0):
                act.activation(std[:, dst:dst + 1], src, ACT.Sqrt, bias=eps[:, which:which + 1], scale=scale)\
                   .then_inc(s[name], 1)

            def norm_a(t):
                act.wait_ge(mem_copied, t + 1)
                need(act, "gs1", t, back=1)
                act.activation(square[:, :], mem[:, :], ACT.Square, accum_out=ss[:, 0:1]).then_inc(s["sq1"], 1)

            def norm_b(t):
                need(act, "gs1", t)
                need(act, "iv", t, back=1)
                root(ps_a[:, 0:1], 0, 0, "sd1", 1.0 / (S * D))
                need(act, "mv0", t)
                root(mv[:, 1:2], 1, 1, "sd0")

            def norm_c(t):
                need(act, "hs", t)
                need(act, "gs2", t, back=1)
                need(act, "sq1", t)
                act.activation(square[:, :], hn[:, :], ACT.Square, accum_out=ss[:, 1:2]).then_inc(s["sq2"], 1)

            def norm_d(t):
                need(act, "gs2", t)
                need(act, "iv2", t, back=1)
                root(ps_a[:, 2:3], 2, 0, "sd2", 1.0 / (S * D))

            def norm_e(t):
                need(act, "mv1", t)
                need(act, "rs", t, back=1)
                root(mv[:, 1:2], 3, 1, "sd3")

            def step(t, ahead, last):
                first = isinstance(t, int) and t == 0
                for c in range(CH):
                    if c:
                        copy_w(t, c - 1, 1)
                    elif not first:
                        copy_w(t - 1, CH - 1, 1)
                    split_n(t, c, 1)
                    if c == CH - 1 and not first:
                        norm_e(t - 1)
                    if c == CH - 1 and not last:
                        softmax(t + 1)
                    if c < CH - 1:
                        if not last:
                            split_t(t + 1, c + 1)
                    elif ahead:
                        split_t(t + 2, 0)
                    if c == 2 and not first:
                        norm_c(t - 1)
                    copy_pw(t, c, 0)
                    if c < CH - 1:
                        split_n(t, c + 1, 0)
                        copy_pw(t, c, 1)
                        copy_w(t, c, 0)
                    else:
                        if not last:
                            exponent(t + 1)
                        copy_pw(t, c, 1)
                        copy_w(t, c, 0)
                        if not last:
                            split_n(t + 1, 0, 0)
                            copy_pt(t + 1)
                    if c == 0 and not first:
                        copy_mem(t - 1)
                    if c < CH - 1 and not first:
                        (norm_a, norm_b, norm_d)[c](t - 1)

            act.wait_ge(zeroed, 10)
            for c in range(CH):
                split_t(0, c)
            split_t(1, 0)
            softmax(0)
            split_n(0, 0, 0)
            exponent(0)
            copy_pt(0)
            step(0, True, False)
            with act.Fori(1, PAIRS - 2) as t:
                step(t, True, False)
            step(PAIRS - 2, False, False)
            step(PAIRS - 1, False, True)
            copy_w(PAIRS - 1, CH - 1, 1)
            copy_mem(PAIRS - 1)
            for norm in (norm_a, norm_b, norm_c, norm_d, norm_e):
                norm(PAIRS - 1)

        @block.vector
        def _(dve):
            dve.wait_ge(a1_ready, 1)
            dve.tensor_copy(a1[:, :, :], ps_a[:, 0:DK * S].rearrange("p (k q) -> p k q", k=DK)).then_inc(a1_copied, 1)
            for n, j, side, i in fold_banks():
                hi, lo = fold_targets(side, i)
                dve.wait_ge(fold_hi, n + 1)
                dve.tensor_tensor(lo, fold_src(n, side), hi.bitcast(F32), ALU.subtract).then_inc(fold_lo, 1)

            def split_t(t, c):
                dve.wait_ge(t_hi_done, CH * t + (c + 1))
                dve.tensor_tensor(t_lo[c % 2][:, :, :], t_raw[c % 2][:, :, :], t_hi[c % 2][:, :, :].bitcast(F32),
                                  ALU.subtract).then_inc(t_lo_done, 1)

            def split_n(t, c, b):
                dve.wait_ge(n_hi_done, 2 * CH * t + (2 * c + b + 1))
                dve.tensor_tensor(n_lo[b][:, :, :], n_raw[c % 2][:, :, b, :], n_hi[b][:, :, :].bitcast(F32),
                                  ALU.subtract).then_inc(n_lo_done, 1)

            def copy_w(t, c, b):
                dve.wait_ge(w_hi_done, 2 * CH * t + (2 * c + b + 1))
                dve.tensor_tensor(w_lo[c % 2][:, :, :, b, :].rearrange("p h k q -> p k h q"),
                                  ps_v[b][:, :].rearrange("p (k h q) -> p k h q", k=CT, h=2),
                                  w_hi[c % 2][:, :, :, b, :].bitcast(F32).rearrange("p h k q -> p k h q"),
                                  ALU.subtract).then_inc(w_lo_done, 1)

            def softmax(t):
                dve.wait_ge(other_done, 2 * t + 2)
                if not (isinstance(t, int) and t == 0):
                    dve.wait_ge(exp_done, t)
                dve.tensor_tensor(score[0:S, :], ps_s[0:S, 0:NWIN], other[0:S, :], ALU.add).then_inc(added, 1)
                dve.tensor_tensor(score[S:P, :], ps_s[S:P, NT + 1:NT + 1 + NWIN], other[S:P, :],
                                  ALU.add).then_inc(added, 1)
                dve.wait_ge(added, 2 * t + 2)
                dve.reduce_max(top[:, :], score[:, :], AX.X).then_inc(top_done, 1)
                dve.wait_ge(top_done, t + 1)
                dve.tensor_scalar(ntop[:, :], top[:, :], -SCALE, None, ALU.mult).then_inc(ntop_done, 1)

            def copy_pt(t):
                dve.wait_ge(exp_done, t + 1)
                dve.reciprocal(rden[:, bass.ds(t, 1)], den[:, :]).then_inc(rden_done, 1)
                dve.wait_ge(pt_hi_done, t + 1)
                dve.tensor_tensor(pt_lo[:, :, :, :, :].rearrange("p k b h q -> p (k b h q)"),
                                  ps_p[0:NROW, :],
                                  pt_hi[:, :, :, :, :].bitcast(F32).rearrange("p k b h q -> p (k b h q)"),
                                  ALU.subtract).then_inc(pt_lo_done, 1)

            def norm_a(t):
                dve.wait_ge(x_landed, 5 * 16)
                need(dve, "mu", t, back=1)
                dve.bn_stats(stat[:, :], row(t)).then_inc(s["st0"], 1)
                dve.wait_ge(x_landed, 5 * 16)
                need(dve, "st0", t)
                dve.bn_aggr(mv[:, :], stat[:, :]).then_inc(s["mv0"], 1)

            def norm_b(t):
                need(dve, "sd1", t)
                need(dve, "sd0", t)
                dve.reciprocal(inv[:, 0:2], std[:, 0:2]).then_inc(s["iv"], 1)
                need(dve, "iv", t)
                dve.tensor_scalar(hn[:, :], row(t), mv[:, 0:1], inv[:, 1:2], ALU.subtract, ALU.mult).then_inc(s["h"], 1)
                dve.scalar_tensor_tensor(memw[:, :], mem[:, :], inv[:, 0:1], rms_w[:, 0, :], ALU.mult, ALU.mult)\
                   .then_inc(s["mw"], 1)
                need(dve, "mw", t)
                dve.tensor_tensor(hn[:, :], hn[:, :], memw[:, :], ALU.add).then_inc(s["hs"], 1)

            def norm_c(t):
                need(dve, "sd2", t)
                dve.reciprocal(inv[:, 2:3], std[:, 2:3]).then_inc(s["iv2"], 1)
                need(dve, "iv2", t)
                dve.scalar_tensor_tensor(memw[:, :], hn[:, :], inv[:, 2:3], rms_w[:, 1, :], ALU.mult, ALU.mult)\
                   .then_inc(s["gr"], 1)
                need(dve, "gr", t)
                dve.tensor_tensor(row(t), row(t), memw[:, :], ALU.add).then_inc(s["x1"], 1)
                dve.wait_ge(x_landed, 5 * 16)
                need(dve, "x1", t)
                dve.bn_stats(stat[:, :], row(t)).then_inc(s["st1"], 1)
                dve.wait_ge(x_landed, 5 * 16)
                need(dve, "st1", t)
                dve.bn_aggr(mv[:, :], stat[:, :]).then_inc(s["mv1"], 1)

            def norm_d(t):
                need(dve, "mv1", t)
                dve.tensor_copy(mean[:, bass.ds(t, 1)], mv[:, 0:1]).then_inc(s["mu"], 1)
                need(dve, "sd3", t)
                dve.reciprocal(rstd[:, bass.ds(t, 1)], std[:, 3:4]).then_inc(s["rs"], 1)

            def step(t, ahead, last):
                first = isinstance(t, int) and t == 0
                for c in range(CH):
                    if c:
                        copy_w(t, c - 1, 1)
                    elif not first:
                        copy_w(t - 1, CH - 1, 1)
                    split_n(t, c, 1)
                    if c == CH - 1 and not first:
                        norm_d(t - 1)
                    if c == CH - 1 and not last:
                        softmax(t + 1)
                    if c < CH - 1:
                        if not last:
                            split_t(t + 1, c + 1)
                    elif ahead:
                        split_t(t + 2, 0)
                    if c < CH - 1:
                        split_n(t, c + 1, 0)
                        copy_w(t, c, 0)
                    else:
                        copy_w(t, c, 0)
                        if not last:
                            split_n(t + 1, 0, 0)
                            copy_pt(t + 1)
                    if c < CH - 1 and not first:
                        (norm_a, norm_b, norm_c)[c](t - 1)

            for c in range(CH):
                split_t(0, c)
            split_t(1, 0)
            softmax(0)
            split_n(0, 0, 0)
            copy_pt(0)
            step(0, True, False)
            with dve.Fori(1, PAIRS - 2) as t:
                step(t, True, False)
            step(PAIRS - 2, False, False)
            step(PAIRS - 1, False, True)
            copy_w(PAIRS - 1, CH - 1, 1)
            for norm in (norm_a, norm_b, norm_c, norm_d):
                norm(PAIRS - 1)

        @block.tensor
        def _(pe):
            pe.wait_ge(qa_landed, 48)
            for m in range(DK):
                for k in range(DK):
                    mm = pe.matmul(ps_a[:, m * S:(m + 1) * S], qa_wk[:, k, m * P:(m + 1) * P], qa_q[:, k, :],
                                   start=k == 0, stop=k == DK - 1)
            mm.then_inc(a1_ready, 1)
            pe.wait_ge(a1_copied, 1)
            for n, j, side, i in fold_banks():
                if side == "g":
                    pe.wait_ge(ws_landed[j % 2], 16 * (j // 2 + 1))
                if n >= 4:
                    pe.wait_ge(fold_lo, n - 3)
                tiles = range(8) if side == "g" else range(2 * i[1], 2 * i[1] + 2)
                rhs = a1 if side == "g" else qa_wv
                width = S if side == "g" else D
                for o, f in enumerate(tiles):
                    for k in range(DK):
                        mm = pe.matmul(ps_fold[n % 4][:, o * width:(o + 1) * width], ws[:, j % 2, k, f * P:(f + 1) * P],
                                       rhs[:, k, :], start=k == 0, stop=k == DK - 1)
                mm.then_inc(fold_ready, 1)

            def scores(t, c):
                pe.wait_ge(t_lo_done, CH * t + (c + 1))
                if c == 0 and not (isinstance(t, int) and t == 0):
                    pe.wait_ge(added, 2 * t)
                for k in range(CT):
                    ft = c * CT + k
                    prods = hi_lo_products(g_hi, g_lo, t_hi[c % 2], t_lo[c % 2])
                    for i, (a, b) in enumerate(prods):
                        mm = pe.matmul(ps_s[:, 0:2 * NT], a[:, ft, :, :], b[:, k, :],
                                       start=ft == 0 and i == 0, stop=ft == CH * CT - 1 and i == 2)
                mm.then_inc(scores_done, 1)

            def blocks(t, c, b):
                if b == 0 and c == 0:
                    pe.wait_ge(pt_lo_done, t + 1)
                pe.wait_ge(n_lo_done, 2 * CH * t + (2 * c + b + 1))
                if not (isinstance(t, int) and t == 0 and c == 0):
                    pe.wait_ge(pw_copied, 2 * CH * t + (2 * c + b - 1))
                i = 0
                for kt in range(2):
                    for x, y in hi_lo_products(pt_hi, pt_lo, n_hi[b], n_lo[b]):
                        mm = pe.matmul(ps_w[b][:, :], x[:, kt, b, :, :], y[:, kt, :], start=i == 0, stop=i == 5)
                        i += 1
                mm.then_inc(pw_done, 1)

            def turn(t, c, b):
                pe.wait_ge(pw_copied, 2 * CH * t + (2 * c + b + 1))
                if not (isinstance(t, int) and t == 0 and c == 0):
                    pe.wait_ge(w_lo_done, 2 * CH * t + (2 * c + b - 1))
                for ft in range(CT):
                    mm = pe.transpose(ps_v[b][:, ft * P:(ft + 1) * P], pw[b][:, ft * P:(ft + 1) * P], ident[:, :])
                mm.then_inc(turned, 1)

            def values(t, c, h):
                if h == 0:
                    pe.wait_ge(w_lo_done, 2 * CH * t + (2 * c + 2))
                    if c == 0 and not (isinstance(t, int) and t == 0):
                        pe.wait_ge(mem_copied, t)
                for k in range(CT):
                    ft = h * CH * CT + c * CT + k
                    for i, (x, y) in enumerate(hi_lo_products(w_hi[c % 2], w_lo[c % 2], v_hi, v_lo)):
                        mm = pe.matmul(ps_m[:, 0:D], x[:, h, k, :, :], y[:, ft, :],
                                       start=c == 0 and h == 0 and k == 0 and i == 0,
                                       stop=c == CH - 1 and h == 1 and k == CT - 1 and i == 2)
                if h:
                    mm.then_inc(mem_done, 1)

            def transpose_prob(t):
                pe.wait_ge(exp_done, t + 1)
                if not (isinstance(t, int) and t == 0):
                    pe.wait_ge(pt_lo_done, t)
                for kt in range(2):
                    for h in range(2):
                        mm = pe.transpose(ps_p[0:NROW, :].rearrange("p (k b h q) -> p k b h q", k=2, b=2, h=2)
                                          [:, kt, :, h, :],
                                          prob[:, 1 - h + kt * NROW:1 - h + (kt + 1) * NROW], ident[:, :])
                mm.then_inc(pt_ready, 1)

            def norm_sum(t, i):
                need(pe, ("sq1", "sq2")[i], t)
                need(pe, ("sd1", "sd2")[i], t, back=1)
                pe.matmul(ps_a[:, 2 * i:2 * i + 1], same[:, :], ss[:, i:i + 1], start=True, stop=True)\
                  .then_inc(s[("gs1", "gs2")[i]], 1)

            def step(t, last):
                first = isinstance(t, int) and t == 0
                for c in range(CH):
                    if not last:
                        scores(t + 1, c)
                    before = (t, c - 1) if c else (t - 1, CH - 1)
                    skip = first and c == 0
                    blocks(t, c, 0)
                    if not skip:
                        values(*before, 0)
                    if c == 1 and not first:
                        norm_sum(t - 1, 0)
                    blocks(t, c, 1)
                    turn(t, c, 0)
                    if c == 2 and not first:
                        norm_sum(t - 1, 1)
                    if not skip:
                        values(*before, 1)
                    turn(t, c, 1)
                if not last:
                    transpose_prob(t + 1)

            pe.wait_ge(fold_lo, 20)
            pe.wait_ge(zeroed, 10)
            for c in range(CH):
                scores(0, c)
            transpose_prob(0)
            step(0, False)
            with pe.Fori(1, PAIRS - 1) as t:
                step(t, False)
            step(PAIRS - 1, True)
            for h in range(2):
                values(PAIRS - 1, CH - 1, h)
            for i in range(2):
                norm_sum(PAIRS - 1, i)


def latent_attention(nc, io, rows, mean, rstd, ident, xt_hi, xt_lo, logits):
    ctx = ExitStack()

    def sb(name, shape, dt=F32):
        return ctx.enter_context(nc.sbuf_tensor("a_" + name, shape, dt))

    def two(name, shape, dt=F32):
        return [sb(f"{name}{i}", shape, dt) for i in range(2)]

    def pb(name):
        return ctx.enter_context(nc.psum_tensor("a_" + name, [P, 512], F32))

    def sem(name):
        return ctx.enter_context(nc.semaphore("a_" + name))

    with ctx:
        eps = sb("ln_eps", [P, 1])
        ind = sb("ind", [P, 2], F32R)
        mask = sb("mask", [P, P])
        ones = sb("ones", [P, P], F32R)
        w_raw = sb("w_raw", [P, DK, 6 * D])
        w_hi = sb("w_hi", [P, DK, 6 * D], F32R)
        w_lo = sb("w_lo", [P, DK, 6 * D], F32R)
        wr_raw = sb("wr_raw", [P, DK, E])
        wr_hi = sb("wr_hi", [P, DK, E], F32R)
        wr_lo = sb("wr_lo", [P, DK, E], F32R)
        NB = 5 * D + E
        bias_raw = sb("bias_raw", [1, NB])
        bias_row = sb("bias_row", [P, NB], F32R)
        cols = sb("cols_sb", [P, 7, DK])
        BQ, G1, G2, G3, G4, LG, LB = range(7)
        stat = sb("stat", [P, 6])
        mv = sb("mv", [P, 2])
        std = sb("std", [P, 1])
        inv = sb("inv", [P, 1])
        fstat = sb("fstat", [P, 6])
        fmv = sb("fmv", [P, 2])
        fstd = sb("fstd", [P, 1])
        finv = sb("finv", [P, 1])
        xn = two("xn", [P, D])
        xa_hi = two("xa_hi", [P, DK, P], F32R)
        xa_lo = two("xa_lo", [P, DK, P], F32R)
        kv_hi = two("kv_hi", [P, 4, D], F32R)
        kv_lo = two("kv_lo", [P, 4, D], F32R)
        q1 = two("q1_", [P, 2, DK, S + 2])
        sm = two("sm", [P, 2, 3, DK, P])
        av = two("av", [P, 2, DK, 2])
        c2 = two("c2_", [P, 2, DK])
        mixed = two("mixed", [P, DK, 2, S])
        on = two("on", [P, D])
        ot_hi = sb("ot_hi", [P, DK, P], F32R)
        ot_lo = sb("ot_lo", [P, DK, P], F32R)
        xf = two("xf", [P, D])
        xr_hi = sb("xr_hi", [P, DK, P], F32R)
        xr_lo = sb("xr_lo", [P, DK, P], F32R)

        ps_t = pb("ps_t")
        ps_kv = [pb("ps_kv0"), pb("ps_kv1")]
        ps_q = pb("ps_q")
        ps_sq = pb("ps_sq")
        ps_o = pb("ps_o")
        ps_d = pb("ps_d")
        ps_e = pb("ps_e")

        landed = sem("w_landed")
        made = sem("made")
        gained = sem("gained")
        bo_ready = sem("bo_ready")
        w_high = sem("w_high")
        w_ready = sem("w_ready")
        s = {n: sem(n) for n in (
            "xn xt xa_h xa_l kv_done kv_h kv_l q_done qc sq sm s12 vm av o c2 m0 m1 m2 tr st mv sd iv on ot ot_h "
            "ot_l wo x2 fst fmv fsd fiv xf xft xr_h xr_l xs lg lgc").split()}
        block = ctx.enter_context(nc.Block())
        NTILE = ROWS // P

        def need(eng, name, t, back=0, per=1, i=None):
            if not (isinstance(t, int) and t < back):
                eng.wait_ge(s[name], per * t + (per if i is None else i + 1) - per * back)

        def ticks(eng, stages):
            deepest = max(lag for lag, _ in stages)
            start = LOOPED

            def tick(n, slot, among):
                for lag, f in stages:
                    if among(lag):
                        f(n - lag, (slot + lag) % 2)

            for n in range(start):
                tick(n, n % 2, lambda lag: n >= lag)
            with eng.Fori(start // 2, NTILE // 2) as i:
                for j in range(2):
                    tick(2 * i + j, j, lambda lag: True)
            for n in range(NTILE, NTILE + deepest):
                tick(n, n % 2, lambda lag: n - lag < NTILE)

        LOOPED = 8

        def o_of(ct, k):
            return ps_o[:, (3 * ct + k) * (S + 2):(3 * ct + k + 1) * (S + 2)]

        def row(t):
            return rows[:, bass.ds(t, 1), :].rearrange("p o d -> p (o d)")

        @block.sync
        def _(sp):
            for i, w in enumerate(("k1", "v1", "k2", "v2", "q", "o")):
                sp.dma_start(w_raw[:, :, i * D:(i + 1) * D], io["W" + w].rearrange("(k p) h -> p k h", p=P))\
                  .then_inc(landed, 16)
            sp.dma_start(bias_raw[:, :], io["bias"]).then_inc(landed, 16)
            sp.dma_start(wr_raw[:, :, :], io["router_w"].rearrange("(k p) e -> p k e", p=P)).then_inc(landed, 16)
            sp.dma_start(cols[:, :, :], io["cols"]).then_inc(landed, 16)

        LANDED = 9 * 16
        MADE = 11

        @block.gpsimd
        def _(pool):
            n = [0]

            def then(ins):
                n[0] += 1
                ins.then_inc(made, 1)
                pool.wait_ge(made, n[0])

            then(pool.memset(eps[:, :], LN_EPS))
            then(pool.memset(ind[:, :].bitcast(F32), 0.0))
            then(pool.memset(ind[0:S, 0:1].bitcast(F32), 1.0 / S))
            then(pool.memset(ind[S:P, 1:2].bitcast(F32), 1.0 / S))
            then(pool.memset(ones[:, :].bitcast(F32), 1.0))
            then(pool.memset(bias_row[:, :].bitcast(F32), 0.0))
            for i in range(2):
                then(pool.memset(q1[i][:, :, :, S:S + 2], 1.0))
            then(pool.memset(mask[:, :], 1.0 / S))
            view = mask[:, :].rearrange("p (j i) -> p j i", i=HD)
            then(pool.affine_select(out=view, in_=view, compare_op=ALU.is_ge, fill=0.0, base=0,
                                    pattern=[[-HD, P // HD], [0, HD]], channel_multiplier=1))
            then(pool.affine_select(out=view, in_=view, compare_op=ALU.is_ge, fill=0.0, base=HD - 1,
                                    pattern=[[HD, P // HD], [0, HD]], channel_multiplier=-1))
            assert n[0] == MADE

            def keep(t, p):
                need(pool, "xr_l", t)
                for src, dst in ((xr_hi, xt_hi), (xr_lo, xt_lo)):
                    pool.tensor_copy(dst[:, :, bass.ds(t * P, P)], src[:, :, :].bitcast(F32)).then_inc(s["xs"], 1)

            with pool.Fori(0, NTILE) as t:
                keep(t, 0)

        @block.scalar
        def _(act):
            act.wait_ge(made, MADE)
            act.wait_ge(gained, 13)
            act.activation(w_hi[:, :, :], w_raw[:, :, :], ACT.Copy).then_inc(w_high, 1)
            act.activation(wr_hi[:, :, :], wr_raw[:, :, :], ACT.Copy).then_inc(w_high, 1)
            act.activation(bias_row[0:1, :], bias_raw[:, :], ACT.Copy).then_inc(w_high, 1)

            def high(dst, src, name):
                act.activation(dst, src, ACT.Copy).then_inc(s[name], 1)

            def transposed(t, p):
                need(act, "xt", t)
                need(act, "q_done", t, back=2)
                high(xa_hi[p][:, :, :], ps_t[:, 0:D].rearrange("p (k r) -> p k r", k=DK), "xa_h")

            def projected(t, p):
                for i in range(2):
                    need(act, "kv_done", t, per=2, i=i)
                    if i == 0:
                        need(act, "vm", t, back=2)
                    high(kv_hi[p][:, 2 * i:2 * i + 2, :], ps_kv[i][:, :].rearrange("p (j d) -> p j d", d=D), "kv_h")
                need(act, "q_done", t)
                need(act, "o", t, back=2, per=2)
                for ct in range(DK):
                    act.activation(q1[p][:, :, ct, 0:S], ps_q[:, ct * P:(ct + 1) * P].rearrange("p (b r) -> p b r", b=2),
                                   ACT.Identity, bias=cols[:, BQ, ct:ct + 1]).then_inc(s["qc"], 1)

            def mix(t, p):
                for b in range(2):
                    need(act, "c2", t, per=2, i=b)
                    if b == 0:
                        need(act, "tr", t, back=2)
                    for ct in range(DK):
                        act.activation(mixed[p][:, ct, b, :], o_of(ct, 2)[:, 0:S], ACT.Identity,
                                       scale=cols[:, G4, ct:ct + 1], bias=c2[p][:, b, ct:ct + 1]).then_inc(s["m0"], 1)

            def norm_mixed(t, p):
                need(act, "mv", t)
                need(act, "iv", t, back=1)
                act.activation(std[:, :], mv[:, 1:2], ACT.Sqrt, bias=eps[:, :]).then_inc(s["sd"], 1)

            def turned(t, p):
                need(act, "ot", t)
                need(act, "wo", t, back=1)
                high(ot_hi[:, :, :], ps_d[:, 0:D].rearrange("p (k r) -> p k r", k=DK), "ot_h")

            def norm_out(t, p):
                need(act, "fmv", t)
                need(act, "fiv", t, back=1)
                act.activation(fstd[:, :], fmv[:, 1:2], ACT.Sqrt, bias=eps[:, :]).then_inc(s["fsd"], 1)

            def routed(t, p):
                need(act, "xft", t)
                need(act, "lg", t, back=1)
                need(act, "xs", t, back=1, per=2)
                high(xr_hi[:, :, :], ps_e[:, 0:D].rearrange("p (k r) -> p k r", k=DK), "xr_h")

            ticks(act, [(1, transposed), (7, routed), (6, turned), (4, mix), (2, projected), (6, norm_out),
                        (5, norm_mixed)])

        @block.vector
        def _(dve):
            def wide(x, shape):
                return x.to_broadcast(shape)

            dve.wait_ge(landed, LANDED)
            n = 0
            for j in range(5):
                for k in range(DK):
                    at = w_raw[:, k, j * D + k * P:j * D + (k + 1) * P]
                    dve.tensor_tensor(at, at, ident[:, :], ALU.add).then_inc(gained, 1)
            dve.wait_ge(bo_ready, 1)
            bo = bias_raw[0:1, 4 * D:5 * D]
            dve.tensor_tensor(bo, bo, ps_e[0:1, 0:D], ALU.add).then_inc(gained, 1)
            for k in range(DK):
                at = w_raw[:, k, 5 * D:6 * D]
                dve.tensor_scalar(at, at, cols[:, LG, k:k + 1], None, ALU.mult).then_inc(gained, 1)
            dve.wait_ge(w_high, 1)
            dve.tensor_tensor(w_lo[:, :, :], w_raw[:, :, :], w_hi[:, :, :].bitcast(F32), ALU.subtract)\
               .then_inc(w_ready, 1)
            dve.wait_ge(w_high, 2)
            dve.tensor_tensor(wr_lo[:, :, :], wr_raw[:, :, :], wr_hi[:, :, :].bitcast(F32), ALU.subtract)\
               .then_inc(w_ready, 1)
            dve.wait_ge(w_high, 3)
            dve.tensor_tensor(bias_row[32:33, :], bias_raw[:, :], bias_row[0:1, :].bitcast(F32), ALU.subtract)\
               .then_inc(w_ready, 1)

            def low(dst, src, hi, name):
                dve.tensor_tensor(dst, src, hi.bitcast(F32), ALU.subtract).then_inc(s[name], 1)

            def norm(t, p):
                need(dve, "xt", t, back=2)
                dve.tensor_scalar(xn[p][:, :], row(t), mean[:, bass.ds(t, 1)], rstd[:, bass.ds(t, 1)], ALU.subtract,
                                  ALU.mult).then_inc(s["xn"], 1)

            def transposed(t, p):
                need(dve, "xa_h", t)
                low(xa_lo[p][:, :, :], ps_t[:, 0:D].rearrange("p (k r) -> p k r", k=DK), xa_hi[p][:, :, :], "xa_l")

            def projected(t, p):
                for i in range(2):
                    need(dve, "kv_h", t, per=2, i=i)
                    low(kv_lo[p][:, 2 * i:2 * i + 2, :], ps_kv[i][:, :].rearrange("p (j d) -> p j d", d=D),
                        kv_hi[p][:, 2 * i:2 * i + 2, :], "kv_l")

            def squares(t, p):
                need(dve, "o", t, back=2, per=2)
                for b in range(2):
                    need(dve, "sq", t, per=2, i=b)
                    dve.tensor_tensor(sm[p][:, b, 0:2, :, :].rearrange("p w c d -> p (w c) d"),
                                      ps_sq[:, :].rearrange("p (w d) -> p w d", d=P),
                                      wide(mask[:, :].rearrange("p (o d) -> p o d", o=1), [P, 4, P]), ALU.mult)\
                       .then_inc(s["sm"], 1)
                    need(dve, "sm", t, per=2, i=b)
                    dve.tensor_tensor(sm[p][:, b, 2, :, :], sm[p][:, b, 0, :, :], sm[p][:, b, 1, :, :], ALU.mult)\
                       .then_inc(s["s12"], 1)
                need(dve, "vm", t)
                for w, g in enumerate((G3, G1)):
                    dve.tensor_tensor(av[p][:, w, :, :],
                                      ps_q[:, D + 4 * w:D + 4 * w + 4].rearrange("p (c b) -> p c b", b=2),
                                      wide(cols[:, g, :].rearrange("p (c o) -> p c o", o=1), [P, DK, 2]), ALU.mult)\
                       .then_inc(s["av"], 1)

            def mix(t, p):
                for b in range(2):
                    need(dve, "o", t, per=2, i=b)
                    dve.tensor_tensor(c2[p][:, b, :],
                                      ps_o[:, 0:6 * (S + 2)].rearrange("p (c k r) -> p c k r", c=DK, k=3)[:, :, 2, S],
                                      cols[:, G2, :], ALU.mult).then_inc(s["c2"], 1)
                    for k, w, got, done in ((0, 1, "m0", "m1"), (1, 0, "m1", "m2")):
                        for ct in range(DK):
                            need(dve, got, t, per=4, i=2 * b + (1 if k == 0 else ct))
                            dve.scalar_tensor_tensor(mixed[p][:, ct, b, :], o_of(ct, k)[:, 0:S],
                                                     av[p][:, w, ct, b:b + 1], mixed[p][:, ct, b, :], ALU.mult,
                                                     ALU.add).then_inc(s[done], 1)

            def stats(t, src, st, out, done_st, done):
                dve.bn_stats(st[:, :], src).then_inc(s[done_st], 1)
                dve.wait_ge(landed, LANDED)
                need(dve, done_st, t)
                dve.bn_aggr(out[:, :], st[:, :]).then_inc(s[done], 1)

            def norm_mixed(t, p):
                dve.wait_ge(landed, LANDED)
                need(dve, "tr", t)
                stats(t, ps_d[:, 0:D], stat, mv, "st", "mv")
                need(dve, "sd", t)
                dve.reciprocal(inv[:, :], std[:, :]).then_inc(s["iv"], 1)
                need(dve, "iv", t)
                need(dve, "ot", t, back=2)
                dve.tensor_scalar(on[p][:, :], ps_d[:, 0:D], mv[:, 0:1], inv[:, :], ALU.subtract, ALU.mult)\
                   .then_inc(s["on"], 1)

            def turned(t, p):
                need(dve, "ot_h", t)
                low(ot_lo[:, :, :], ps_d[:, 0:D].rearrange("p (k r) -> p k r", k=DK), ot_hi[:, :, :], "ot_l")

            def norm_out(t, p):
                need(dve, "wo", t)
                dve.tensor_tensor(row(t), row(t), ps_e[:, 0:D], ALU.add).then_inc(s["x2"], 1)
                dve.wait_ge(landed, LANDED)
                need(dve, "x2", t)
                stats(t, row(t), fstat, fmv, "fst", "fmv")
                need(dve, "fsd", t)
                dve.reciprocal(finv[:, :], fstd[:, :]).then_inc(s["fiv"], 1)
                need(dve, "fiv", t)
                need(dve, "xft", t, back=2)
                dve.tensor_scalar(xf[p][:, :], row(t), fmv[:, 0:1], finv[:, :], ALU.subtract, ALU.mult)\
                   .then_inc(s["xf"], 1)

            def routed(t, p):
                need(dve, "xr_h", t)
                low(xr_lo[:, :, :], ps_e[:, 0:D].rearrange("p (k r) -> p k r", k=DK), xr_hi[:, :, :], "xr_l")

            def logit(t, p):
                need(dve, "lg", t)
                dve.tensor_copy(logits[:, bass.ds(t, 1), :].rearrange("p o e -> p (o e)"), ps_e[:, D:D + E])\
                   .then_inc(s["lgc"], 1)

            ticks(dve, [(1, transposed), (7, routed), (6, turned), (4, mix), (2, projected), (7, logit), (3, squares),
                        (6, norm_out), (5, norm_mixed), (0, norm)])

        @block.tensor
        def _(pe):
            pe.wait_ge(landed, LANDED)
            for k in range(DK):
                mm = pe.matmul(ps_e[0:1, 0:D], cols[:, LB, k:k + 1], w_raw[:, k, 5 * D:6 * D], start=k == 0,
                               stop=k == DK - 1)
            mm.then_inc(bo_ready, 1)
            pe.wait_ge(w_ready, 3)

            def turn(bank, src, name):
                for k in range(DK):
                    mm = pe.transpose(bank[:, k * P:(k + 1) * P], src(k), ident[:, :])
                mm.then_inc(s[name], 1)

            def product(out, lhs, rhs, bias=None):
                i, n = 0, 3 * DK + (bias is not None)
                for k in range(DK):
                    for a, b in hi_lo_products(*lhs, *rhs):
                        mm = pe.matmul(out, a(k), b(k), start=i == 0, stop=i == n - 1)
                        i += 1
                if bias is not None:
                    mm = pe.matmul(out, ones[:, :], bias, start=False, stop=True)
                return mm

            def tiles(x):
                return lambda k: x[:, k, :]

            def transposed(t, p):
                need(pe, "xn", t)
                need(pe, "xa_l", t, back=1)
                turn(ps_t, lambda k: xn[p][:, k * P:(k + 1) * P], "xt")

            def projected(t, p):
                need(pe, "xa_l", t)
                need(pe, "kv_l", t, back=1, per=2)
                x = (tiles(xa_hi[p]), tiles(xa_lo[p]))
                for i in range(2):
                    at = slice(2 * i * D, 2 * (i + 1) * D)
                    product(ps_kv[i][:, :], x, [lambda k, w=w: w[:, k, at] for w in (w_hi, w_lo)],
                            bias_row[:, at]).then_inc(s["kv_done"], 1)
                need(pe, "qc", t, back=1, per=2)
                need(pe, "av", t, back=2, per=2)
                for ct in range(DK):
                    at = slice(4 * D + ct * P, 4 * D + (ct + 1) * P)
                    mm = product(ps_q[:, ct * P:(ct + 1) * P], [lambda k, w=w: w[:, k, at] for w in (w_hi, w_lo)], x)
                mm.then_inc(s["q_done"], 1)

            def squares(t, p):
                need(pe, "kv_l", t, per=2)
                for b in range(2):
                    if b:
                        need(pe, "sm", t, per=2, i=0)
                    else:
                        need(pe, "sm", t, back=1, per=2)
                    r = slice(b * S, (b + 1) * S)
                    for j in range(2):
                        for ct in range(DK):
                            c = slice(ct * P, (ct + 1) * P)
                            for i, (x, y) in enumerate(hi_lo_products(kv_hi[p], kv_lo[p], kv_hi[p], kv_lo[p])):
                                o = (2 * j + ct) * P
                                mm = pe.matmul(ps_sq[:, o:o + P], x[r, 2 * j, c], y[r, 2 * j + 1, c], start=i == 0,
                                               stop=i == 2)
                    mm.then_inc(s["sq"], 1)
                need(pe, "qc", min(t + 1, NTILE - 1) if isinstance(t, int) else t + 1, per=2)
                for w in range(2):
                    for ct in range(DK):
                        o = D + 4 * w + 2 * ct
                        for i, x in enumerate((kv_hi[p], kv_lo[p])):
                            mm = pe.matmul(ps_q[:, o:o + 2], x[:, 2 * w + 1, ct * P:(ct + 1) * P], ind[:, :],
                                           start=i == 0, stop=i == 1)
                mm.then_inc(s["vm"], 1)

            def mix(t, p):
                need(pe, "s12", t, per=2)
                need(pe, "qc", t, per=2)
                for b in range(2):
                    if b:
                        need(pe, "m2", t, per=4, i=1)
                    else:
                        need(pe, "m2", t, back=1, per=4)
                    for ct in range(DK):
                        for k in range(3):
                            mm = pe.matmul(o_of(ct, k), sm[p][:, b, k, ct, :], q1[p][:, b, ct, :], start=True,
                                           stop=True)
                    mm.then_inc(s["o"], 1)

            def norm_mixed(t, p):
                need(pe, "m2", t, per=4)
                need(pe, "ot_l", t, back=1)
                turn(ps_d, lambda k: mixed[p][:, k, :, :].rearrange("p b r -> p (b r)"), "tr")

            def turned(t, p):
                need(pe, "on", t)
                turn(ps_d, lambda k: on[p][:, k * P:(k + 1) * P], "ot")

            def output(t, p):
                need(pe, "ot_l", t)
                need(pe, "lgc", t, back=1)
                at = slice(5 * D, 6 * D)
                product(ps_e[:, 0:D], (tiles(ot_hi), tiles(ot_lo)),
                        [lambda k, w=w: w[:, k, at] for w in (w_hi, w_lo)],
                        bias_row[:, 4 * D:5 * D]).then_inc(s["wo"], 1)

            def routed(t, p):
                need(pe, "xf", t)
                turn(ps_e, lambda k: xf[p][:, k * P:(k + 1) * P], "xft")

            def logit(t, p):
                need(pe, "xr_l", t)
                product(ps_e[:, D:D + E], (tiles(xr_hi), tiles(xr_lo)), (tiles(wr_hi), tiles(wr_lo)),
                        bias_row[:, 5 * D:]).then_inc(s["lg"], 1)

            ticks(pe, [(1, transposed), (7, routed), (6, turned), (4, mix), (2, projected), (7, logit), (6, output),
                       (3, squares), (5, norm_mixed)])


I = 512
TOP = 4
ALPHA, LIMIT = 1.702, 7.0
TC = 512
NQ = ROWS // TC
NI = I // P


def experts(nc, io, rows, xt_hi, xt_lo, logits, ident, out):
    ctx = ExitStack()

    def sb(name, shape, dt=F32):
        return ctx.enter_context(nc.sbuf_tensor("e_" + name, shape, dt))

    def two(name, shape, dt=F32):
        return [sb(f"{name}{i}", shape, dt) for i in range(2)]

    def pb(name):
        return ctx.enter_context(nc.psum_tensor("e_" + name, [P, 512], F32))

    def sem(name):
        return ctx.enter_context(nc.semaphore("e_" + name))

    NTILE = ROWS // P
    TQ = TC // P
    SHIFTED = 2

    with ctx:
        gu_raw = sb("gu_raw", [P, DK, 2 * I])
        gu_hi = two("gu_hi", [P, DK, 2 * I], F32R)
        gu_lo = two("gu_lo", [P, DK, 2 * I], F32R)
        dn_raw = sb("dn_raw", [P, NI, D])
        dn_hi = two("dn_hi", [P, NI, D], F32R)
        dn_lo = two("dn_lo", [P, NI, D], F32R)
        gub = two("gub", [P, 2 * NI])
        dnb = sb("dnb", [E, D])
        gate = two("gate", [P, TC])
        up = two("up", [P, TC])
        sig = two("sig", [P, TC])
        prod = two("prod", [P, TC])
        a_hi = two("a_hi", [P, NI, TC], F32R)
        a_lo = two("a_lo", [P, NI, TC], F32R)
        beats = sb("beats", [P, NTILE, E])
        rank = sb("rank", [P, NTILE, E])
        best = sb("best", [P, NTILE])
        comb = sb("comb", [P, NTILE, E])
        total = sb("total", [P, NTILE])
        comb_t = two("comb_t", [E, 4 * P])

        ps_g = [pb("ps_g0"), pb("ps_g1")]
        ps_u = [pb("ps_u0"), pb("ps_u1")]
        ps_d = [pb("ps_d0"), pb("ps_d1")]
        ps_c = pb("ps_c")
        ps_b = pb("ps_b")

        gu_landed = sem("gu_landed")
        dn_landed = sem("dn_landed")
        gub_landed = [sem("gub_landed0"), sem("gub_landed1")]
        dnb_landed = sem("dnb_landed")
        stored = sem("stored")
        ranked = sem("ranked")
        exp_done = sem("exp_done")
        combined = sem("combined")
        ct_done = sem("ct_done")
        ct_copied = sem("ct_copied")
        bias_done = sem("bias_done")
        biased = sem("biased")
        s = {n: sem(n) for n in (
            "wh wl "
            "gu_g gu_u "
            "gate up clip sig h act a_hi a_lo "
            "down y").split()}
        block = ctx.enter_context(nc.Block())
        WS = NQ * NI

        def need(eng, name, t, back=0, per=1, i=None):
            if not (isinstance(t, int) and t < back):
                eng.wait_ge(s[name], per * t + (per if i is None else i + 1) - per * back)

        def schedule(eng, chunk, split=None):
            def body(e, p):
                if split:
                    split(e, p)
                chunk(e - 1, 1 - p, 2)
                chunk(e - 1, 1 - p, 3)
                chunk(e, p, 0)
                chunk(e, p, 1)

            if split:
                split(0, 0)
            chunk(0, 0, 0)
            chunk(0, 0, 1)
            body(1, 1)
            with eng.Fori(1, E // 2) as i:
                for j in range(2):
                    body(2 * i + j, j)
            chunk(E - 1, 1, 2)
            chunk(E - 1, 1, 3)

        def bias_there(eng, e, p):
            eng.wait_ge(gub_landed[p], 8 * e + (16 - 8 * p))

        @block.sync
        def _(sp):
            def load(e, p):
                need(sp, "wl", e, back=1, per=2, i=0)
                sp.dma_start(gu_raw[:, :, :], io["gu"][bass.ds(e, 1)].rearrange("o (k p) j -> p (o k) j", p=P))\
                  .then_inc(gu_landed, 16)
                need(sp, "wl", e, back=1, per=2)
                sp.dma_start(dn_raw[:, :, :], io["dn"][bass.ds(e, 1)].rearrange("o (k p) d -> p (o k) d", p=P))\
                  .then_inc(dn_landed, 16)
                need(sp, "gate", e, back=2, per=WS)
                need(sp, "up", e, back=2, per=WS)
                sp.dma_start(gub[p][:, :], io["gub"][bass.ds(e, 1)].rearrange("o p j -> p (o j)"))\
                  .then_inc(gub_landed[p], 16)

            sp.dma_start(dnb[:, :], io["dnb"]).then_inc(dnb_landed, 16)
            load(0, 0)
            load(1, 1)
            with sp.Fori(1, E // 2) as i:
                for j in range(2):
                    load(2 * i + j, j)
            o = out.rearrange("(t b) s d -> (b s) t d", b=2)
            for q in range(NQ):
                sp.wait_ge(s["y"], TQ * (NQ * (E - 1) + q + 1))
                sp.dma_start(o[:, TQ * q:TQ * (q + 1), :], rows[:, TQ * q:TQ * (q + 1), :]).then_inc(stored, 16)
            sp.wait_ge(stored, 16 * NQ)

        @block.scalar
        def _(act):
            def split(e, p):
                act.wait_ge(gu_landed, 16 * e + 16)
                need(act, "gu_u", e, back=2, per=WS)
                act.activation(gu_hi[p][:, :, :], gu_raw[:, :, :], ACT.Copy).then_inc(s["wh"], 1)
                act.wait_ge(dn_landed, 16 * e + 16)
                need(act, "down", e, back=2, per=2 * NQ)
                act.activation(dn_hi[p][:, :, :], dn_raw[:, :, :], ACT.Copy).then_inc(s["wh"], 1)

            def high(e, q, it):
                need(act, "act", WS * e + NI * q + it)
                if it == 0:
                    need(act, "down", NQ * e + q, back=2, per=2)
                act.activation(a_hi[q % 2][:, it, :], prod[it % 2][:, :], ACT.Copy).then_inc(s["a_hi"], 1)

            def chunk(e, p, q):
                start = isinstance(e, int) and e == 0 and q == 0
                if q == 0:
                    bias_there(act, e, p)
                for it in range(NI):
                    w, v = WS * e + (NI * q + it), it % 2
                    need(act, "gu_u", w)
                    need(act, "h", w, back=2)
                    act.activation(up[v][:, :], ps_u[v][:, :], ACT.Identity, bias=gub[p][:, NI + it:NI + it + 1])\
                       .then_inc(s["up"], 1)
                    need(act, "gate", w)
                    need(act, "act", w, back=2)
                    act.activation(sig[v][:, :], gate[v][:, :], ACT.Sigmoid, scale=ALPHA).then_inc(s["sig"], 1)
                    if it:
                        high(e, q, it - 1)
                    elif not start:
                        high(e, q - 1, NI - 1)
                if start:
                    for g in range(NTILE // 4):
                        act.wait_ge(ct_done, g + 1)
                        if g >= 2:
                            act.wait_ge(bias_done, 2 * (g - 1))
                        act.activation(comb_t[g % 2][:, :], ps_c[0:E, :], ACT.Copy).then_inc(ct_copied, 1)

            routed = [False]

            def split_and_route(e, p):
                split(e, p)
                if not routed[0]:
                    routed[0] = True
                    act.wait_ge(ranked, SHIFTED)
                    act.activation(comb[:, :, :], comb[:, :, :], ACT.Exp).then_inc(exp_done, 1)

            schedule(act, chunk, split_and_route)
            high(E - 1, NQ - 1, NI - 1)

        @block.vector
        def _(dve):
            def split(e, p):
                for i, (raw, hi, lo) in enumerate(((gu_raw, gu_hi, gu_lo), (dn_raw, dn_hi, dn_lo))):
                    need(dve, "wh", e, per=2, i=i)
                    dve.tensor_tensor(lo[p][:, :, :], raw[:, :, :], hi[p][:, :, :].bitcast(F32), ALU.subtract)\
                       .then_inc(s["wl"], 1)

            def over(x, shape=(P, NTILE, E)):
                return x.rearrange("p (t o) -> p t o", o=1).to_broadcast(list(shape))

            def route():
                n = [0]

                def step(ins):
                    n[0] += 1
                    ins.then_inc(ranked, 1)
                    dve.wait_ge(ranked, n[0])

                step(dve.tensor_reduce(best[:, :], logits[:, :, :], AX.X, ALU.max))
                step(dve.tensor_tensor(comb[:, :, :], logits[:, :, :], over(best[:, :]), ALU.subtract))
                assert n[0] == SHIFTED
                step(dve.memset(rank[:, :, :], 0.0))
                for j in range(E):
                    for op, at in ((ALU.is_gt, slice(0, j)), (ALU.is_ge, slice(j + 1, E))):
                        k = at.stop - at.start
                        if k:
                            step(dve.tensor_tensor(beats[:, :, at], over(logits[:, :, j], (P, NTILE, k)),
                                                   logits[:, :, at], op))
                            step(dve.tensor_tensor(rank[:, :, at], rank[:, :, at], beats[:, :, at], ALU.add))
                step(dve.tensor_scalar(rank[:, :, :], rank[:, :, :], float(TOP), None, ALU.is_lt))
                dve.wait_ge(exp_done, 1)
                step(dve.tensor_tensor(comb[:, :, :], comb[:, :, :], rank[:, :, :], ALU.mult))
                step(dve.tensor_reduce(total[:, :], comb[:, :, :], AX.X, ALU.add))
                step(dve.reciprocal(total[:, :], total[:, :]))
                dve.tensor_tensor(comb[:, :, :], comb[:, :, :], over(total[:, :]), ALU.mult).then_inc(combined, 1)

            def low(e, q, it):
                need(dve, "a_hi", WS * e + (NI * q + it))
                dve.tensor_tensor(a_lo[q % 2][:, it, :], prod[it % 2][:, :], a_hi[q % 2][:, it, :].bitcast(F32),
                                  ALU.subtract).then_inc(s["a_lo"], 1)

            def activate(e, q, it):
                w, v = WS * e + (NI * q + it), it % 2
                need(dve, "up", w)
                dve.tensor_scalar(up[v][:, :], up[v][:, :], LIMIT, -LIMIT, ALU.min, ALU.max).then_inc(s["clip"], 1)
                need(dve, "clip", w)
                need(dve, "a_lo", w, back=2)
                dve.scalar_tensor_tensor(prod[v][:, :], up[v][:, :], 1.0, gate[v][:, :], ALU.add, ALU.mult)\
                   .then_inc(s["h"], 1)
                need(dve, "sig", w)
                need(dve, "h", w)
                dve.tensor_tensor(prod[v][:, :], prod[v][:, :], sig[v][:, :], ALU.mult).then_inc(s["act"], 1)

            def add(e, q, d):
                need(dve, "down", NQ * e + q, per=2, i=d)
                for i in range(2):
                    t = TQ * q + 2 * d + i
                    dve.scalar_tensor_tensor(rows[:, t, :], ps_d[d][:, i * D:(i + 1) * D], comb[:, t, bass.ds(e, 1)],
                                             rows[:, t, :], ALU.mult, ALU.add).then_inc(s["y"], 1)

            def chunk(e, p, q):
                start = isinstance(e, int) and e == 0 and q == 0
                second = isinstance(e, int) and e == 0 and q == 1
                if q == 0:
                    bias_there(dve, e, p)
                before = (e, q - 1) if q else (e - 1, NQ - 1)
                twice = (e, q - 2) if q >= 2 else (e - 1, q + 2)
                for it in range(NI):
                    w, v = WS * e + (NI * q + it), it % 2
                    need(dve, "gu_g", w)
                    need(dve, "sig", w, back=2)
                    dve.tensor_scalar(gate[v][:, :], ps_g[v][:, :], gub[p][:, it:it + 1], LIMIT, ALU.add, ALU.min)\
                       .then_inc(s["gate"], 1)
                    if it >= 2:
                        low(e, q, it - 2)
                    elif not start:
                        low(*before, NI - 2 + it)
                    if it:
                        activate(e, q, it - 1)
                    elif not start:
                        activate(*before, NI - 1)
                    if it == 0 and not start and not second:
                        add(*twice, 1)
                    if it == NI - 1 and not start:
                        add(*before, 0)
                if start:
                    for g in range(NTILE // 2):
                        dve.wait_ge(bias_done, g + 1)
                        dve.tensor_tensor(rows[:, 2 * g:2 * g + 2, :], rows[:, 2 * g:2 * g + 2, :],
                                          ps_b[:, :].rearrange("p (t d) -> p t d", d=D), ALU.add).then_inc(biased, 1)
                    dve.wait_ge(biased, NTILE // 2)
                    dve.wait_ge(combined, 1)

            routed = [False]

            def split_and_route(e, p):
                split(e, p)
                if not routed[0]:
                    routed[0] = True
                    route()

            schedule(dve, chunk, split_and_route)
            low(E - 1, NQ - 1, NI - 2)
            activate(E - 1, NQ - 1, NI - 1)
            low(E - 1, NQ - 1, NI - 1)
            add(E - 1, NQ - 2, 1)
            add(E - 1, NQ - 1, 0)
            add(E - 1, NQ - 1, 1)

        @block.tensor
        def _(pe):
            def down(e, p, q, d):
                u = NQ * e + q
                if d == 0:
                    need(pe, "a_lo", u, per=NI)
                need(pe, "wl", e, per=2)
                need(pe, "y", u, back=1, per=TQ, i=2 * d + 1)
                for i in range(2):
                    r = slice((2 * d + i) * P, (2 * d + i + 1) * P)
                    for k in range(NI):
                        for n, (x, y) in enumerate(hi_lo_products(a_hi[q % 2], a_lo[q % 2], dn_hi[p], dn_lo[p])):
                            mm = pe.matmul(ps_d[d][:, i * D:(i + 1) * D], x[:, k, r], y[:, k, :],
                                           start=k == 0 and n == 0, stop=k == NI - 1 and n == 2)
                mm.then_inc(s["down"], 1)

            def chunk(e, p, q):
                start = isinstance(e, int) and e == 0 and q == 0
                before = (e, p, q - 1) if q else (e - 1, 1 - p, NQ - 1)
                if q == 0:
                    need(pe, "wl", e, per=2, i=0)
                r = slice(q * TC, (q + 1) * TC)
                for it in range(NI):
                    w, v = WS * e + (NI * q + it), it % 2
                    for bank, made, free, o in ((ps_g, "gu_g", "gate", 0), (ps_u, "gu_u", "up", I)):
                        need(pe, free, w, back=2)
                        c = slice(o + it * P, o + (it + 1) * P)
                        i = 0
                        for k in range(DK):
                            for x, y in hi_lo_products(gu_hi[p], gu_lo[p], xt_hi, xt_lo):
                                mm = pe.matmul(bank[v][:, :], x[:, k, c], y[:, k, r], start=i == 0, stop=i == 5)
                                i += 1
                        mm.then_inc(s[made], 1)
                    if it >= 2 and not start:
                        down(*before, it - 2)
                if start:
                    biases()

            def biases():
                pe.wait_ge(combined, 1)
                pe.wait_ge(dnb_landed, 16)
                for g in range(NTILE // 4):
                    if g:
                        pe.wait_ge(ct_copied, g)
                    for t in range(4):
                        mm = pe.transpose(ps_c[0:E, t * P:(t + 1) * P], comb[:, 4 * g + t, :], ident[:, :])
                    mm.then_inc(ct_done, 1)
                    pe.wait_ge(ct_copied, g + 1)
                    for h in range(2):
                        if g or h:
                            pe.wait_ge(biased, 2 * g + h)
                        for t in range(2):
                            o = (2 * h + t) * P
                            mm = pe.matmul(ps_b[:, t * D:(t + 1) * D], comb_t[g % 2][:, o:o + P], dnb[:, :],
                                           start=True, stop=True)
                        mm.then_inc(bias_done, 1)

            schedule(pe, chunk)
            for d in range(2):
                down(E - 1, 1, NQ - 1, d)


def program(nc, io, out):
    NTILE = ROWS // P
    with ExitStack() as outer:
        def sb(name, shape, dt=F32):
            return outer.enter_context(nc.sbuf_tensor(name, shape, dt))

        ident = sb("ident", [P, P])
        rows = sb("rows", [P, NTILE, D])
        mean = sb("mean", [P, NTILE])
        rstd = sb("rstd", [P, NTILE])
        cross_attention(nc, io, rows, mean, rstd, ident)
        xt_hi = sb("xt_hi", [P, DK, ROWS], F32R)
        xt_lo = sb("xt_lo", [P, DK, ROWS], F32R)
        logits = sb("logits", [P, NTILE, E])
        latent_attention(nc, io, rows, mean, rstd, ident, xt_hi, xt_lo, logits)
        experts(nc, io, rows, xt_hi, xt_lo, logits, ident, out)


def lay_out(inputs):
    import numpy as np
    a = {k: np.asarray(v) for k, v in inputs.items()}
    xa, la, ff = "L0_xattn_", "L0_attn_", "L0_ffn_"
    ctx = np.zeros((B, NBLK, BF), np.float32)
    ctx.reshape(B, NBLK * STRIDE, D)[:, :CTX] = a["ctx_1024"]
    t = ctx[:, :NT].reshape(PAIRS, 2, NT, CH, CT, P).transpose(0, 3, 5, 4, 1, 2).reshape(PAIRS, CH, P, CT, 2 * NT)
    col = [a[la + "bq"]] + [np.repeat(a[la + f"g{i}"], HD) for i in range(1, 5)] + [a[la + "ln_g"], a[la + "ln_b"]]
    io = {"x": a["x"], "ctxN": ctx, "ctxT": t, "qa_qT": a[xa + "qa_q"].T, "qa_wk": a[xa + "qa_wk"],
          "qa_wvT": a[xa + "qa_wv"].T, "ws_w": a[xa + "ws_w"], "mn_w": a[xa + "mn_w"], "hn_w": a[xa + "hn_w"],
          "bias": np.concatenate([a[la + n] for n in ("bk1", "bv1", "bk2", "bv2", "bo")]
                                 + [a[ff + "router_bias"]])[None],
          "cols": np.stack(col).reshape(7, DK, P).transpose(2, 0, 1), "router_w": a[ff + "router_weight"].T}
    io |= {"W" + n: a[la + "W" + n].T for n in ("q", "k1", "v1", "k2", "v2", "o")}
    io |= {"gu": a[ff + "gate_up_proj"].transpose(0, 2, 1), "dn": a[ff + "down_proj"].transpose(0, 2, 1),
           "gub": a[ff + "gate_up_proj_bias"].reshape(E, 2 * I // P, P).transpose(0, 2, 1),
           "dnb": a[ff + "down_proj_bias"]}
    return {k: np.ascontiguousarray(v) for k, v in io.items()}


def kernel(**inputs):
    import concourse.bacc as bacc
    from concourse.bass_utils import run_bass_kernel_spmd

    arrays = lay_out(inputs)
    nc = bacc.Bacc("TRN2", target_bir_lowering=False, num_devices=1)
    io = {k: nc.dram_tensor(k, v.shape, F32, kind="ExternalInput").ap() for k, v in arrays.items()}
    out = nc.dram_tensor("out", (B, S, D), F32, kind="ExternalOutput").ap()
    program(nc, io, out)
    return run_bass_kernel_spmd(nc, [arrays], core_ids=[0]).results[0]["out"]
```

```python
import concourse.bass as bass
from concourse import mybir
from contextlib import ExitStack

F32 = mybir.dt.float32
F32R = mybir.dt.float32r
ALU = mybir.AluOpType
ACT = mybir.ActivationFunctionType
AX = mybir.AxisListType

P = 128
B, S, D = 32, 64, 256
CTX = 1601
STRIDE, WIN = 8, 16
NWIN = (CTX + STRIDE - (CTX - WIN) % STRIDE - WIN) // STRIDE + 1
BF = STRIDE * D
NROW = 112
NREST = 96
NBLK = NROW + NREST
NT = 202
PAIRS = B // 2
CH = 4
CF = BF // CH
CT = CF // P
FT = WIN * D // P
DK = D // P
SCALE = 1.0 / D ** 0.5


def hi_lo_products(hi_a, lo_a, hi_b, lo_b):
    return ((hi_a, hi_b), (hi_a, lo_b), (lo_a, hi_b))


H = 16
HD = D // H
E = 8
ROWS = B * S
LN_EPS = 1e-5
RMS_EPS = 1.1920929e-07


def cross_attention(nc, io, rows, mean, rstd, ident, stage, halves, attention_weights):
    ctx = ExitStack()

    def sb(name, shape, dt=F32):
        return ctx.enter_context(nc.sbuf_tensor(name, shape, dt))

    def pb(name):
        return ctx.enter_context(nc.psum_tensor(name, [P, 512], F32))

    def sem(name):
        return ctx.enter_context(nc.semaphore(name))

    with ctx:
        t_raw = [stage[:, i] for i in range(2)]
        t_hi = [halves[:, i] for i in range(2)]
        t_lo = [halves[:, 2 + i] for i in range(2)]
        n_raw = [sb(f"n_raw{i}", [NROW, 2, 2, CF]) for i in range(2)]
        n_hi = [sb(f"n_hi{i}", [NROW, 2, CF], F32R) for i in range(2)]
        n_lo = [sb(f"n_lo{i}", [NROW, 2, CF], F32R) for i in range(2)]
        attention_weights.place_staged_bias(n_raw[0][:, :, :, :].rearrange("p k b f -> p (k b f)"))
        g_hi = sb("g_hi", [P, FT // 2, 2, S], F32R)
        g_lo = sb("g_lo", [P, FT // 2, 2, S], F32R)
        v_hi = sb("v_hi", [P, FT, D], F32R)
        v_lo = sb("v_lo", [P, FT, D], F32R)
        w_hi = [sb(f"w_hi{i}", [P, 2, CT, 2, S], F32R) for i in range(2)]
        w_lo = [sb(f"w_lo{i}", [P, 2, CT, 2, S], F32R) for i in range(2)]
        pt_hi = sb("pt_hi", [NROW, 2, 2, 2, S], F32R)
        pt_lo = sb("pt_lo", [NROW, 2, 2, 2, S], F32R)
        pw = [sb(f"pw{i}", [P, CF]) for i in range(2)]
        prob = sb("prob", [P, 1 + 2 * NROW])
        other = sb("other", [P, NWIN])
        score = sb("score", [P, NWIN])
        top = sb("top", [P, 1])
        ntop = sb("ntop", [P, 1])
        den = sb("den", [P, 1])
        a1 = sb("a1", [P, DK, S])
        mem = sb("mem", [P, D])
        rden = sb("rden", [P, PAIRS])
        rms_w = sb("rms_w", [P, 2, D])
        eps = sb("eps", [P, 2])
        same = sb("same", [P, P])
        square = sb("square", [P, D])
        ss = sb("ss", [P, 2])
        stat = sb("stat", [P, 6])
        mv = sb("mv", [P, 2])
        std = sb("std", [P, 4])
        inv = sb("inv", [P, 3])
        hn = sb("hn", [P, D])
        memw = sb("memw", [P, D])
        ws = rows[:, :, :].rearrange("p (s m x) d -> p s m (x d)", s=2, m=DK)
        qa_q = sb("qa_q_sb", [P, DK, S])
        qa_wk, qa_wv = [x[:, :].rearrange("p (k d) -> p k d", k=DK) for x in pw]

        ps_s = pb("ps_s")
        ps_w = [pb(f"ps_w{i}") for i in range(2)]
        ps_v = [pb(f"ps_v{i}") for i in range(2)]
        ps_fold = ps_w + ps_v
        ps_m = pb("ps_m")
        ps_p = pb("ps_p")
        ps_a = pb("ps_a")

        qa_landed = sem("qa_landed")
        ws_landed = [sem(f"ws_landed{i}") for i in range(2)]
        a1_ready = sem("a1_ready")
        a1_copied = sem("a1_copied")
        fold_ready = sem("fold_ready")
        fold_hi = sem("fold_hi")
        fold_lo = sem("fold_lo")
        zeroed = sem("zeroed")
        t_landed = [sem(f"t_landed{i}") for i in range(2)]
        n_landed = [sem(f"n_landed{i}") for i in range(2)]
        t_hi_done = sem("t_hi_done")
        t_lo_done = sem("t_lo_done")
        n_hi_done = sem("n_hi_done")
        n_lo_done = sem("n_lo_done")
        scores_done = sem("scores_done")
        pw_done = sem("pw_done")
        pw_copied = sem("pw_copied")
        turned = sem("turned")
        w_hi_done = sem("w_hi_done")
        w_lo_done = sem("w_lo_done")
        mem_done = sem("mem_done")
        mem_copied = sem("mem_copied")
        other_done = sem("other_done")
        added = sem("added")
        top_done = sem("top_done")
        ntop_done = sem("ntop_done")
        exp_done = sem("exp_done")
        rden_done = sem("rden_done")
        pt_ready = sem("pt_ready")
        pt_hi_done = sem("pt_hi_done")
        pt_lo_done = sem("pt_lo_done")
        x_landed = sem("x_landed")
        s = {n: sem("n_" + n) for n in (
            "sq1 gs1 sd1 st0 mv0 sd0 iv h mw hs sq2 gs2 sd2 iv2 gr x1 st1 mv1 sd3 mu rs").split()}
        block = ctx.enter_context(nc.Block())

        WCH = 4
        WF = WIN * D // WCH
        LAG = CH

        @block.sync
        def _(sp):
            sp.dma_start(qa_q[:, :, :], io["qa_qT"].rearrange("(k p) q -> p k q", p=P)).then_inc(qa_landed, 16)
            sp.dma_start(qa_wk[:, :, :], io["qa_wk"].rearrange("(k p) m -> p k m", p=P)).then_inc(qa_landed, 16)
            sp.dma_start(qa_wv[:, :, :], io["qa_wvT"].rearrange("(k p) h -> p k h", p=P)).then_inc(qa_landed, 16)
            def load_t(t, c):
                sp.dma_start(t_raw[c % 2][:, :, :], io["ctxT"][bass.ds(t, 1), c].rearrange("o p k n -> p (o k) n"))\
                  .then_inc(t_landed[c % 2], 16)

            for j in range(WCH):
                if j == 2:
                    for c in range(2):
                        load_t(0, c)
                if j >= 2:
                    sp.wait_ge(fold_ready, 5 * (j - 1))
                sp.dma_start(ws[:, j % 2], io["ws_w"][:, j * WF:(j + 1) * WF].rearrange("(k p) f -> p k f", p=P))\
                  .then_inc(ws_landed[j % 2], 16)

            def load_n(t, c):
                for rows, kt in ((NROW, 0), (NREST, 1)):
                    sp.dma_start(n_raw[c % 2][0:rows, kt],
                                 io["ctxN"][bass.ds(2 * t, 2), kt * NROW:kt * NROW + rows, c * CF:(c + 1) * CF]
                                 .rearrange("b p f -> p b f")).then_inc(n_landed[c % 2], 16)

            for i, w in enumerate(("mn_w", "hn_w")):
                for b in range(2):
                    sp.dma_start(rms_w[b * S:(b + 1) * S, i, :], io[w]).then_inc(x_landed, 16)
            for c in range(2, CH):
                sp.wait_ge(t_lo_done, c - 1)
                load_t(0, c)
            sp.wait_ge(zeroed, 3)

            for c in range(CH):
                sp.wait_ge(t_lo_done, CH + c - 1)
                load_t(1, c)
                if c >= 2:
                    sp.wait_ge(n_lo_done, 2 * (c - 1))
                load_n(0, c)
                if c == 1:
                    sp.wait_ge(fold_ready, 20)
                    sp.dma_start(rows[:, :, :], io["x"].rearrange("(t b) s d -> (b s) t d", b=2))\
                      .then_inc(x_landed, 16)
            with sp.Fori(1, PAIRS - 1) as t:
                for c in range(CH):
                    sp.wait_ge(t_lo_done, CH * t + (CH + c - 1))
                    load_t(t + 1, c)
                    sp.wait_ge(n_lo_done, 2 * CH * t + 2 * (c - 1))
                    load_n(t, c)
            for c in range(CH):
                sp.wait_ge(n_lo_done, 2 * CH * (PAIRS - 1) + 2 * (c - 1))
                load_n(PAIRS - 1, c)
                if c == 0:
                    sp.wait_ge(t_lo_done, CH * PAIRS)
                    attention_weights.load(sp)
            sp.wait_ge(n_lo_done, 2 * CH * PAIRS - 2)
            attention_weights.load_bias(sp)

        @block.gpsimd
        def _(pool):
            tiles = [n_raw[0][NREST:NROW, 1, :, :], n_raw[1][NREST:NROW, 1, :, :], prob[:, :], ident[:, :]]
            for i, tile in enumerate(tiles):
                pool.memset(tile, 0.0).then_inc(zeroed, 1)
                pool.wait_ge(zeroed, i + 1)
            pool.affine_select(out=ident[:, :], in_=ident[:, :], compare_op=ALU.not_equal, fill=1.0, base=0,
                               pattern=[[-1, P]], channel_multiplier=1).then_inc(zeroed, 1)
            pool.wait_ge(zeroed, 5)
            consts = [(eps[:, 0:1], RMS_EPS), (eps[:, 1:2], LN_EPS), (same[:, :], 0.0), (same[0:S, 0:S], 1.0),
                      (same[S:P, S:P], 1.0)]
            for i, (tile, value) in enumerate(consts):
                pool.memset(tile, value).then_inc(zeroed, 1)
                pool.wait_ge(zeroed, 6 + i)
            attention_weights.make_constants(pool)

        def need(eng, name, t, back=0):
            if not (isinstance(t, int) and t < back):
                eng.wait_ge(s[name], t + 1 - back)

        def row(t):
            return rows[:, bass.ds(t, 1), :].rearrange("p o d -> p (o d)")

        def fold_targets(side, i):
            if side == "g":
                j, = i
                at = slice(8 * (j % 2), 8 * (j % 2) + 8)
                return [x[:, at, j // 2, :] for x in (g_hi, g_lo)]
            j, k = i
            return [x[:, 8 * j + 2 * k:8 * j + 2 * k + 2, :] for x in (v_hi, v_lo)]

        def fold_banks():
            n = 0
            for j in range(WCH):
                for side, i in [("g", (j,))] + [("v", (j, k)) for k in range(4)]:
                    yield n, j, side, i
                    n += 1

        FIRST_SPLITS = {3: 0, 6: 1, 14: 2, 16: 3}
        FIRST_SCORES = {12: (0, 1), 17: (2, 3)}

        def fold_src(n, side):
            return ps_fold[n % 4][:, :].rearrange("p (k q) -> p k q", q=S if side == "g" else D)

        @block.scalar
        def _(act):

            def split_t(t, c):
                act.wait_ge(t_landed[c % 2], 16 * (2 * t + (c // 2 + 1)))
                if not (isinstance(t, int) and t == 0 and c < 2):
                    act.wait_ge(scores_done, CH * t + (c - 1))
                act.activation(t_hi[c % 2][:, :, :], t_raw[c % 2][:, :, :], ACT.Copy).then_inc(t_hi_done, 1)

            def split_n(t, c, b):
                if b == 0:
                    act.wait_ge(n_landed[c % 2], 32 * (2 * t + (c // 2 + 1)))
                if not (isinstance(t, int) and t == 0 and c == 0):
                    act.wait_ge(pw_done, 2 * CH * t + (2 * c + b - 1))
                act.activation(n_hi[b][:, :, :], n_raw[c % 2][:, :, b, :], ACT.Copy).then_inc(n_hi_done, 1)

            def copy_pw(t, c, b):
                act.wait_ge(pw_done, 2 * CH * t + (2 * c + b + 1))
                if not (isinstance(t, int) and t == 0 and c == 0):
                    act.wait_ge(turned, 2 * CH * t + (2 * c + b - 1))
                act.activation(pw[b][:, :], ps_w[b][:, :], ACT.Copy).then_inc(pw_copied, 1)

            def copy_w(t, c, b):
                act.wait_ge(turned, 2 * CH * t + (2 * c + b + 1))
                if b == 0 and not (isinstance(t, int) and t == 0 and c < 2):
                    act.wait_ge(mem_done, CH * t + (c - 1))
                act.activation(w_hi[c % 2][:, :, :, b, :].rearrange("p h k q -> p k h q"),
                               ps_v[b][:, :].rearrange("p (k h q) -> p k h q", k=CT, h=2),
                               ACT.Copy).then_inc(w_hi_done, 1)

            def softmax(t):
                act.wait_ge(scores_done, CH * t + CH)
                if not (isinstance(t, int) and t == 0):
                    act.wait_ge(added, 2 * t)
                act.activation(other[0:S, :], ps_s[S:P, 1:1 + NWIN], ACT.Copy).then_inc(other_done, 1)
                act.activation(other[S:P, :], ps_s[0:S, NT:NT + NWIN], ACT.Copy).then_inc(other_done, 1)

            def exponent(t):
                act.wait_ge(ntop_done, t + 1)
                if not (isinstance(t, int) and t == 0):
                    act.wait_ge(pt_ready, t)
                    act.wait_ge(rden_done, t)
                act.activation(prob[:, 1:1 + NWIN], score[:, :], ACT.Exp, bias=ntop[:, :], scale=SCALE,
                               accum_out=den[:, :]).then_inc(exp_done, 1)

            def copy_pt(t):
                act.wait_ge(pt_ready, t + 1)
                if not (isinstance(t, int) and t == 0):
                    act.wait_ge(pw_done, 2 * CH * t)
                act.activation(pt_hi[:, :, :, :, :].rearrange("p k b h q -> p (k b h q)"),
                               ps_p[0:NROW, :], ACT.Copy).then_inc(pt_hi_done, 1)

            def copy_mem(t):
                act.wait_ge(mem_done, CH * t + CH)
                act.wait_ge(rden_done, t + 1)
                need(act, "mw", t, back=1)
                act.activation(mem[:, :], ps_m[:, 0:D], ACT.Copy, scale=rden[:, bass.ds(t, 1)]).then_inc(mem_copied, 1)

            def root(src, dst, which, name, scale=1.0):
                act.activation(std[:, dst:dst + 1], src, ACT.Sqrt, bias=eps[:, which:which + 1], scale=scale)\
                   .then_inc(s[name], 1)

            def norm_a(t):
                act.wait_ge(mem_copied, t + 1)
                need(act, "gs1", t, back=1)
                act.activation(square[:, :], mem[:, :], ACT.Square, accum_out=ss[:, 0:1]).then_inc(s["sq1"], 1)

            def norm_b(t):
                need(act, "gs1", t)
                need(act, "iv", t, back=1)
                root(ps_a[:, 0:1], 0, 0, "sd1", 1.0 / (S * D))
                need(act, "mv0", t)
                root(mv[:, 1:2], 1, 1, "sd0")

            def norm_c(t):
                need(act, "hs", t)
                need(act, "gs2", t, back=1)
                need(act, "sq1", t)
                act.activation(square[:, :], hn[:, :], ACT.Square, accum_out=ss[:, 1:2]).then_inc(s["sq2"], 1)

            def norm_d(t):
                need(act, "gs2", t)
                need(act, "iv2", t, back=1)
                root(ps_a[:, 2:3], 2, 0, "sd2", 1.0 / (S * D))

            def norm_e(t):
                need(act, "mv1", t)
                need(act, "rs", t, back=1)
                root(mv[:, 1:2], 3, 1, "sd3")

            def prepare(j):
                if j == 0:
                    act.wait_ge(scores_done, CH * PAIRS)
                attention_weights.split_high(act, j)

            def step(t, ahead, last):
                first = isinstance(t, int) and t == 0
                for c in range(CH):
                    if c:
                        copy_w(t, c - 1, 1)
                    elif not first:
                        copy_w(t - 1, CH - 1, 1)
                    split_n(t, c, 1)
                    if last and c:
                        prepare(2 * c - 2)
                        prepare(2 * c - 1)
                    if c == CH - 1 and not first:
                        norm_e(t - 1)
                    if c == CH - 1 and not last:
                        softmax(t + 1)
                    if c < CH - 1:
                        if not last:
                            split_t(t + 1, c + 1)
                    elif ahead:
                        split_t(t + 2, 0)
                    if c == 2 and not first:
                        norm_c(t - 1)
                    copy_pw(t, c, 0)
                    if c < CH - 1:
                        split_n(t, c + 1, 0)
                        copy_pw(t, c, 1)
                        copy_w(t, c, 0)
                    else:
                        if not last:
                            exponent(t + 1)
                        copy_pw(t, c, 1)
                        copy_w(t, c, 0)
                        if not last:
                            split_n(t + 1, 0, 0)
                            copy_pt(t + 1)
                    if c == 0 and not first:
                        copy_mem(t - 1)
                    if c < CH - 1 and not first:
                        (norm_a, norm_b, norm_d)[c](t - 1)

            for n, j, side, i in fold_banks():
                act.wait_ge(fold_ready, n + 1)
                act.activation(fold_targets(side, i)[0], fold_src(n, side), ACT.Copy).then_inc(fold_hi, 1)
                if n in FIRST_SPLITS:
                    split_t(0, FIRST_SPLITS[n])
                if n == 17:
                    softmax(0)
                    split_t(1, 0)
                if n == 18:
                    act.wait_ge(zeroed, 10)
                    exponent(0)
            split_n(0, 0, 0)
            copy_pt(0)
            step(0, True, False)
            with act.Fori(1, PAIRS - 2) as t:
                step(t, True, False)
            step(PAIRS - 2, False, False)
            step(PAIRS - 1, False, True)
            copy_w(PAIRS - 1, CH - 1, 1)
            copy_mem(PAIRS - 1)
            attention_weights.split_vectors_high(act)
            for norm in (norm_a, norm_b, norm_c, norm_d, norm_e):
                norm(PAIRS - 1)

        @block.vector
        def _(dve):
            dve.wait_ge(a1_ready, 1)
            dve.tensor_copy(a1[:, :, :], ps_a[:, 0:DK * S].rearrange("p (k q) -> p k q", k=DK)).then_inc(a1_copied, 1)
            def split_t(t, c):
                dve.wait_ge(t_hi_done, CH * t + (c + 1))
                dve.tensor_tensor(t_lo[c % 2][:, :, :], t_raw[c % 2][:, :, :], t_hi[c % 2][:, :, :].bitcast(F32),
                                  ALU.subtract).then_inc(t_lo_done, 1)

            def split_n(t, c, b):
                dve.wait_ge(n_hi_done, 2 * CH * t + (2 * c + b + 1))
                dve.tensor_tensor(n_lo[b][:, :, :], n_raw[c % 2][:, :, b, :], n_hi[b][:, :, :].bitcast(F32),
                                  ALU.subtract).then_inc(n_lo_done, 1)

            def copy_w(t, c, b):
                dve.wait_ge(w_hi_done, 2 * CH * t + (2 * c + b + 1))
                dve.tensor_tensor(w_lo[c % 2][:, :, :, b, :].rearrange("p h k q -> p k h q"),
                                  ps_v[b][:, :].rearrange("p (k h q) -> p k h q", k=CT, h=2),
                                  w_hi[c % 2][:, :, :, b, :].bitcast(F32).rearrange("p h k q -> p k h q"),
                                  ALU.subtract).then_inc(w_lo_done, 1)

            def softmax(t):
                dve.wait_ge(other_done, 2 * t + 2)
                if not (isinstance(t, int) and t == 0):
                    dve.wait_ge(exp_done, t)
                dve.tensor_tensor(score[0:S, :], ps_s[0:S, 0:NWIN], other[0:S, :], ALU.add).then_inc(added, 1)
                dve.tensor_tensor(score[S:P, :], ps_s[S:P, NT + 1:NT + 1 + NWIN], other[S:P, :],
                                  ALU.add).then_inc(added, 1)
                dve.wait_ge(added, 2 * t + 2)
                dve.reduce_max(top[:, :], score[:, :], AX.X).then_inc(top_done, 1)
                dve.wait_ge(top_done, t + 1)
                dve.tensor_scalar(ntop[:, :], top[:, :], -SCALE, None, ALU.mult).then_inc(ntop_done, 1)

            def copy_pt(t):
                dve.wait_ge(exp_done, t + 1)
                dve.reciprocal(rden[:, bass.ds(t, 1)], den[:, :]).then_inc(rden_done, 1)
                dve.wait_ge(pt_hi_done, t + 1)
                dve.tensor_tensor(pt_lo[:, :, :, :, :].rearrange("p k b h q -> p (k b h q)"),
                                  ps_p[0:NROW, :],
                                  pt_hi[:, :, :, :, :].bitcast(F32).rearrange("p k b h q -> p (k b h q)"),
                                  ALU.subtract).then_inc(pt_lo_done, 1)

            def norm_a(t):
                dve.wait_ge(x_landed, 5 * 16)
                need(dve, "mu", t, back=1)
                dve.bn_stats(stat[:, :], row(t)).then_inc(s["st0"], 1)
                dve.wait_ge(x_landed, 5 * 16)
                need(dve, "st0", t)
                dve.bn_aggr(mv[:, :], stat[:, :]).then_inc(s["mv0"], 1)

            def norm_b(t):
                need(dve, "sd1", t)
                need(dve, "sd0", t)
                dve.reciprocal(inv[:, 0:2], std[:, 0:2]).then_inc(s["iv"], 1)
                need(dve, "iv", t)
                dve.tensor_scalar(hn[:, :], row(t), mv[:, 0:1], inv[:, 1:2], ALU.subtract, ALU.mult).then_inc(s["h"], 1)
                dve.scalar_tensor_tensor(memw[:, :], mem[:, :], inv[:, 0:1], rms_w[:, 0, :], ALU.mult, ALU.mult)\
                   .then_inc(s["mw"], 1)
                need(dve, "mw", t)
                dve.tensor_tensor(hn[:, :], hn[:, :], memw[:, :], ALU.add).then_inc(s["hs"], 1)

            def norm_c(t):
                need(dve, "sd2", t)
                dve.reciprocal(inv[:, 2:3], std[:, 2:3]).then_inc(s["iv2"], 1)
                need(dve, "iv2", t)
                dve.scalar_tensor_tensor(memw[:, :], hn[:, :], inv[:, 2:3], rms_w[:, 1, :], ALU.mult, ALU.mult)\
                   .then_inc(s["gr"], 1)
                need(dve, "gr", t)
                dve.tensor_tensor(row(t), row(t), memw[:, :], ALU.add).then_inc(s["x1"], 1)
                dve.wait_ge(x_landed, 5 * 16)
                need(dve, "x1", t)
                dve.bn_stats(stat[:, :], row(t)).then_inc(s["st1"], 1)
                dve.wait_ge(x_landed, 5 * 16)
                need(dve, "st1", t)
                dve.bn_aggr(mv[:, :], stat[:, :]).then_inc(s["mv1"], 1)

            def norm_d(t):
                need(dve, "mv1", t)
                dve.tensor_copy(mean[:, bass.ds(t, 1)], mv[:, 0:1]).then_inc(s["mu"], 1)
                need(dve, "sd3", t)
                dve.reciprocal(rstd[:, bass.ds(t, 1)], std[:, 3:4]).then_inc(s["rs"], 1)

            def prepare(j):
                attention_weights.gain(dve, j)
                if j:
                    attention_weights.split_low(dve, j - 1)

            def step(t, ahead, last):
                first = isinstance(t, int) and t == 0
                for c in range(CH):
                    if c:
                        copy_w(t, c - 1, 1)
                    elif not first:
                        copy_w(t - 1, CH - 1, 1)
                    split_n(t, c, 1)
                    if last and c:
                        prepare(2 * c - 2)
                        prepare(2 * c - 1)
                    if c == CH - 1 and not first:
                        norm_d(t - 1)
                    if c == CH - 1 and not last:
                        softmax(t + 1)
                    if c < CH - 1:
                        if not last:
                            split_t(t + 1, c + 1)
                    elif ahead:
                        split_t(t + 2, 0)
                    if c < CH - 1:
                        split_n(t, c + 1, 0)
                        copy_w(t, c, 0)
                    else:
                        copy_w(t, c, 0)
                        if not last:
                            split_n(t + 1, 0, 0)
                            copy_pt(t + 1)
                    if c < CH - 1 and not first:
                        (norm_a, norm_b, norm_c)[c](t - 1)

            for n, j, side, i in fold_banks():
                hi, lo = fold_targets(side, i)
                dve.wait_ge(fold_hi, n + 1)
                dve.tensor_tensor(lo, fold_src(n, side), hi.bitcast(F32), ALU.subtract).then_inc(fold_lo, 1)
                if n in FIRST_SPLITS:
                    split_t(0, FIRST_SPLITS[n])
                if n == 17:
                    softmax(0)
                    split_t(1, 0)
            split_n(0, 0, 0)
            copy_pt(0)
            step(0, True, False)
            with dve.Fori(1, PAIRS - 2) as t:
                step(t, True, False)
            step(PAIRS - 2, False, False)
            step(PAIRS - 1, False, True)
            copy_w(PAIRS - 1, CH - 1, 1)
            attention_weights.split_low(dve, 5)
            attention_weights.gain_vectors(dve, ps_s)
            norm_a(PAIRS - 1)
            norm_b(PAIRS - 1)
            attention_weights.split_vectors_low(dve)
            norm_c(PAIRS - 1)
            norm_d(PAIRS - 1)

        @block.tensor
        def _(pe):
            pe.wait_ge(qa_landed, 48)
            for m in range(DK):
                for k in range(DK):
                    mm = pe.matmul(ps_a[:, m * S:(m + 1) * S], qa_wk[:, k, m * P:(m + 1) * P], qa_q[:, k, :],
                                   start=k == 0, stop=k == DK - 1)
            mm.then_inc(a1_ready, 1)
            pe.wait_ge(a1_copied, 1)
            def scores(t, c):
                pe.wait_ge(t_lo_done, CH * t + (c + 1))
                if c == 0 and not (isinstance(t, int) and t == 0):
                    pe.wait_ge(added, 2 * t)
                for k in range(CT):
                    ft = c * CT + k
                    prods = hi_lo_products(g_hi, g_lo, t_hi[c % 2], t_lo[c % 2])
                    for i, (a, b) in enumerate(prods):
                        mm = pe.matmul(ps_s[:, 0:2 * NT], a[:, ft, :, :], b[:, k, :],
                                       start=ft == 0 and i == 0, stop=ft == CH * CT - 1 and i == 2)
                mm.then_inc(scores_done, 1)

            def blocks(t, c, b):
                if b == 0 and c == 0:
                    pe.wait_ge(pt_lo_done, t + 1)
                pe.wait_ge(n_lo_done, 2 * CH * t + (2 * c + b + 1))
                if not (isinstance(t, int) and t == 0 and c == 0):
                    pe.wait_ge(pw_copied, 2 * CH * t + (2 * c + b - 1))
                i = 0
                for kt in range(2):
                    for x, y in hi_lo_products(pt_hi, pt_lo, n_hi[b], n_lo[b]):
                        mm = pe.matmul(ps_w[b][:, :], x[:, kt, b, :, :], y[:, kt, :], start=i == 0, stop=i == 5)
                        i += 1
                mm.then_inc(pw_done, 1)

            def turn(t, c, b):
                pe.wait_ge(pw_copied, 2 * CH * t + (2 * c + b + 1))
                if not (isinstance(t, int) and t == 0 and c == 0):
                    pe.wait_ge(w_lo_done, 2 * CH * t + (2 * c + b - 1))
                for ft in range(CT):
                    mm = pe.transpose(ps_v[b][:, ft * P:(ft + 1) * P], pw[b][:, ft * P:(ft + 1) * P], ident[:, :])
                mm.then_inc(turned, 1)

            def values(t, c, h):
                if h == 0:
                    pe.wait_ge(w_lo_done, 2 * CH * t + (2 * c + 2))
                    if c == 0 and not (isinstance(t, int) and t == 0):
                        pe.wait_ge(mem_copied, t)
                for k in range(CT):
                    ft = h * CH * CT + c * CT + k
                    for i, (x, y) in enumerate(hi_lo_products(w_hi[c % 2], w_lo[c % 2], v_hi, v_lo)):
                        mm = pe.matmul(ps_m[:, 0:D], x[:, h, k, :, :], y[:, ft, :],
                                       start=c == 0 and h == 0 and k == 0 and i == 0,
                                       stop=c == CH - 1 and h == 1 and k == CT - 1 and i == 2)
                if h:
                    mm.then_inc(mem_done, 1)

            def transpose_prob(t):
                pe.wait_ge(exp_done, t + 1)
                if not (isinstance(t, int) and t == 0):
                    pe.wait_ge(pt_lo_done, t)
                for kt in range(2):
                    for h in range(2):
                        mm = pe.transpose(ps_p[0:NROW, :].rearrange("p (k b h q) -> p k b h q", k=2, b=2, h=2)
                                          [:, kt, :, h, :],
                                          prob[:, 1 - h + kt * NROW:1 - h + (kt + 1) * NROW], ident[:, :])
                mm.then_inc(pt_ready, 1)

            def norm_sum(t, i):
                need(pe, ("sq1", "sq2")[i], t)
                need(pe, ("sd1", "sd2")[i], t, back=1)
                pe.matmul(ps_a[:, 2 * i:2 * i + 1], same[:, :], ss[:, i:i + 1], start=True, stop=True)\
                  .then_inc(s[("gs1", "gs2")[i]], 1)

            def step(t, last):
                first = isinstance(t, int) and t == 0
                for c in range(CH):
                    if not last:
                        scores(t + 1, c)
                    before = (t, c - 1) if c else (t - 1, CH - 1)
                    skip = first and c == 0
                    blocks(t, c, 0)
                    if not skip:
                        values(*before, 0)
                    if c == 1 and not first:
                        norm_sum(t - 1, 0)
                    blocks(t, c, 1)
                    turn(t, c, 0)
                    if c == 2 and not first:
                        norm_sum(t - 1, 1)
                    if not skip:
                        values(*before, 1)
                    turn(t, c, 1)
                    if last and c == 0:
                        pe.wait_ge(added, 2 * PAIRS)
                        attention_weights.norm_bias(pe, ps_s)
                if not last:
                    transpose_prob(t + 1)

            for n, j, side, i in fold_banks():
                if side == "g":
                    pe.wait_ge(ws_landed[j % 2], 16 * (j // 2 + 1))
                if n >= 4:
                    pe.wait_ge(fold_lo, n - 3)
                tiles = range(8) if side == "g" else range(2 * i[1], 2 * i[1] + 2)
                rhs = a1 if side == "g" else qa_wv
                width = S if side == "g" else D
                for o, f in enumerate(tiles):
                    for k in range(DK):
                        mm = pe.matmul(ps_fold[n % 4][:, o * width:(o + 1) * width], ws[:, j % 2, k, f * P:(f + 1) * P],
                                       rhs[:, k, :], start=k == 0, stop=k == DK - 1)
                mm.then_inc(fold_ready, 1)
                for c in FIRST_SCORES.get(n, ()):
                    pe.wait_ge(fold_lo, 5 * (2 + c // 2) + 1)
                    scores(0, c)
            pe.wait_ge(fold_lo, 20)
            pe.wait_ge(zeroed, 10)
            transpose_prob(0)
            step(0, False)
            with pe.Fori(1, PAIRS - 1) as t:
                step(t, False)
            step(PAIRS - 1, True)
            for h in range(2):
                values(PAIRS - 1, CH - 1, h)
            for i in range(2):
                norm_sum(PAIRS - 1, i)


class AttentionWeights:
    BQ, G1, G3, G4, G2, LG, LB = range(7)
    LANDED = 8 * 16
    MADE = 7
    GAINED = 17
    NB = 5 * D + E

    def __init__(self, nc, outer, io, stage, halves, ident):
        def sb(name, shape, dt=F32):
            return outer.enter_context(nc.sbuf_tensor("a_" + name, shape, dt))

        def sem(name):
            return outer.enter_context(nc.semaphore("a_" + name))

        def inside(x):
            flat = x.rearrange("p s c n -> p (s c n)")
            return flat[:, 0:DK * 6 * D].rearrange("p (k d) -> p k d", k=DK)

        self.io, self.ident = io, ident
        self.raw = inside(stage[:, :, :, :])
        self.hi, self.lo = inside(halves[:, 0:2]), inside(halves[:, 2:4])
        self.eps = sb("ln_eps", [P, 1])
        self.mean_of = sb("mean_of", [P, P], F32R)
        self.mask = sb("mask", [P, P])
        self.ones = sb("ones", [P, P], F32R)
        self.wr_raw = sb("wr_raw", [P, DK, E])
        self.wr_hi = sb("wr_hi", [P, DK, E], F32R)
        self.wr_lo = sb("wr_lo", [P, DK, E], F32R)
        self.bias_row = sb("bias_row", [P, self.NB], F32R)
        self.cols = sb("cols_sb", [P, 7, DK])
        self.q_bias = sb("q_bias", [P, 3, DK])
        self.landed = sem("w_landed")
        self.bias_landed = sem("bias_landed")
        self.made = sem("made")
        self.gained = sem("gained")
        self.bo_ready = sem("bo_ready")
        self.high = sem("w_high")
        self.ready = sem("w_ready")

    def place_staged_bias(self, space):
        self.bias_raw = space[0:1, 0:self.NB]

    def load(self, sp):
        for i, w in enumerate(("k2", "v2", "k1", "v1", "q", "o")):
            sp.dma_start(self.raw[:, :, i * D:(i + 1) * D], self.io["W" + w].rearrange("(k p) h -> p k h", p=P))\
              .then_inc(self.landed, 16)
        sp.dma_start(self.wr_raw[:, :, :], self.io["router_w"].rearrange("(k p) e -> p k e", p=P))\
          .then_inc(self.landed, 16)
        sp.dma_start(self.cols[:, :, :], self.io["cols"]).then_inc(self.landed, 16)

    def load_bias(self, sp):
        sp.dma_start(self.bias_raw[:, :], self.io["bias"]).then_inc(self.bias_landed, 16)

    def make_constants(self, pool):
        n = [0]

        def then(ins):
            n[0] += 1
            ins.then_inc(self.made, 1)
            pool.wait_ge(self.made, n[0])

        then(pool.memset(self.eps[:, :], LN_EPS))
        then(pool.memset(self.mean_of[:, :].bitcast(F32), 1.0 / S))
        then(pool.memset(self.ones[:, :].bitcast(F32), 1.0))
        then(pool.memset(self.bias_row[:, :].bitcast(F32), 0.0))
        then(pool.memset(self.mask[:, :], 1.0 / S))
        view = self.mask[:, :].rearrange("p (j i) -> p j i", i=HD)
        then(pool.affine_select(out=view, in_=view, compare_op=ALU.is_ge, fill=0.0, base=0,
                                pattern=[[-HD, P // HD], [0, HD]], channel_multiplier=1))
        then(pool.affine_select(out=view, in_=view, compare_op=ALU.is_ge, fill=0.0, base=HD - 1,
                                pattern=[[HD, P // HD], [0, HD]], channel_multiplier=-1))
        assert n[0] == self.MADE

    def norm_bias(self, pe, bank):
        pe.wait_ge(self.landed, self.LANDED)
        for k in range(DK):
            mm = pe.matmul(bank[0:1, 0:D], self.cols[:, self.LB, k:k + 1], self.raw[:, k, 5 * D:6 * D],
                           start=k == 0, stop=k == DK - 1)
        mm.then_inc(self.bo_ready, 1)

    def gain(self, dve, j):
        if j == 0:
            dve.wait_ge(self.landed, self.LANDED)
        if j == 5:
            dve.wait_ge(self.bo_ready, 1)
        for k in range(DK):
            if j < 5:
                at = self.raw[:, k, j * D + k * P:j * D + (k + 1) * P]
                dve.tensor_tensor(at, at, self.ident[:, :], ALU.add).then_inc(self.gained, 1)
            else:
                at = self.raw[:, k, 5 * D:6 * D]
                dve.tensor_scalar(at, at, self.cols[:, self.LG, k:k + 1], None, ALU.mult).then_inc(self.gained, 1)

    def gain_vectors(self, dve, bank):
        cols, gained = self.cols, self.gained
        for k, g in enumerate((self.G1, self.G3, self.G4)):
            dve.tensor_tensor(self.q_bias[:, k, :], cols[:, g, :], cols[:, self.BQ, :], ALU.mult).then_inc(gained, 1)
        dve.wait_ge(gained, 15)
        dve.tensor_tensor(self.q_bias[:, 2, :], self.q_bias[:, 2, :], cols[:, self.G2, :], ALU.add)\
           .then_inc(gained, 1)
        dve.wait_ge(self.bias_landed, 16)
        bo = self.bias_raw[0:1, 4 * D:5 * D]
        dve.tensor_tensor(bo, bo, bank[0:1, 0:D], ALU.add).then_inc(gained, 1)

    def split_high(self, act, j):
        act.wait_ge(self.gained, 2 * (j + 1))
        at = slice(j * D, (j + 1) * D)
        act.activation(self.hi[:, :, at], self.raw[:, :, at], ACT.Copy).then_inc(self.high, 1)

    def split_low(self, dve, j):
        dve.wait_ge(self.high, j + 1)
        at = slice(j * D, (j + 1) * D)
        dve.tensor_tensor(self.lo[:, :, at], self.raw[:, :, at], self.hi[:, :, at].bitcast(F32), ALU.subtract)\
           .then_inc(self.ready, 1)

    def split_vectors_high(self, act):
        act.wait_ge(self.made, self.MADE)
        act.wait_ge(self.gained, self.GAINED)
        act.activation(self.wr_hi[:, :, :], self.wr_raw[:, :, :], ACT.Copy).then_inc(self.high, 1)
        act.activation(self.bias_row[0:1, :], self.bias_raw[:, :], ACT.Copy).then_inc(self.high, 1)

    def split_vectors_low(self, dve):
        for i, (lo, raw, hi) in enumerate(((self.wr_lo[:, :, :], self.wr_raw[:, :, :], self.wr_hi[:, :, :]),
                                           (self.bias_row[32:33, :], self.bias_raw[:, :], self.bias_row[0:1, :]))):
            dve.wait_ge(self.high, 7 + i)
            dve.tensor_tensor(lo, raw, hi.bitcast(F32), ALU.subtract).then_inc(self.ready, 1)


def latent_attention(nc, io, rows, mean, rstd, ident, weights, xt_hi, xt_lo, logits, experts_weights):
    ctx = ExitStack()

    def sb(name, shape, dt=F32):
        return ctx.enter_context(nc.sbuf_tensor("a_" + name, shape, dt))

    def two(name, shape, dt=F32):
        return [sb(f"{name}{i}", shape, dt) for i in range(2)]

    def pb(name):
        return ctx.enter_context(nc.psum_tensor("a_" + name, [P, 512], F32))

    def sem(name):
        return ctx.enter_context(nc.semaphore("a_" + name))

    with ctx:
        w_hi, w_lo, wr_hi, wr_lo = weights.hi, weights.lo, weights.wr_hi, weights.wr_lo
        bias_row, cols, q_bias, ones = weights.bias_row, weights.cols, weights.q_bias, weights.ones
        eps, mean_of, mask = weights.eps, weights.mean_of, weights.mask
        landed, LANDED = weights.landed, weights.LANDED
        stat = sb("stat", [P, 6])
        mv = sb("mv", [P, 2])
        std = sb("std", [P, 1])
        inv = sb("inv", [P, 1])
        fstat = sb("fstat", [P, 6])
        fmv = sb("fmv", [P, 2])
        fstd = sb("fstd", [P, 1])
        finv = sb("finv", [P, 1])
        xn = sb("xn", [P, D])
        xa_hi = sb("xa_hi", [P, DK, P], F32R)
        xa_lo = sb("xa_lo", [P, DK, P], F32R)
        kv_hi = two("kv_hi", [P, 4, D], F32R)
        kv_lo = two("kv_lo", [P, 4, D], F32R)
        qv = two("qv", [P, 3, DK, P])
        sq = sb("sq", [P, 2, DK * P])
        mx = sb("mx", [P, 2, 3, DK * P])
        on = sb("on", [P, D])
        ot_hi = sb("ot_hi", [P, DK, P], F32R)
        ot_lo = sb("ot_lo", [P, DK, P], F32R)
        xf = sb("xf", [P, D])
        xr_hi = sb("xr_hi", [P, DK, P], F32R)
        xr_lo = sb("xr_lo", [P, DK, P], F32R)

        ps_x = pb("ps_x")
        ps_kv = [pb("ps_kv0"), pb("ps_kv1")]
        ps_qw = pb("ps_qw")
        ps_sq = pb("ps_sq")
        ps_vm = pb("ps_vm")
        ps_o = pb("ps_o")
        ps_d = pb("ps_d")

        s = {n: sem(n) for n in (
            "xn xt xa_h xa_l kv0 kv1 kv_h kv_l q_done qc sq sm s12 av o st mv sd iv on ot ot_h "
            "ot_l wo x2 fst fmv fsd fiv xf xft xr_h xr_l xs lg lgc").split()}
        block = ctx.enter_context(nc.Block())
        NTILE = ROWS // P

        def need(eng, name, t, back=0, per=1, i=None):
            if isinstance(t, int):
                if t < back:
                    return
                t = min(t - back, NTILE - 1) + back
            eng.wait_ge(s[name], per * t + (per if i is None else i + 1) - per * back)

        def ticks(eng, stages, split=None):
            def tick(n, slot, among):
                for lag, f in stages:
                    if among(lag):
                        f(n - lag, (slot + lag) % 2)

            for n in range(DEEPEST):
                tick(n, n % 2, lambda lag: n >= lag)
            with eng.Fori(DEEPEST // 2, NTILE // 2) as i:
                for j in range(2):
                    tick(2 * i + j, j, lambda lag: True)
            for n in range(NTILE, NTILE + DEEPEST):
                tick(n, n % 2, lambda lag: n - lag < NTILE)
                if split:
                    for piece in range(2 * (n - NTILE), 2 * (n - NTILE) + 2):
                        split(eng, 0, 0, piece)

        DEEPEST = 4

        def row(t):
            return rows[:, bass.ds(t, 1), :].rearrange("p o d -> p (o d)")

        @block.sync
        def _(sp):
            experts_weights.load(sp, 0, wait=False)

        @block.gpsimd
        def _(pool):
            def keep(t, p):
                need(pool, "xr_l", t)
                for src, dst in ((xr_hi, xt_hi), (xr_lo, xt_lo)):
                    pool.tensor_copy(dst[:, :, bass.ds(t * P, P)], src[:, :, :].bitcast(F32)).then_inc(s["xs"], 1)

            with pool.Fori(0, NTILE) as t:
                keep(t, 0)

        @block.scalar
        def _(act):
            def high(dst, src, name):
                act.activation(dst, src, ACT.Copy).then_inc(s[name], 1)

            def routed(t, p):
                need(act, "xft", t)
                need(act, "xt", t, back=-3)
                need(act, "lg", t, back=1)
                need(act, "xs", t, back=1, per=2)
                high(xr_hi[:, :, :], ps_x[:, D:].rearrange("p (k r) -> p k r", k=DK), "xr_h")

            def transposed(t, p):
                need(act, "xt", t)
                need(act, "q_done", t, back=1)
                high(xa_hi[:, :, :], ps_x[:, 0:D].rearrange("p (k r) -> p k r", k=DK), "xa_h")

            def norm_mixed(t, p):
                need(act, "mv", t)
                need(act, "iv", t, back=1)
                act.activation(std[:, :], mv[:, 1:2], ACT.Sqrt, bias=eps[:, :]).then_inc(s["sd"], 1)

            def projected(i):
                def f(t, p):
                    need(act, f"kv{i}", t)
                    need(act, "sq", t, back=2, per=2)
                    high(kv_hi[p][:, 2 * i:2 * i + 2, :], ps_kv[i][:, :].rearrange("p (j d) -> p j d", d=D), "kv_h")
                return f

            def turned(t, p):
                need(act, "ot", t)
                need(act, "wo", t, back=1)
                high(ot_hi[:, :, :], ps_d[:, 0:D].rearrange("p (k r) -> p k r", k=DK), "ot_h")

            def queries(ks):
                def f(t, p):
                    if 0 in ks:
                        need(act, "q_done", t)
                        need(act, "o", t, back=2)
                        need(act, "x2", t, back=2)
                    for k in ks:
                        g = (weights.G1, weights.G3, weights.G4)[k]
                        for ct in range(DK):
                            act.activation(qv[p][:, k, ct, :], ps_qw[:, ct * P:(ct + 1) * P], ACT.Identity,
                                           scale=cols[:, g, ct:ct + 1], bias=q_bias[:, k, ct:ct + 1])\
                               .then_inc(s["qc"], 1)
                return f

            def norm_out(t, p):
                need(act, "fmv", t)
                need(act, "fiv", t, back=1)
                act.activation(fstd[:, :], fmv[:, 1:2], ACT.Sqrt, bias=eps[:, :]).then_inc(s["fsd"], 1)

            ticks(act, [(4, routed), (1, transposed), (3, norm_mixed), (1, projected(0)), (3, turned),
                        (1, queries((0,))), (3, norm_out), (1, projected(1)),
                        (1, queries((1, 2)))], experts_weights.split_high)

        @block.vector
        def _(dve):
            def wide(x, shape):
                return x.to_broadcast(shape)

            def low(dst, src, hi, name):
                dve.tensor_tensor(dst, src, hi.bitcast(F32), ALU.subtract).then_inc(s[name], 1)

            def stats(src, st, out, done_st, done, t):
                dve.wait_ge(landed, LANDED)
                dve.bn_stats(st[:, :], src).then_inc(s[done_st], 1)
                dve.wait_ge(landed, LANDED)
                need(dve, done_st, t)
                dve.bn_aggr(out[:, :], st[:, :]).then_inc(s[done], 1)

            def stats_mixed(t, p):
                need(dve, "o", t)
                stats(ps_o[:, 0:D], stat, mv, "st", "mv", t)

            def routed(t, p):
                need(dve, "xr_h", t)
                need(dve, "xa_h", t, back=-3)
                low(xr_lo[:, :, :], ps_x[:, D:].rearrange("p (k r) -> p k r", k=DK), xr_hi[:, :, :], "xr_l")

            def transposed(t, p):
                need(dve, "xa_h", t)
                low(xa_lo[:, :, :], ps_x[:, 0:D].rearrange("p (k r) -> p k r", k=DK), xa_hi[:, :, :], "xa_l")

            def norm_mixed(t, p):
                need(dve, "sd", t)
                dve.reciprocal(inv[:, :], std[:, :]).then_inc(s["iv"], 1)
                need(dve, "iv", t)
                need(dve, "ot", t, back=1)
                dve.tensor_scalar(on[:, :], ps_o[:, 0:D], mv[:, 0:1], inv[:, :], ALU.subtract, ALU.mult)\
                   .then_inc(s["on"], 1)

            def squares(b):
                def f(t, p):
                    need(dve, "sq", t, per=2, i=b)
                    need(dve, "o", t, back=1)
                    dve.tensor_tensor(sq[:, :, :].rearrange("p w (c d) -> p (w c) d", d=P),
                                      ps_sq[:, :].rearrange("p (w d) -> p w d", d=P),
                                      wide(mask[:, :].rearrange("p (o d) -> p o d", o=1), [P, 4, P]), ALU.mult)\
                       .then_inc(s["sm"], 1)
                    need(dve, "sm", t, per=2, i=b)
                    dve.tensor_tensor(mx[:, b, 2, :], sq[:, 0, :], sq[:, 1, :], ALU.mult).then_inc(s["s12"], 1)
                    dve.tensor_tensor(mx[:, b, 0:2, :], ps_vm[:, :].rearrange("p (w d) -> p w d", w=2), sq[:, :, :],
                                      ALU.mult).then_inc(s["av"], 1)
                return f

            def projected(i):
                def f(t, p):
                    need(dve, "kv_h", t, per=2, i=i)
                    low(kv_lo[p][:, 2 * i:2 * i + 2, :], ps_kv[i][:, :].rearrange("p (j d) -> p j d", d=D),
                        kv_hi[p][:, 2 * i:2 * i + 2, :], "kv_l")
                return f

            def logit(t, p):
                need(dve, "lg", t)
                need(dve, "ot_h", t, back=-1)
                dve.tensor_copy(logits[:, bass.ds(t, 1), :].rearrange("p o e -> p (o e)"), ps_d[:, D:D + E])\
                   .then_inc(s["lgc"], 1)

            def turned(t, p):
                need(dve, "ot_h", t)
                low(ot_lo[:, :, :], ps_d[:, 0:D].rearrange("p (k r) -> p k r", k=DK), ot_hi[:, :, :], "ot_l")

            def norm(t, p):
                need(dve, "xt", t, back=1)
                dve.tensor_scalar(xn[:, :], row(t), mean[:, bass.ds(t, 1)], rstd[:, bass.ds(t, 1)], ALU.subtract,
                                  ALU.mult).then_inc(s["xn"], 1)

            def norm_out(t, p):
                need(dve, "wo", t)
                need(dve, "q_done", t, back=-2)
                dve.tensor_tensor(row(t), row(t), ps_qw[:, D:], ALU.add).then_inc(s["x2"], 1)
                dve.wait_ge(landed, LANDED)
                need(dve, "x2", t)
                stats(row(t), fstat, fmv, "fst", "fmv", t)
                need(dve, "fsd", t)
                dve.reciprocal(finv[:, :], fstd[:, :]).then_inc(s["fiv"], 1)
                need(dve, "fiv", t)
                need(dve, "xft", t, back=1)
                dve.tensor_scalar(xf[:, :], row(t), fmv[:, 0:1], finv[:, :], ALU.subtract, ALU.mult)\
                   .then_inc(s["xf"], 1)

            ticks(dve, [(3, stats_mixed), (4, routed), (1, transposed), (3, norm_mixed), (2, squares(0)),
                        (1, projected(0)), (4, logit), (3, turned), (2, squares(1)), (0, norm), (3, norm_out),
                        (1, projected(1))], experts_weights.split_low)

        @block.tensor
        def _(pe):
            pe.wait_ge(weights.ready, 8)

            def turn(bank, src, name):
                for k in range(DK):
                    mm = pe.transpose(bank[:, k * P:(k + 1) * P], src[:, k * P:(k + 1) * P], ident[:, :])
                mm.then_inc(s[name], 1)

            def product(out, lhs, rhs, bias=None):
                i, n = 0, 3 * DK + (bias is not None)
                for k in range(DK):
                    for a, b in hi_lo_products(*lhs, *rhs):
                        mm = pe.matmul(out, a(k), b(k), start=i == 0, stop=i == n - 1)
                        i += 1
                if bias is not None:
                    mm = pe.matmul(out, ones[:, :], bias, start=False, stop=True)
                return mm

            def tiles(x):
                return lambda k: x[:, k, :]

            xa = (tiles(xa_hi), tiles(xa_lo))

            def columns(at):
                return [lambda k, w=w: w[:, k, at] for w in (w_hi, w_lo)]

            def routed(t, p):
                need(pe, "xf", t)
                need(pe, "xr_l", t, back=1)
                need(pe, "xa_l", t, back=-2)
                turn(ps_x[:, D:], xf, "xft")

            def transposed(t, p):
                need(pe, "xn", t)
                need(pe, "xr_l", t, back=4)
                need(pe, "xa_l", t, back=1)
                turn(ps_x[:, 0:D], xn, "xt")

            def squares(b):
                def f(t, p):
                    need(pe, "kv_l", t, per=2)
                    if b:
                        need(pe, "av", t, per=2, i=0)
                    else:
                        need(pe, "av", t, back=1, per=2)
                    r = slice(b * S, (b + 1) * S)
                    for j in range(2):
                        for ct in range(DK):
                            c = slice(ct * P, (ct + 1) * P)
                            o = (2 * j + ct) * P
                            for i, (x, y) in enumerate(hi_lo_products(kv_hi[p], kv_lo[p], kv_hi[p], kv_lo[p])):
                                mm = pe.matmul(ps_sq[:, o:o + P], x[r, 2 - 2 * j, c], y[r, 3 - 2 * j, c],
                                               start=i == 0, stop=i == 2)
                    for i, x in enumerate((kv_hi[p], kv_lo[p])):
                        mm = pe.matmul(ps_vm[:, :], mean_of[r, :],
                                       x[r, :, :].rearrange("r (w o) d -> r w o d", o=2)[:, :, 1, :],
                                       start=i == 0, stop=i == 1)
                    mm.then_inc(s["sq"], 1)
                return f

            def projected(i):
                def f(t, p):
                    need(pe, "xa_l", t)
                    need(pe, "kv_l", t, back=1, per=2, i=i)
                    at = slice(2 * i * D, 2 * (i + 1) * D)
                    product(ps_kv[i][:, :], xa, columns(at), bias_row[:, at]).then_inc(s[f"kv{i}"], 1)
                return f

            def logit(t, p):
                need(pe, "xr_l", t)
                need(pe, "lgc", t, back=1)
                need(pe, "ot_l", t)
                product(ps_d[:, D:D + E], (tiles(xr_hi), tiles(xr_lo)), (tiles(wr_hi), tiles(wr_lo)),
                        bias_row[:, 5 * D:]).then_inc(s["lg"], 1)

            def turned(t, p):
                need(pe, "on", t)
                need(pe, "ot_l", t, back=1)
                need(pe, "lgc", t, back=2)
                turn(ps_d[:, 0:D], on, "ot")

            def output(t, p):
                need(pe, "ot_l", t)
                need(pe, "x2", t, back=1)
                need(pe, "qc", t, back=-1, per=6)
                product(ps_qw[:, D:], (tiles(ot_hi), tiles(ot_lo)), columns(slice(5 * D, 6 * D)),
                        bias_row[:, 4 * D:5 * D]).then_inc(s["wo"], 1)

            def queries(t, p):
                need(pe, "qc", t, back=1, per=6)
                need(pe, "x2", t, back=3)
                for ct in range(DK):
                    mm = product(ps_qw[:, ct * P:(ct + 1) * P], columns(slice(4 * D + ct * P, 4 * D + (ct + 1) * P)),
                                 xa)
                mm.then_inc(s["q_done"], 1)

            def mix(t, p):
                need(pe, "av", t, per=2)
                need(pe, "qc", t, per=6)
                need(pe, "on", t, back=1)
                for b in range(2):
                    r = slice(b * S, (b + 1) * S)
                    for ct in range(DK):
                        c = slice(ct * P, (ct + 1) * P)
                        for k in range(3):
                            mm = pe.matmul(ps_o[r, c], qv[p][:, k, ct, r], mx[:, b, k, c], start=k == 0,
                                           stop=k == 2)
                mm.then_inc(s["o"], 1)

            ticks(pe, [(4, routed), (1, transposed), (2, squares(0)), (1, projected(0)), (4, logit), (3, turned),
                       (2, squares(1)), (3, output), (1, queries), (1, projected(1)), (2, mix)])


I = 512
TOP = 4
ALPHA, LIMIT = 1.702, 7.0
TC = 512
NQ = ROWS // TC
NI = I // P


class ExpertWeights:
    PIECES = 2 * NI

    def __init__(self, nc, outer, io):
        def sb(name, shape, dt=F32):
            return outer.enter_context(nc.sbuf_tensor("e_" + name, shape, dt))

        def sem(name):
            return outer.enter_context(nc.semaphore("e_" + name))

        self.io = io
        self.gu = sb("gu_raw", [P, DK, 2 * I])
        self.dn = sb("dn_raw", [P, NI, D])
        self.gu_hi, self.gu_lo = [sb("gu_hi0", [P, DK, 2 * I], F32R)], [sb("gu_lo0", [P, DK, 2 * I], F32R)]
        self.dn_hi, self.dn_lo = [sb("dn_hi0", [P, NI, D], F32R)], [sb("dn_lo0", [P, NI, D], F32R)]
        self.gu_landed = sem("gu_landed")
        self.dn_landed = sem("dn_landed")
        self.high = sem("wh")
        self.low = sem("wl")

    def load(self, sp, e, wait=True):
        if wait:
            sp.wait_ge(self.low, self.PIECES * e + (NI - self.PIECES))
        sp.dma_start(self.gu[:, :, :], self.io["gu"][bass.ds(e, 1)].rearrange("o (k p) j -> p (o k) j", p=P))\
          .then_inc(self.gu_landed, 16)
        if wait:
            sp.wait_ge(self.low, self.PIECES * e)
        sp.dma_start(self.dn[:, :, :], self.io["dn"][bass.ds(e, 1)].rearrange("o (k p) d -> p (o k) d", p=P))\
          .then_inc(self.dn_landed, 16)

    def piece(self, gu, dn, piece):
        w = 2 * I // NI
        return gu[:, :, piece * w:(piece + 1) * w] if piece < NI else dn[:, piece - NI, :]

    def split_high(self, act, e, p, piece):
        if piece == 0:
            act.wait_ge(self.gu_landed, 16 * e + 16)
        if piece == NI:
            act.wait_ge(self.dn_landed, 16 * e + 16)
        act.activation(self.piece(self.gu_hi[p], self.dn_hi[p], piece), self.piece(self.gu, self.dn, piece), ACT.Copy)\
           .then_inc(self.high, 1)

    def split_low(self, dve, e, p, piece):
        dve.wait_ge(self.high, self.PIECES * e + (piece + 1))
        dve.tensor_tensor(self.piece(self.gu_lo[p], self.dn_lo[p], piece), self.piece(self.gu, self.dn, piece),
                          self.piece(self.gu_hi[p], self.dn_hi[p], piece).bitcast(F32), ALU.subtract)\
           .then_inc(self.low, 1)


def experts(nc, io, rows, xt_hi, xt_lo, logits, ident, weights, out):
    ctx = ExitStack()

    def sb(name, shape, dt=F32):
        return ctx.enter_context(nc.sbuf_tensor("e_" + name, shape, dt))

    def two(name, shape, dt=F32):
        return [sb(f"{name}{i}", shape, dt) for i in range(2)]

    def pb(name):
        return ctx.enter_context(nc.psum_tensor("e_" + name, [P, 512], F32))

    def sem(name):
        return ctx.enter_context(nc.semaphore("e_" + name))

    NTILE = ROWS // P
    TQ = TC // P
    SHIFTED = 2

    with ctx:
        weights.gu_hi.append(sb("gu_hi1", [P, DK, 2 * I], F32R))
        weights.gu_lo.append(sb("gu_lo1", [P, DK, 2 * I], F32R))
        weights.dn_hi.append(sb("dn_hi1", [P, NI, D], F32R))
        weights.dn_lo.append(sb("dn_lo1", [P, NI, D], F32R))
        gu_hi, gu_lo, dn_hi, dn_lo = weights.gu_hi, weights.gu_lo, weights.dn_hi, weights.dn_lo
        PIECES = weights.PIECES
        gub = two("gub", [P, 2 * NI])
        dnb = sb("dnb", [E, D])
        gate = two("gate", [P, TC])
        up = two("up", [P, TC])
        silu = two("silu", [P, TC])
        prod = two("prod", [P, TC])
        a_hi = two("a_hi", [P, NI, TC], F32R)
        a_lo = two("a_lo", [P, NI, TC], F32R)
        beats = sb("beats", [P, NTILE, E])
        rank = sb("rank", [P, NTILE, E])
        best = sb("best", [P, NTILE])
        comb = sb("comb", [P, NTILE, E])
        total = sb("total", [P, NTILE])
        comb_t = sb("comb_t", [E, TC])

        ps_g = [pb("ps_g0"), pb("ps_g1")]
        ps_u = [pb("ps_u0"), pb("ps_u1")]
        ps_d = [pb("ps_d0"), pb("ps_d1")]
        ps_c = pb("ps_c")
        ps_b = pb("ps_b")

        LAST_DOWN = ps_d + ps_g

        gub_landed = [sem("gub_landed0"), sem("gub_landed1")]
        dnb_landed = sem("dnb_landed")
        stored = sem("stored")
        ranked = sem("ranked")
        exp_done = sem("exp_done")
        combined = sem("combined")
        ct_done = sem("ct_done")
        ct_copied = sem("ct_copied")
        bias_done = sem("bias_done")
        biased = sem("biased")
        s = {n: sem(n) for n in (
            "gu_g gu_u "
            "gate up clip silu h a_hi a_lo "
            "down y").split()}
        block = ctx.enter_context(nc.Block())
        WS = NQ * NI

        def need(eng, name, t, back=0, per=1, i=None):
            if not (isinstance(t, int) and t < back):
                eng.wait_ge(s[name], per * t + (per if i is None else i + 1) - per * back)

        def schedule(eng, chunk, split=None):
            def body(e, p):
                ahead = split and (lambda piece: split(e, p, piece))
                chunk(e - 1, 1 - p, 2, ahead)
                chunk(e - 1, 1 - p, 3, ahead)
                chunk(e, p, 0)
                chunk(e, p, 1)

            chunk(0, 0, 0)
            chunk(0, 0, 1)
            body(1, 1)
            with eng.Fori(1, E // 2) as i:
                for j in range(2):
                    body(2 * i + j, j)
            chunk(E - 1, 1, 2)
            chunk(E - 1, 1, 3)

        def bias_group(e, q):
            u = NQ * e + q - 2 if isinstance(e, int) else None
            return u if u is not None and 0 <= u < NQ else None

        def bias_there(eng, e, p):
            eng.wait_ge(gub_landed[p], 8 * e + (16 - 8 * p))

        @block.sync
        def _(sp):
            def load(e, p):
                if not (isinstance(e, int) and e == 0):
                    weights.load(sp, e)
                need(sp, "gate", e, back=2, per=WS)
                need(sp, "up", e, back=2, per=WS)
                sp.dma_start(gub[p][:, :], io["gub"][bass.ds(e, 1)].rearrange("o p j -> p (o j)"))\
                  .then_inc(gub_landed[p], 16)

            sp.dma_start(dnb[:, :], io["dnb"]).then_inc(dnb_landed, 16)
            load(0, 0)
            load(1, 1)
            with sp.Fori(1, E // 2) as i:
                for j in range(2):
                    load(2 * i + j, j)
            o = out.rearrange("(t b) s d -> (b s) t d", b=2)
            for q in range(NQ):
                sp.wait_ge(s["y"], TQ * (NQ * (E - 1) + q + 1))
                sp.dma_start(o[:, TQ * q:TQ * (q + 1), :], rows[:, TQ * q:TQ * (q + 1), :]).then_inc(stored, 16)
            sp.wait_ge(stored, 16 * NQ)

        @block.scalar
        def _(act):
            def split(e, p, piece):
                if piece == 0:
                    need(act, "gu_u", e, back=2, per=WS)
                if piece == NI:
                    need(act, "down", e, back=2, per=2 * NQ)
                weights.split_high(act, e, p, piece)

            def high(e, q, it):
                need(act, "h", WS * e + NI * q + it)
                if it == 0:
                    need(act, "down", NQ * e + q, back=2, per=2)
                act.activation(a_hi[q % 2][:, it, :], prod[it % 2][:, :], ACT.Copy, scale=1 / ALPHA)\
                   .then_inc(s["a_hi"], 1)

            def chunk(e, p, q, ahead=None):
                start = isinstance(e, int) and e == 0 and q == 0
                g = bias_group(e, q)
                if q == 0:
                    bias_there(act, e, p)
                for it in range(NI):
                    w, v = WS * e + (NI * q + it), it % 2
                    need(act, "gu_u", w)
                    need(act, "h", w, back=2)
                    act.activation(up[v][:, :], ps_u[v][:, :], ACT.Identity, bias=gub[p][:, NI + it:NI + it + 1])\
                       .then_inc(s["up"], 1)
                    need(act, "gate", w)
                    act.activation(silu[v][:, :], gate[v][:, :], ACT.Silu, scale=ALPHA).then_inc(s["silu"], 1)
                    if it:
                        high(e, q, it - 1)
                    elif not start:
                        high(e, q - 1, NI - 1)
                    if ahead:
                        ahead(NI * (q - 2) + it)
                    if start and it == 1:
                        act.wait_ge(ranked, SHIFTED)
                        act.activation(comb[:, :, :], comb[:, :, :], ACT.Exp).then_inc(exp_done, 1)
                    if g is not None and it == 1:
                        act.wait_ge(ct_done, g + 1)
                        if g:
                            act.wait_ge(bias_done, g)
                        act.activation(comb_t[:, :], ps_c[0:E, :], ACT.Copy).then_inc(ct_copied, 1)

            schedule(act, chunk, split)
            high(E - 1, NQ - 1, NI - 1)

        @block.vector
        def _(dve):
            def over(x, shape=(P, NTILE, E)):
                return x.rearrange("p (t o) -> p t o", o=1).to_broadcast(list(shape))

            routing = [0]

            def step(ins):
                routing[0] += 1
                ins.then_inc(ranked, 1)
                dve.wait_ge(ranked, routing[0])

            def route_start():
                step(dve.tensor_reduce(best[:, :], logits[:, :, :], AX.X, ALU.max))
                step(dve.tensor_tensor(comb[:, :, :], logits[:, :, :], over(best[:, :]), ALU.subtract))
                assert routing[0] == SHIFTED
                step(dve.memset(rank[:, :, :], 0.0))

            def route_rank(j):
                for op, at in ((ALU.is_gt, slice(0, j)), (ALU.is_ge, slice(j + 1, E))):
                    k = at.stop - at.start
                    if k:
                        step(dve.tensor_tensor(beats[:, :, at], over(logits[:, :, j], (P, NTILE, k)),
                                               logits[:, :, at], op))
                        step(dve.tensor_tensor(rank[:, :, at], rank[:, :, at], beats[:, :, at], ALU.add))

            def route_end():
                step(dve.tensor_scalar(rank[:, :, :], rank[:, :, :], float(TOP), None, ALU.is_lt))
                dve.wait_ge(exp_done, 1)
                step(dve.tensor_tensor(comb[:, :, :], comb[:, :, :], rank[:, :, :], ALU.mult))
                step(dve.tensor_reduce(total[:, :], comb[:, :, :], AX.X, ALU.add))
                step(dve.reciprocal(total[:, :], total[:, :]))
                dve.tensor_tensor(comb[:, :, :], comb[:, :, :], over(total[:, :]), ALU.mult).then_inc(combined, 1)
                dve.wait_ge(combined, 1)

            def route(step):
                if step == 0:
                    route_start()
                if 1 <= step <= E // 2 + 1:
                    for j in (2 * step - 2, 2 * step - 1):
                        if j < E:
                            route_rank(j)
                if step == E // 2 + 1:
                    route_end()

            def low(e, q, it):
                need(dve, "a_hi", WS * e + (NI * q + it))
                dve.scalar_tensor_tensor(a_lo[q % 2][:, it, :], prod[it % 2][:, :], 1 / ALPHA,
                                         a_hi[q % 2][:, it, :].bitcast(F32), ALU.mult, ALU.subtract)\
                   .then_inc(s["a_lo"], 1)

            def activate(e, q, it):
                w, v = WS * e + (NI * q + it), it % 2
                need(dve, "up", w)
                dve.tensor_scalar(up[v][:, :], up[v][:, :], LIMIT, -LIMIT, ALU.min, ALU.max).then_inc(s["clip"], 1)
                need(dve, "clip", w)
                need(dve, "a_lo", w, back=2)
                need(dve, "silu", w)
                dve.scalar_tensor_tensor(prod[v][:, :], up[v][:, :], 1.0, silu[v][:, :], ALU.add, ALU.mult)\
                   .then_inc(s["h"], 1)

            def add(e, q, d):
                need(dve, "down", NQ * e + q, per=2, i=d)
                for i in range(2):
                    t = TQ * q + 2 * d + i
                    dve.scalar_tensor_tensor(rows[:, t, :], ps_d[d][:, i * D:(i + 1) * D], comb[:, t, bass.ds(e, 1)],
                                             rows[:, t, :], ALU.mult, ALU.add).then_inc(s["y"], 1)

            def chunk(e, p, q, ahead=None):
                start = isinstance(e, int) and e == 0 and q == 0
                second = isinstance(e, int) and e == 0 and q == 1
                g = bias_group(e, q)
                u = NQ * e + q
                if q == 0:
                    bias_there(dve, e, p)
                before = (e, q - 1) if q else (e - 1, NQ - 1)
                twice = (e, q - 2) if q >= 2 else (e - 1, q + 2)
                for it in range(NI):
                    w, v = WS * e + (NI * q + it), it % 2
                    need(dve, "gu_g", w)
                    need(dve, "silu", w, back=2)
                    dve.tensor_scalar(gate[v][:, :], ps_g[v][:, :], gub[p][:, it:it + 1], LIMIT, ALU.add, ALU.min)\
                       .then_inc(s["gate"], 1)
                    if it >= 2:
                        low(e, q, it - 2)
                    elif not start:
                        low(*before, NI - 2 + it)
                    if it:
                        activate(e, q, it - 1)
                    elif not start:
                        activate(*before, NI - 1)
                    if it == 0 and not start and not second:
                        add(*twice, 1)
                    if start or second:
                        route(NI * q + it)
                    if it == NI - 1 and not start:
                        add(*before, 0)
                        if g is not None:
                            add_bias(g, u)
                    if ahead:
                        ahead(NI * (q - 2) + it)
            def add_bias(g, u):
                dve.wait_ge(bias_done, g + 1)
                dve.wait_ge(s["y"], TQ * (u - 1) + 2)
                for h, bank in enumerate((ps_b, ps_c)):
                    t = 4 * g + 2 * h
                    dve.tensor_tensor(rows[:, t:t + 2, :], rows[:, t:t + 2, :],
                                      bank[:, :].rearrange("p (t d) -> p t d", d=D), ALU.add).then_inc(biased, 1)
                dve.wait_ge(biased, 2 * (g + 1))

            schedule(dve, chunk, lambda e, p, piece: weights.split_low(dve, e, p, piece))
            low(E - 1, NQ - 1, NI - 2)
            activate(E - 1, NQ - 1, NI - 1)
            low(E - 1, NQ - 1, NI - 1)
            add(E - 1, NQ - 2, 1)
            for t in range(TQ):
                dve.wait_ge(s["down"], 2 * (NQ * E - 1) + t + 1)
                n = TQ * (NQ - 1) + t
                dve.scalar_tensor_tensor(rows[:, n, :], LAST_DOWN[t][:, 0:D], comb[:, n, E - 1:E], rows[:, n, :],
                                         ALU.mult, ALU.add).then_inc(s["y"], 1)

        @block.tensor
        def _(pe):
            def down(e, p, q, d):
                u = NQ * e + q
                if d == 0:
                    need(pe, "a_lo", u, per=NI)
                pe.wait_ge(weights.low, PIECES * e + PIECES)
                need(pe, "y", u, back=1, per=TQ, i=2 * d + 1)
                for i in range(2):
                    r = slice((2 * d + i) * P, (2 * d + i + 1) * P)
                    for k in range(NI):
                        for n, (x, y) in enumerate(hi_lo_products(a_hi[q % 2], a_lo[q % 2], dn_hi[p], dn_lo[p])):
                            mm = pe.matmul(ps_d[d][:, i * D:(i + 1) * D], x[:, k, r], y[:, k, :],
                                           start=k == 0 and n == 0, stop=k == NI - 1 and n == 2)
                mm.then_inc(s["down"], 1)

            def chunk(e, p, q, ahead=None):
                start = isinstance(e, int) and e == 0 and q == 0
                before = (e, p, q - 1) if q else (e - 1, 1 - p, NQ - 1)
                g = bias_group(e, q)
                if q == 0:
                    pe.wait_ge(weights.low, PIECES * e + NI)
                r = slice(q * TC, (q + 1) * TC)
                for it in range(NI):
                    w, v = WS * e + (NI * q + it), it % 2
                    for bank, made, free, o in ((ps_g, "gu_g", "gate", 0), (ps_u, "gu_u", "up", I)):
                        need(pe, free, w, back=2)
                        c = slice(o + it * P, o + (it + 1) * P)
                        i = 0
                        for k in range(DK):
                            for x, y in hi_lo_products(gu_hi[p], gu_lo[p], xt_hi, xt_lo):
                                mm = pe.matmul(bank[v][:, :], x[:, k, c], y[:, k, r], start=i == 0, stop=i == 5)
                                i += 1
                        mm.then_inc(s[made], 1)
                    if it >= 2 and not start:
                        down(*before, it - 2)
                    if g is not None and it == 0:
                        turn_weights(g)
                    if g is not None and it == 2:
                        biases(g)

            def turn_weights(g):
                if g == 0:
                    pe.wait_ge(combined, 1)
                else:
                    pe.wait_ge(biased, 2 * g)
                for t in range(4):
                    mm = pe.transpose(ps_c[0:E, t * P:(t + 1) * P], comb[:, 4 * g + t, :], ident[:, :])
                mm.then_inc(ct_done, 1)

            def biases(g):
                if g == 0:
                    pe.wait_ge(dnb_landed, 16)
                pe.wait_ge(ct_copied, g + 1)
                for t in range(4):
                    mm = pe.matmul((ps_b, ps_c)[t // 2][:, t % 2 * D:(t % 2 + 1) * D], comb_t[:, t * P:(t + 1) * P],
                                   dnb[:, :], start=True, stop=True)
                mm.then_inc(bias_done, 1)

            schedule(pe, chunk)
            u = NQ * E - 1
            need(pe, "y", u, back=1, per=TQ)
            need(pe, "gate", u, per=NI)
            need(pe, "up", u, per=NI)
            for k in range(NI):
                need(pe, "a_lo", u, per=NI, i=k)
                for t in range(TQ):
                    for n, (x, y) in enumerate(hi_lo_products(a_hi[(NQ - 1) % 2], a_lo[(NQ - 1) % 2], dn_hi[1], dn_lo[1])):
                        mm = pe.matmul(LAST_DOWN[t][:, 0:D], x[:, k, t * P:(t + 1) * P], y[:, k, :],
                                       start=k == 0 and n == 0, stop=k == NI - 1 and n == 2)
                    if k == NI - 1:
                        mm.then_inc(s["down"], 1)


def program(nc, io, out):
    NTILE = ROWS // P
    with ExitStack() as outer:
        def sb(name, shape, dt=F32):
            return outer.enter_context(nc.sbuf_tensor(name, shape, dt))

        ident = sb("ident", [P, P])
        rows = sb("rows", [P, NTILE, D])
        mean = sb("mean", [P, NTILE])
        rstd = sb("rstd", [P, NTILE])
        stage = sb("stage", [P, 2, CT, 2 * NT])
        halves = sb("halves", [P, 4, CT, 2 * NT], F32R)
        attention_weights = AttentionWeights(nc, outer, io, stage, halves, ident)
        cross_attention(nc, io, rows, mean, rstd, ident, stage, halves, attention_weights)
        xt_hi = sb("xt_hi", [P, DK, ROWS], F32R)
        xt_lo = sb("xt_lo", [P, DK, ROWS], F32R)
        logits = sb("logits", [P, NTILE, E])
        weights = ExpertWeights(nc, outer, io)
        latent_attention(nc, io, rows, mean, rstd, ident, attention_weights, xt_hi, xt_lo, logits, weights)
        experts(nc, io, rows, xt_hi, xt_lo, logits, ident, weights, out)


def lay_out(inputs):
    import numpy as np
    a = {k: np.asarray(v) for k, v in inputs.items()}
    xa, la, ff = "L0_xattn_", "L0_attn_", "L0_ffn_"
    ctx = np.zeros((B, NBLK, BF), np.float32)
    ctx.reshape(B, NBLK * STRIDE, D)[:, :CTX] = a["ctx_1024"]
    t = ctx[:, :NT].reshape(PAIRS, 2, NT, CH, CT, P).transpose(0, 3, 5, 4, 1, 2).reshape(PAIRS, CH, P, CT, 2 * NT)
    col = [a[la + "bq"]] + [np.repeat(a[la + f"g{i}"], HD) for i in (1, 3, 4, 2)] + [a[la + "ln_g"], a[la + "ln_b"]]
    io = {"x": a["x"], "ctxN": ctx, "ctxT": t, "qa_qT": a[xa + "qa_q"].T, "qa_wk": a[xa + "qa_wk"],
          "qa_wvT": a[xa + "qa_wv"].T, "ws_w": a[xa + "ws_w"], "mn_w": a[xa + "mn_w"], "hn_w": a[xa + "hn_w"],
          "bias": np.concatenate([a[la + n] for n in ("bk2", "bv2", "bk1", "bv1", "bo")]
                                 + [a[ff + "router_bias"]])[None],
          "cols": np.stack(col).reshape(7, DK, P).transpose(2, 0, 1), "router_w": a[ff + "router_weight"].T}
    io |= {"W" + n: a[la + "W" + n].T for n in ("q", "k1", "v1", "k2", "v2", "o")}
    io |= {"gu": a[ff + "gate_up_proj"].transpose(0, 2, 1), "dn": a[ff + "down_proj"].transpose(0, 2, 1),
           "gub": a[ff + "gate_up_proj_bias"].reshape(E, 2 * I // P, P).transpose(0, 2, 1),
           "dnb": a[ff + "down_proj_bias"]}
    return {k: np.ascontiguousarray(v) for k, v in io.items()}


def kernel(**inputs):
    import concourse.bacc as bacc
    from concourse.bass_utils import run_bass_kernel_spmd

    arrays = lay_out(inputs)
    nc = bacc.Bacc("TRN2", target_bir_lowering=False, num_devices=1)
    io = {k: nc.dram_tensor(k, v.shape, F32, kind="ExternalInput").ap() for k, v in arrays.items()}
    out = nc.dram_tensor("out", (B, S, D), F32, kind="ExternalOutput").ap()
    program(nc, io, out)
    return run_bass_kernel_spmd(nc, [arrays], core_ids=[0]).results[0]["out"]
```

```python
import concourse.bass as bass
from concourse import mybir
from contextlib import ExitStack

F32 = mybir.dt.float32
F32R = mybir.dt.float32r
ALU = mybir.AluOpType
ACT = mybir.ActivationFunctionType
AX = mybir.AxisListType

P = 128
B, S, D = 32, 64, 256
CTX = 1601
STRIDE, WIN = 8, 16
NWIN = (CTX + STRIDE - (CTX - WIN) % STRIDE - WIN) // STRIDE + 1
BF = STRIDE * D
NROW = 112
NREST = 96
NBLK = NROW + NREST
NT = 202
PAIRS = B // 2
CH = 4
CF = BF // CH
CT = CF // P
FT = WIN * D // P
DK = D // P
SCALE = 1.0 / D ** 0.5


def hi_lo_products(hi_a, lo_a, hi_b, lo_b):
    return ((hi_a, hi_b), (hi_a, lo_b), (lo_a, hi_b))


H = 16
HD = D // H
E = 8
ROWS = B * S
LN_EPS = 1e-5
RMS_EPS = 1.1920929e-07


class RowNorms:

    def __init__(self, nc, outer, rows, mean, rstd):
        def sb(name, shape):
            return outer.enter_context(nc.sbuf_tensor(name, shape, F32))

        self.rows, self.mean, self.rstd = rows, mean, rstd
        self.mem = sb("mem", [P, D])
        self.rms_w = sb("rms_w", [P, 2, D])
        self.eps = sb("eps", [P, 2])
        self.same = sb("same", [P, P])
        self.square = sb("square", [P, D])
        self.ss = sb("ss", [P, 2])
        self.stat = sb("stat", [P, 6])
        self.mv = sb("mv", [P, 2])
        self.std = sb("std", [P, 4])
        self.inv = sb("inv", [P, 3])
        self.hn = sb("hn", [P, D])
        self.memw = sb("memw", [P, D])
        self.mem_copied = outer.enter_context(nc.semaphore("mem_copied"))
        self.x_landed = outer.enter_context(nc.semaphore("x_landed"))
        self.s = {n: outer.enter_context(nc.semaphore("n_" + n)) for n in (
            "sq1 gs1 sd1 st0 mv0 sd0 iv h mw hs sq2 gs2 sd2 iv2 gr x1 st1 mv1 sd3 mu rs").split()}

    def need(self, eng, name, t, back=0):
        if not (isinstance(t, int) and t < back):
            eng.wait_ge(self.s[name], t + 1 - back)

    def row(self, t):
        return self.rows[:, bass.ds(t, 1), :].rearrange("p o d -> p (o d)")

    def root(self, act, src, dst, which, name, scale=1.0):
        act.activation(self.std[:, dst:dst + 1], src, ACT.Sqrt, bias=self.eps[:, which:which + 1], scale=scale)\
           .then_inc(self.s[name], 1)

    def act_a(self, act, t, bank):
        act.wait_ge(self.mem_copied, t + 1)
        self.need(act, "gs1", t, back=1)
        act.activation(self.square[:, :], self.mem[:, :], ACT.Square, accum_out=self.ss[:, 0:1])\
           .then_inc(self.s["sq1"], 1)

    def act_b(self, act, t, bank):
        self.need(act, "gs1", t)
        self.need(act, "iv", t, back=1)
        self.root(act, bank[:, 0:1], 0, 0, "sd1", 1.0 / (S * D))
        self.need(act, "mv0", t)
        self.root(act, self.mv[:, 1:2], 1, 1, "sd0")

    def act_c(self, act, t):
        self.need(act, "hs", t)
        self.need(act, "gs2", t, back=1)
        self.need(act, "sq1", t)
        act.activation(self.square[:, :], self.hn[:, :], ACT.Square, accum_out=self.ss[:, 1:2])\
           .then_inc(self.s["sq2"], 1)

    def act_d(self, act, t, bank):
        self.need(act, "gs2", t)
        self.need(act, "iv2", t, back=1)
        self.root(act, bank[:, 2:3], 2, 0, "sd2", 1.0 / (S * D))

    def act_e(self, act, t):
        self.need(act, "mv1", t)
        self.need(act, "rs", t, back=1)
        self.root(act, self.mv[:, 1:2], 3, 1, "sd3")

    def pe_sum(self, pe, t, i, bank):
        self.need(pe, ("sq1", "sq2")[i], t)
        self.need(pe, ("sd1", "sd2")[i], t, back=1)
        pe.matmul(bank[:, 2 * i:2 * i + 1], self.same[:, :], self.ss[:, i:i + 1], start=True, stop=True)\
          .then_inc(self.s[("gs1", "gs2")[i]], 1)

    def dve_stats(self, dve, t, after, st, mv):
        dve.wait_ge(self.x_landed, 5 * 16)
        self.need(dve, *after)
        dve.bn_stats(self.stat[:, :], self.row(t)).then_inc(self.s[st], 1)
        dve.wait_ge(self.x_landed, 5 * 16)
        self.need(dve, st, t)
        dve.bn_aggr(self.mv[:, :], self.stat[:, :]).then_inc(self.s[mv], 1)

    def dve_a(self, dve, t):
        self.dve_stats(dve, t, ("mu", t, 1), "st0", "mv0")

    def dve_b(self, dve, t):
        inv, hn, memw = self.inv, self.hn, self.memw
        self.need(dve, "sd1", t)
        self.need(dve, "sd0", t)
        dve.reciprocal(inv[:, 0:2], self.std[:, 0:2]).then_inc(self.s["iv"], 1)
        self.need(dve, "iv", t)
        dve.tensor_scalar(hn[:, :], self.row(t), self.mv[:, 0:1], inv[:, 1:2], ALU.subtract, ALU.mult)\
           .then_inc(self.s["h"], 1)
        dve.scalar_tensor_tensor(memw[:, :], self.mem[:, :], inv[:, 0:1], self.rms_w[:, 0, :], ALU.mult, ALU.mult)\
           .then_inc(self.s["mw"], 1)
        self.need(dve, "mw", t)
        dve.tensor_tensor(hn[:, :], hn[:, :], memw[:, :], ALU.add).then_inc(self.s["hs"], 1)

    def dve_c(self, dve, t):
        inv, memw = self.inv, self.memw
        self.need(dve, "sd2", t)
        dve.reciprocal(inv[:, 2:3], self.std[:, 2:3]).then_inc(self.s["iv2"], 1)
        self.need(dve, "iv2", t)
        dve.scalar_tensor_tensor(memw[:, :], self.hn[:, :], inv[:, 2:3], self.rms_w[:, 1, :], ALU.mult, ALU.mult)\
           .then_inc(self.s["gr"], 1)
        self.need(dve, "gr", t)
        dve.tensor_tensor(self.row(t), self.row(t), memw[:, :], ALU.add).then_inc(self.s["x1"], 1)
        self.dve_stats(dve, t, ("x1", t), "st1", "mv1")

    def dve_d(self, dve, t):
        self.need(dve, "mv1", t)
        dve.tensor_copy(self.mean[:, bass.ds(t, 1)], self.mv[:, 0:1]).then_inc(self.s["mu"], 1)
        self.need(dve, "sd3", t)
        dve.reciprocal(self.rstd[:, bass.ds(t, 1)], self.std[:, 3:4]).then_inc(self.s["rs"], 1)


def cross_attention(nc, io, rows, mean, rstd, ident, stage, halves, attention_weights, norms):
    ctx = ExitStack()

    def sb(name, shape, dt=F32):
        return ctx.enter_context(nc.sbuf_tensor(name, shape, dt))

    def pb(name):
        return ctx.enter_context(nc.psum_tensor(name, [P, 512], F32))

    def sem(name):
        return ctx.enter_context(nc.semaphore(name))

    with ctx:
        mem, mem_copied, x_landed, rms_w = norms.mem, norms.mem_copied, norms.x_landed, norms.rms_w
        t_raw = [stage[:, i] for i in range(2)]
        t_hi = [halves[:, i] for i in range(2)]
        t_lo = [halves[:, 2 + i] for i in range(2)]
        n_raw = [sb(f"n_raw{i}", [NROW, 2, 2, CF]) for i in range(2)]
        n_hi = [sb(f"n_hi{i}", [NROW, 2, CF], F32R) for i in range(2)]
        n_lo = [sb(f"n_lo{i}", [NROW, 2, CF], F32R) for i in range(2)]
        attention_weights.place_staged_bias(n_raw[0][:, :, :, :].rearrange("p k b f -> p (k b f)"))
        g_hi = sb("g_hi", [P, FT // 2, 2, S], F32R)
        g_lo = sb("g_lo", [P, FT // 2, 2, S], F32R)
        v_hi = sb("v_hi", [P, FT, D], F32R)
        v_lo = sb("v_lo", [P, FT, D], F32R)
        w_hi = [sb(f"w_hi{i}", [P, 2, CT, 2, S], F32R) for i in range(2)]
        w_lo = [sb(f"w_lo{i}", [P, 2, CT, 2, S], F32R) for i in range(2)]
        pt_hi = sb("pt_hi", [NROW, 2, 2, 2, S], F32R)
        pt_lo = sb("pt_lo", [NROW, 2, 2, 2, S], F32R)
        pw = [sb(f"pw{i}", [P, CF]) for i in range(2)]
        prob = sb("prob", [P, 1 + 2 * NROW])
        other = sb("other", [P, NWIN])
        score = sb("score", [P, NWIN])
        top = sb("top", [P, 1])
        ntop = sb("ntop", [P, 1])
        den = sb("den", [P, 1])
        a1 = sb("a1", [P, DK, S])
        rden = sb("rden", [P, PAIRS])
        ws = rows[:, :, :].rearrange("p (s m x) d -> p s m (x d)", s=2, m=DK)
        qa_q = sb("qa_q_sb", [P, DK, S])
        qa_wk, qa_wv = [x[:, :].rearrange("p (k d) -> p k d", k=DK) for x in pw]

        ps_s = pb("ps_s")
        ps_w = [pb(f"ps_w{i}") for i in range(2)]
        ps_v = [pb(f"ps_v{i}") for i in range(2)]
        ps_fold = ps_w + ps_v
        ps_m = pb("ps_m")
        ps_p = pb("ps_p")
        ps_a = pb("ps_a")

        qa_landed = sem("qa_landed")
        ws_landed = [sem(f"ws_landed{i}") for i in range(2)]
        a1_ready = sem("a1_ready")
        a1_copied = sem("a1_copied")
        fold_ready = sem("fold_ready")
        fold_hi = sem("fold_hi")
        fold_lo = sem("fold_lo")
        zeroed = sem("zeroed")
        t_landed = [sem(f"t_landed{i}") for i in range(2)]
        n_landed = [sem(f"n_landed{i}") for i in range(2)]
        t_hi_done = sem("t_hi_done")
        t_lo_done = sem("t_lo_done")
        n_hi_done = sem("n_hi_done")
        n_lo_done = sem("n_lo_done")
        scores_done = sem("scores_done")
        pw_done = sem("pw_done")
        pw_copied = sem("pw_copied")
        turned = sem("turned")
        w_hi_done = sem("w_hi_done")
        w_lo_done = sem("w_lo_done")
        mem_done = sem("mem_done")
        other_done = sem("other_done")
        added = sem("added")
        top_done = sem("top_done")
        ntop_done = sem("ntop_done")
        exp_done = sem("exp_done")
        rden_done = sem("rden_done")
        pt_ready = sem("pt_ready")
        pt_hi_done = sem("pt_hi_done")
        pt_lo_done = sem("pt_lo_done")
        block = ctx.enter_context(nc.Block())

        WCH = 4
        WF = WIN * D // WCH

        @block.sync
        def _(sp):
            def load_t(t, c):
                sp.dma_start(t_raw[c % 2][:, :, :], io["ctxT"][bass.ds(t, 1), c].rearrange("o p k n -> p (o k) n"))\
                  .then_inc(t_landed[c % 2], 16)

            def load_n(t, c):
                for rows, kt in ((NROW, 0), (NREST, 1)):
                    sp.dma_start(n_raw[c % 2][0:rows, kt],
                                 io["ctxN"][bass.ds(2 * t, 2), kt * NROW:kt * NROW + rows, c * CF:(c + 1) * CF]
                                 .rearrange("b p f -> p b f")).then_inc(n_landed[c % 2], 16)

            sp.dma_start(qa_q[:, :, :], io["qa_qT"].rearrange("(k p) q -> p k q", p=P)).then_inc(qa_landed, 16)
            sp.dma_start(qa_wk[:, :, :], io["qa_wk"].rearrange("(k p) m -> p k m", p=P)).then_inc(qa_landed, 16)
            sp.dma_start(qa_wv[:, :, :], io["qa_wvT"].rearrange("(k p) h -> p k h", p=P)).then_inc(qa_landed, 16)
            for j in range(WCH):
                if j == 2:
                    for c in range(2):
                        load_t(0, c)
                if j >= 2:
                    sp.wait_ge(fold_ready, 5 * (j - 1))
                sp.dma_start(ws[:, j % 2], io["ws_w"][:, j * WF:(j + 1) * WF].rearrange("(k p) f -> p k f", p=P))\
                  .then_inc(ws_landed[j % 2], 16)

            for i, w in enumerate(("mn_w", "hn_w")):
                for b in range(2):
                    sp.dma_start(rms_w[b * S:(b + 1) * S, i, :], io[w]).then_inc(x_landed, 16)
            for c in range(2, CH):
                sp.wait_ge(t_lo_done, c - 1)
                load_t(0, c)
            sp.wait_ge(zeroed, 3)
            for c in range(CH):
                sp.wait_ge(t_lo_done, CH + c - 1)
                load_t(1, c)
                if c >= 2:
                    sp.wait_ge(n_lo_done, 2 * (c - 1))
                load_n(0, c)
                if c == 1:
                    sp.wait_ge(fold_ready, 20)
                    sp.dma_start(rows[:, :, :], io["x"].rearrange("(t b) s d -> (b s) t d", b=2))\
                      .then_inc(x_landed, 16)
            with sp.Fori(1, PAIRS - 1) as t:
                for c in range(CH):
                    sp.wait_ge(t_lo_done, CH * t + (CH + c - 1))
                    load_t(t + 1, c)
                    sp.wait_ge(n_lo_done, 2 * CH * t + 2 * (c - 1))
                    load_n(t, c)
            for c in range(CH):
                sp.wait_ge(n_lo_done, 2 * CH * (PAIRS - 1) + 2 * (c - 1))
                load_n(PAIRS - 1, c)
                if c == 0:
                    sp.wait_ge(t_lo_done, CH * PAIRS)
                    attention_weights.load(sp)
            sp.wait_ge(n_lo_done, 2 * CH * PAIRS - 2)
            attention_weights.load_bias(sp)

        @block.gpsimd
        def _(pool):
            tiles = [n_raw[0][NREST:NROW, 1, :, :], n_raw[1][NREST:NROW, 1, :, :], prob[:, :], ident[:, :]]
            for i, tile in enumerate(tiles):
                pool.memset(tile, 0.0).then_inc(zeroed, 1)
                pool.wait_ge(zeroed, i + 1)
            pool.affine_select(out=ident[:, :], in_=ident[:, :], compare_op=ALU.not_equal, fill=1.0, base=0,
                               pattern=[[-1, P]], channel_multiplier=1).then_inc(zeroed, 1)
            pool.wait_ge(zeroed, 5)
            consts = [(norms.eps[:, 0:1], RMS_EPS), (norms.eps[:, 1:2], LN_EPS), (norms.same[:, :], 0.0),
                      (norms.same[0:S, 0:S], 1.0), (norms.same[S:P, S:P], 1.0)]
            for i, (tile, value) in enumerate(consts):
                pool.memset(tile, value).then_inc(zeroed, 1)
                pool.wait_ge(zeroed, 6 + i)
            attention_weights.make_constants(pool)

        def fold_targets(side, i):
            if side == "g":
                j, = i
                at = slice(8 * (j % 2), 8 * (j % 2) + 8)
                return [x[:, at, j // 2, :] for x in (g_hi, g_lo)]
            j, k = i
            return [x[:, 8 * j + 2 * k:8 * j + 2 * k + 2, :] for x in (v_hi, v_lo)]

        def fold_banks():
            n = 0
            for j in range(WCH):
                for side, i in [("g", (j,))] + [("v", (j, k)) for k in range(4)]:
                    yield n, j, side, i
                    n += 1

        FIRST_SPLITS = {3: 0, 6: 1, 14: 2, 16: 3}
        FIRST_SCORES = {12: (0, 1), 17: (2, 3)}

        def fold_src(n, side):
            return ps_fold[n % 4][:, :].rearrange("p (k q) -> p k q", q=S if side == "g" else D)

        @block.scalar
        def _(act):

            def split_t(t, c):
                act.wait_ge(t_landed[c % 2], 16 * (2 * t + (c // 2 + 1)))
                if not (isinstance(t, int) and t == 0 and c < 2):
                    act.wait_ge(scores_done, CH * t + (c - 1))
                act.activation(t_hi[c % 2][:, :, :], t_raw[c % 2][:, :, :], ACT.Copy).then_inc(t_hi_done, 1)

            def split_n(t, c, b):
                if b == 0:
                    act.wait_ge(n_landed[c % 2], 32 * (2 * t + (c // 2 + 1)))
                if not (isinstance(t, int) and t == 0 and c == 0):
                    act.wait_ge(pw_done, 2 * CH * t + (2 * c + b - 1))
                act.activation(n_hi[b][:, :, :], n_raw[c % 2][:, :, b, :], ACT.Copy).then_inc(n_hi_done, 1)

            def copy_pw(t, c, b):
                act.wait_ge(pw_done, 2 * CH * t + (2 * c + b + 1))
                if not (isinstance(t, int) and t == 0 and c == 0):
                    act.wait_ge(turned, 2 * CH * t + (2 * c + b - 1))
                act.activation(pw[b][:, :], ps_w[b][:, :], ACT.Copy).then_inc(pw_copied, 1)

            def copy_w(t, c, b):
                act.wait_ge(turned, 2 * CH * t + (2 * c + b + 1))
                if b == 0 and not (isinstance(t, int) and t == 0 and c < 2):
                    act.wait_ge(mem_done, CH * t + (c - 1))
                act.activation(w_hi[c % 2][:, :, :, b, :].rearrange("p h k q -> p k h q"),
                               ps_v[b][:, :].rearrange("p (k h q) -> p k h q", k=CT, h=2),
                               ACT.Copy).then_inc(w_hi_done, 1)

            def softmax(t):
                act.wait_ge(scores_done, CH * t + CH)
                if not (isinstance(t, int) and t == 0):
                    act.wait_ge(added, 2 * t)
                act.activation(other[0:S, :], ps_s[S:P, 1:1 + NWIN], ACT.Copy).then_inc(other_done, 1)
                act.activation(other[S:P, :], ps_s[0:S, NT:NT + NWIN], ACT.Copy).then_inc(other_done, 1)

            def exponent(t):
                act.wait_ge(ntop_done, t + 1)
                if not (isinstance(t, int) and t == 0):
                    act.wait_ge(pt_ready, t)
                    act.wait_ge(rden_done, t)
                act.activation(prob[:, 1:1 + NWIN], score[:, :], ACT.Exp, bias=ntop[:, :], scale=SCALE,
                               accum_out=den[:, :]).then_inc(exp_done, 1)

            def copy_pt(t):
                act.wait_ge(pt_ready, t + 1)
                if not (isinstance(t, int) and t == 0):
                    act.wait_ge(pw_done, 2 * CH * t)
                act.activation(pt_hi[:, :, :, :, :].rearrange("p k b h q -> p (k b h q)"),
                               ps_p[0:NROW, :], ACT.Copy).then_inc(pt_hi_done, 1)

            def copy_mem(t):
                act.wait_ge(mem_done, CH * t + CH)
                act.wait_ge(rden_done, t + 1)
                norms.need(act, "mw", t, back=1)
                act.activation(mem[:, :], ps_m[:, 0:D], ACT.Copy, scale=rden[:, bass.ds(t, 1)]).then_inc(mem_copied, 1)

            def prepare(j):
                if j == 0:
                    act.wait_ge(scores_done, CH * PAIRS)
                attention_weights.split_high(act, j)

            def step(t, ahead, last):
                first = isinstance(t, int) and t == 0
                for c in range(CH):
                    if c:
                        copy_w(t, c - 1, 1)
                    elif not first:
                        copy_w(t - 1, CH - 1, 1)
                    split_n(t, c, 1)
                    if last and c:
                        prepare(2 * c - 2)
                        prepare(2 * c - 1)
                    if c == CH - 1 and not first:
                        norms.act_e(act, t - 1)
                    if c == CH - 1 and not last:
                        softmax(t + 1)
                    if c < CH - 1:
                        if not last:
                            split_t(t + 1, c + 1)
                    elif ahead:
                        split_t(t + 2, 0)
                    if c == 2 and not first:
                        norms.act_c(act, t - 1)
                    copy_pw(t, c, 0)
                    if c < CH - 1:
                        split_n(t, c + 1, 0)
                        copy_pw(t, c, 1)
                        copy_w(t, c, 0)
                    else:
                        if not last:
                            exponent(t + 1)
                        copy_pw(t, c, 1)
                        copy_w(t, c, 0)
                        if not last:
                            split_n(t + 1, 0, 0)
                            copy_pt(t + 1)
                    if c == 0 and not first:
                        copy_mem(t - 1)
                    if c < CH - 1 and not first:
                        (norms.act_a, norms.act_b, norms.act_d)[c](act, t - 1, ps_a)

            for n, j, side, i in fold_banks():
                act.wait_ge(fold_ready, n + 1)
                act.activation(fold_targets(side, i)[0], fold_src(n, side), ACT.Copy).then_inc(fold_hi, 1)
                if n in FIRST_SPLITS:
                    split_t(0, FIRST_SPLITS[n])
                if n == 17:
                    softmax(0)
                    split_t(1, 0)
                if n == 18:
                    act.wait_ge(zeroed, 10)
                    exponent(0)
            split_n(0, 0, 0)
            copy_pt(0)
            step(0, True, False)
            with act.Fori(1, PAIRS - 2) as t:
                step(t, True, False)
            step(PAIRS - 2, False, False)
            step(PAIRS - 1, False, True)
            copy_w(PAIRS - 1, CH - 1, 1)
            attention_weights.split_vectors_high(act)
            copy_mem(PAIRS - 1)

        @block.vector
        def _(dve):
            dve.wait_ge(a1_ready, 1)
            dve.tensor_copy(a1[:, :, :], ps_a[:, 0:DK * S].rearrange("p (k q) -> p k q", k=DK)).then_inc(a1_copied, 1)
            def split_t(t, c):
                dve.wait_ge(t_hi_done, CH * t + (c + 1))
                dve.tensor_tensor(t_lo[c % 2][:, :, :], t_raw[c % 2][:, :, :], t_hi[c % 2][:, :, :].bitcast(F32),
                                  ALU.subtract).then_inc(t_lo_done, 1)

            def split_n(t, c, b):
                dve.wait_ge(n_hi_done, 2 * CH * t + (2 * c + b + 1))
                dve.tensor_tensor(n_lo[b][:, :, :], n_raw[c % 2][:, :, b, :], n_hi[b][:, :, :].bitcast(F32),
                                  ALU.subtract).then_inc(n_lo_done, 1)

            def copy_w(t, c, b):
                dve.wait_ge(w_hi_done, 2 * CH * t + (2 * c + b + 1))
                dve.tensor_tensor(w_lo[c % 2][:, :, :, b, :].rearrange("p h k q -> p k h q"),
                                  ps_v[b][:, :].rearrange("p (k h q) -> p k h q", k=CT, h=2),
                                  w_hi[c % 2][:, :, :, b, :].bitcast(F32).rearrange("p h k q -> p k h q"),
                                  ALU.subtract).then_inc(w_lo_done, 1)

            def softmax(t):
                dve.wait_ge(other_done, 2 * t + 2)
                if not (isinstance(t, int) and t == 0):
                    dve.wait_ge(exp_done, t)
                dve.tensor_tensor(score[0:S, :], ps_s[0:S, 0:NWIN], other[0:S, :], ALU.add).then_inc(added, 1)
                dve.tensor_tensor(score[S:P, :], ps_s[S:P, NT + 1:NT + 1 + NWIN], other[S:P, :],
                                  ALU.add).then_inc(added, 1)
                dve.wait_ge(added, 2 * t + 2)
                dve.reduce_max(top[:, :], score[:, :], AX.X).then_inc(top_done, 1)
                dve.wait_ge(top_done, t + 1)
                dve.tensor_scalar(ntop[:, :], top[:, :], -SCALE, None, ALU.mult).then_inc(ntop_done, 1)

            def copy_pt(t):
                dve.wait_ge(exp_done, t + 1)
                dve.reciprocal(rden[:, bass.ds(t, 1)], den[:, :]).then_inc(rden_done, 1)
                dve.wait_ge(pt_hi_done, t + 1)
                dve.tensor_tensor(pt_lo[:, :, :, :, :].rearrange("p k b h q -> p (k b h q)"),
                                  ps_p[0:NROW, :],
                                  pt_hi[:, :, :, :, :].bitcast(F32).rearrange("p k b h q -> p (k b h q)"),
                                  ALU.subtract).then_inc(pt_lo_done, 1)

            def prepare(j):
                attention_weights.gain(dve, j)
                if j:
                    attention_weights.split_low(dve, j - 1)

            def step(t, ahead, last):
                first = isinstance(t, int) and t == 0
                for c in range(CH):
                    if c:
                        copy_w(t, c - 1, 1)
                    elif not first:
                        copy_w(t - 1, CH - 1, 1)
                    split_n(t, c, 1)
                    if last and c:
                        prepare(2 * c - 2)
                        prepare(2 * c - 1)
                    if c == CH - 1 and not first:
                        norms.dve_d(dve, t - 1)
                    if c == CH - 1 and not last:
                        softmax(t + 1)
                    if c < CH - 1:
                        if not last:
                            split_t(t + 1, c + 1)
                    elif ahead:
                        split_t(t + 2, 0)
                    if c < CH - 1:
                        split_n(t, c + 1, 0)
                        copy_w(t, c, 0)
                    else:
                        copy_w(t, c, 0)
                        if not last:
                            split_n(t + 1, 0, 0)
                            copy_pt(t + 1)
                    if c < CH - 1 and not first:
                        (norms.dve_a, norms.dve_b, norms.dve_c)[c](dve, t - 1)

            for n, j, side, i in fold_banks():
                hi, lo = fold_targets(side, i)
                dve.wait_ge(fold_hi, n + 1)
                dve.tensor_tensor(lo, fold_src(n, side), hi.bitcast(F32), ALU.subtract).then_inc(fold_lo, 1)
                if n in FIRST_SPLITS:
                    split_t(0, FIRST_SPLITS[n])
                if n == 17:
                    softmax(0)
                    split_t(1, 0)
            split_n(0, 0, 0)
            copy_pt(0)
            step(0, True, False)
            with dve.Fori(1, PAIRS - 2) as t:
                step(t, True, False)
            step(PAIRS - 2, False, False)
            step(PAIRS - 1, False, True)
            attention_weights.gain_vectors(dve, ps_s)
            copy_w(PAIRS - 1, CH - 1, 1)
            attention_weights.split_low(dve, 5)
            attention_weights.split_vectors_low(dve)

        @block.tensor
        def _(pe):
            pe.wait_ge(qa_landed, 48)
            for m in range(DK):
                for k in range(DK):
                    mm = pe.matmul(ps_a[:, m * S:(m + 1) * S], qa_wk[:, k, m * P:(m + 1) * P], qa_q[:, k, :],
                                   start=k == 0, stop=k == DK - 1)
            mm.then_inc(a1_ready, 1)
            pe.wait_ge(a1_copied, 1)
            def scores(t, c):
                pe.wait_ge(t_lo_done, CH * t + (c + 1))
                if c == 0 and not (isinstance(t, int) and t == 0):
                    pe.wait_ge(added, 2 * t)
                for k in range(CT):
                    ft = c * CT + k
                    prods = hi_lo_products(g_hi, g_lo, t_hi[c % 2], t_lo[c % 2])
                    for i, (a, b) in enumerate(prods):
                        mm = pe.matmul(ps_s[:, 0:2 * NT], a[:, ft, :, :], b[:, k, :],
                                       start=ft == 0 and i == 0, stop=ft == CH * CT - 1 and i == 2)
                mm.then_inc(scores_done, 1)

            def blocks(t, c, b):
                if b == 0 and c == 0:
                    pe.wait_ge(pt_lo_done, t + 1)
                pe.wait_ge(n_lo_done, 2 * CH * t + (2 * c + b + 1))
                if not (isinstance(t, int) and t == 0 and c == 0):
                    pe.wait_ge(pw_copied, 2 * CH * t + (2 * c + b - 1))
                i = 0
                for kt in range(2):
                    for x, y in hi_lo_products(pt_hi, pt_lo, n_hi[b], n_lo[b]):
                        mm = pe.matmul(ps_w[b][:, :], x[:, kt, b, :, :], y[:, kt, :], start=i == 0, stop=i == 5)
                        i += 1
                mm.then_inc(pw_done, 1)

            def turn(t, c, b):
                pe.wait_ge(pw_copied, 2 * CH * t + (2 * c + b + 1))
                if not (isinstance(t, int) and t == 0 and c == 0):
                    pe.wait_ge(w_lo_done, 2 * CH * t + (2 * c + b - 1))
                for ft in range(CT):
                    mm = pe.transpose(ps_v[b][:, ft * P:(ft + 1) * P], pw[b][:, ft * P:(ft + 1) * P], ident[:, :])
                mm.then_inc(turned, 1)

            def values(t, c, h):
                if h == 0:
                    pe.wait_ge(w_lo_done, 2 * CH * t + (2 * c + 2))
                    if c == 0 and not (isinstance(t, int) and t == 0):
                        pe.wait_ge(mem_copied, t)
                for k in range(CT):
                    ft = h * CH * CT + c * CT + k
                    for i, (x, y) in enumerate(hi_lo_products(w_hi[c % 2], w_lo[c % 2], v_hi, v_lo)):
                        mm = pe.matmul(ps_m[:, 0:D], x[:, h, k, :, :], y[:, ft, :],
                                       start=c == 0 and h == 0 and k == 0 and i == 0,
                                       stop=c == CH - 1 and h == 1 and k == CT - 1 and i == 2)
                if h:
                    mm.then_inc(mem_done, 1)

            def transpose_prob(t):
                pe.wait_ge(exp_done, t + 1)
                if not (isinstance(t, int) and t == 0):
                    pe.wait_ge(pt_lo_done, t)
                for kt in range(2):
                    for h in range(2):
                        mm = pe.transpose(ps_p[0:NROW, :].rearrange("p (k b h q) -> p k b h q", k=2, b=2, h=2)
                                          [:, kt, :, h, :],
                                          prob[:, 1 - h + kt * NROW:1 - h + (kt + 1) * NROW], ident[:, :])
                mm.then_inc(pt_ready, 1)

            def step(t, last):
                first = isinstance(t, int) and t == 0
                for c in range(CH):
                    if not last:
                        scores(t + 1, c)
                    before = (t, c - 1) if c else (t - 1, CH - 1)
                    skip = first and c == 0
                    blocks(t, c, 0)
                    if not skip:
                        values(*before, 0)
                    if c == 1 and not first:
                        norms.pe_sum(pe, t - 1, 0, ps_a)
                    blocks(t, c, 1)
                    turn(t, c, 0)
                    if c == 2 and not first:
                        norms.pe_sum(pe, t - 1, 1, ps_a)
                    if not skip:
                        values(*before, 1)
                    turn(t, c, 1)
                    if last and c == 0:
                        pe.wait_ge(added, 2 * PAIRS)
                        attention_weights.norm_bias(pe, ps_s)
                if not last:
                    transpose_prob(t + 1)

            for n, j, side, i in fold_banks():
                if side == "g":
                    pe.wait_ge(ws_landed[j % 2], 16 * (j // 2 + 1))
                if n >= 4:
                    pe.wait_ge(fold_lo, n - 3)
                tiles = range(8) if side == "g" else range(2 * i[1], 2 * i[1] + 2)
                rhs = a1 if side == "g" else qa_wv
                width = S if side == "g" else D
                for o, f in enumerate(tiles):
                    for k in range(DK):
                        mm = pe.matmul(ps_fold[n % 4][:, o * width:(o + 1) * width], ws[:, j % 2, k, f * P:(f + 1) * P],
                                       rhs[:, k, :], start=k == 0, stop=k == DK - 1)
                mm.then_inc(fold_ready, 1)
                for c in FIRST_SCORES.get(n, ()):
                    pe.wait_ge(fold_lo, 5 * (2 + c // 2) + 1)
                    scores(0, c)
            pe.wait_ge(fold_lo, 20)
            pe.wait_ge(zeroed, 10)
            transpose_prob(0)
            step(0, False)
            with pe.Fori(1, PAIRS - 1) as t:
                step(t, False)
            step(PAIRS - 1, True)
            for h in range(2):
                values(PAIRS - 1, CH - 1, h)


class AttentionWeights:
    BQ, G1, G3, G4, G2, LG, LB = range(7)
    LANDED = 8 * 16
    MADE = 7
    GAINED = 17
    NB = 5 * D + E

    def __init__(self, nc, outer, io, stage, halves, ident):
        def sb(name, shape, dt=F32):
            return outer.enter_context(nc.sbuf_tensor("a_" + name, shape, dt))

        def sem(name):
            return outer.enter_context(nc.semaphore("a_" + name))

        def inside(x):
            flat = x.rearrange("p s c n -> p (s c n)")
            return flat[:, 0:DK * 6 * D].rearrange("p (k d) -> p k d", k=DK)

        self.io, self.ident = io, ident
        self.raw = inside(stage[:, :, :, :])
        self.hi, self.lo = inside(halves[:, 0:2]), inside(halves[:, 2:4])
        self.eps = sb("ln_eps", [P, 1])
        self.mean_of = sb("mean_of", [P, P], F32R)
        self.mask = sb("mask", [P, P])
        self.ones = sb("ones", [P, P], F32R)
        self.wr_raw = sb("wr_raw", [P, DK, E])
        self.wr_hi = sb("wr_hi", [P, DK, E], F32R)
        self.wr_lo = sb("wr_lo", [P, DK, E], F32R)
        self.bias_row = sb("bias_row", [P, self.NB], F32R)
        self.cols = sb("cols_sb", [P, 7, DK])
        self.q_bias = sb("q_bias", [P, 3, DK])
        self.landed = sem("w_landed")
        self.bias_landed = sem("bias_landed")
        self.made = sem("made")
        self.gained = sem("gained")
        self.bo_ready = sem("bo_ready")
        self.high = sem("w_high")
        self.ready = sem("w_ready")

    def place_staged_bias(self, space):
        self.bias_raw = space[0:1, 0:self.NB]

    def load(self, sp):
        for i, w in enumerate(("k2", "v2", "k1", "v1", "q", "o")):
            sp.dma_start(self.raw[:, :, i * D:(i + 1) * D], self.io["W" + w].rearrange("(k p) h -> p k h", p=P))\
              .then_inc(self.landed, 16)
        sp.dma_start(self.wr_raw[:, :, :], self.io["router_w"].rearrange("(k p) e -> p k e", p=P))\
          .then_inc(self.landed, 16)
        sp.dma_start(self.cols[:, :, :], self.io["cols"]).then_inc(self.landed, 16)

    def load_bias(self, sp):
        sp.dma_start(self.bias_raw[:, :], self.io["bias"]).then_inc(self.bias_landed, 16)

    def make_constants(self, pool):
        n = [0]

        def then(ins):
            n[0] += 1
            ins.then_inc(self.made, 1)
            pool.wait_ge(self.made, n[0])

        then(pool.memset(self.eps[:, :], LN_EPS))
        then(pool.memset(self.mean_of[:, :].bitcast(F32), 1.0 / S))
        then(pool.memset(self.ones[:, :].bitcast(F32), 1.0))
        then(pool.memset(self.bias_row[:, :].bitcast(F32), 0.0))
        then(pool.memset(self.mask[:, :], 1.0 / S))
        view = self.mask[:, :].rearrange("p (j i) -> p j i", i=HD)
        then(pool.affine_select(out=view, in_=view, compare_op=ALU.is_ge, fill=0.0, base=0,
                                pattern=[[-HD, P // HD], [0, HD]], channel_multiplier=1))
        then(pool.affine_select(out=view, in_=view, compare_op=ALU.is_ge, fill=0.0, base=HD - 1,
                                pattern=[[HD, P // HD], [0, HD]], channel_multiplier=-1))
        assert n[0] == self.MADE

    def norm_bias(self, pe, bank):
        pe.wait_ge(self.landed, self.LANDED)
        for k in range(DK):
            mm = pe.matmul(bank[0:1, 0:D], self.cols[:, self.LB, k:k + 1], self.raw[:, k, 5 * D:6 * D],
                           start=k == 0, stop=k == DK - 1)
        mm.then_inc(self.bo_ready, 1)

    def gain(self, dve, j):
        if j == 0:
            dve.wait_ge(self.landed, self.LANDED)
        if j == 5:
            dve.wait_ge(self.bo_ready, 1)
        for k in range(DK):
            if j < 5:
                at = self.raw[:, k, j * D + k * P:j * D + (k + 1) * P]
                dve.tensor_tensor(at, at, self.ident[:, :], ALU.add).then_inc(self.gained, 1)
            else:
                at = self.raw[:, k, 5 * D:6 * D]
                dve.tensor_scalar(at, at, self.cols[:, self.LG, k:k + 1], None, ALU.mult).then_inc(self.gained, 1)

    def gain_vectors(self, dve, bank):
        cols, gained = self.cols, self.gained
        for k, g in enumerate((self.G1, self.G3, self.G4)):
            dve.tensor_tensor(self.q_bias[:, k, :], cols[:, g, :], cols[:, self.BQ, :], ALU.mult).then_inc(gained, 1)
        dve.wait_ge(gained, 15)
        dve.tensor_tensor(self.q_bias[:, 2, :], self.q_bias[:, 2, :], cols[:, self.G2, :], ALU.add)\
           .then_inc(gained, 1)
        dve.wait_ge(self.bias_landed, 16)
        bo = self.bias_raw[0:1, 4 * D:5 * D]
        dve.tensor_tensor(bo, bo, bank[0:1, 0:D], ALU.add).then_inc(gained, 1)

    def split_high(self, act, j):
        act.wait_ge(self.gained, 2 * (j + 1))
        at = slice(j * D, (j + 1) * D)
        act.activation(self.hi[:, :, at], self.raw[:, :, at], ACT.Copy).then_inc(self.high, 1)

    def split_low(self, dve, j):
        dve.wait_ge(self.high, j + 1)
        at = slice(j * D, (j + 1) * D)
        dve.tensor_tensor(self.lo[:, :, at], self.raw[:, :, at], self.hi[:, :, at].bitcast(F32), ALU.subtract)\
           .then_inc(self.ready, 1)

    def split_vectors_high(self, act):
        act.wait_ge(self.made, self.MADE)
        act.wait_ge(self.gained, self.GAINED)
        act.activation(self.wr_hi[:, :, :], self.wr_raw[:, :, :], ACT.Copy).then_inc(self.high, 1)
        act.activation(self.bias_row[0:1, :], self.bias_raw[:, :], ACT.Copy).then_inc(self.high, 1)

    def split_vectors_low(self, dve):
        for i, (lo, raw, hi) in enumerate(((self.wr_lo[:, :, :], self.wr_raw[:, :, :], self.wr_hi[:, :, :]),
                                           (self.bias_row[32:33, :], self.bias_raw[:, :], self.bias_row[0:1, :]))):
            dve.wait_ge(self.high, 7 + i)
            dve.tensor_tensor(lo, raw, hi.bitcast(F32), ALU.subtract).then_inc(self.ready, 1)


def latent_attention(nc, io, rows, mean, rstd, ident, weights, norms, xt_hi, xt_lo, logits, experts_weights):
    ctx = ExitStack()

    def sb(name, shape, dt=F32):
        return ctx.enter_context(nc.sbuf_tensor("a_" + name, shape, dt))

    def two(name, shape, dt=F32):
        return [sb(f"{name}{i}", shape, dt) for i in range(2)]

    def pb(name):
        return ctx.enter_context(nc.psum_tensor("a_" + name, [P, 512], F32))

    def sem(name):
        return ctx.enter_context(nc.semaphore("a_" + name))

    with ctx:
        w_hi, w_lo, wr_hi, wr_lo = weights.hi, weights.lo, weights.wr_hi, weights.wr_lo
        bias_row, cols, q_bias, ones = weights.bias_row, weights.cols, weights.q_bias, weights.ones
        eps, mean_of, mask = weights.eps, weights.mean_of, weights.mask
        landed, LANDED = weights.landed, weights.LANDED
        stat = sb("stat", [P, 6])
        mv = sb("mv", [P, 2])
        std = sb("std", [P, 1])
        inv = sb("inv", [P, 1])
        fstat = sb("fstat", [P, 6])
        fmv = sb("fmv", [P, 2])
        fstd = sb("fstd", [P, 1])
        finv = sb("finv", [P, 1])
        xn = sb("xn", [P, D])
        xa_hi = sb("xa_hi", [P, DK, P], F32R)
        xa_lo = sb("xa_lo", [P, DK, P], F32R)
        kv_hi = two("kv_hi", [P, 4, D], F32R)
        kv_lo = two("kv_lo", [P, 4, D], F32R)
        qv = two("qv", [P, 3, DK, P])
        sq = sb("sq", [P, 2, DK * P])
        mx = sb("mx", [P, 2, 3, DK * P])
        on = sb("on", [P, D])
        ot_hi = sb("ot_hi", [P, DK, P], F32R)
        ot_lo = sb("ot_lo", [P, DK, P], F32R)
        xf = sb("xf", [P, D])
        xr_hi = sb("xr_hi", [P, DK, P], F32R)
        xr_lo = sb("xr_lo", [P, DK, P], F32R)

        ps_x = pb("ps_x")
        ps_kv = [pb("ps_kv0"), pb("ps_kv1")]
        ps_qw = pb("ps_qw")
        ps_sq = pb("ps_sq")
        ps_vm = pb("ps_vm")
        ps_o = pb("ps_o")
        ps_d = pb("ps_d")

        s = {n: sem(n) for n in (
            "xn xt xa_h xa_l kv0 kv1 kv_h kv_l q_done qc sq sm s12 av o st mv sd iv on ot ot_h "
            "ot_l wo x2 fst fmv fsd fiv xf xft xr_h xr_l xs lg lgc").split()}
        block = ctx.enter_context(nc.Block())
        NTILE = ROWS // P

        def need(eng, name, t, back=0, per=1, i=None):
            if isinstance(t, int):
                if t < back:
                    return
                t = min(t - back, NTILE - 1) + back
            eng.wait_ge(s[name], per * t + (per if i is None else i + 1) - per * back)

        def ticks(eng, stages, after):
            def tick(n, slot, among):
                for lag, f in stages:
                    if among(lag):
                        f(n - lag, (slot + lag) % 2)

            for n in range(LOOPED):
                tick(n, n % 2, lambda lag: n >= lag)
                after(n, n % 2)
            with eng.Fori(LOOPED // 2, NTILE // 2) as i:
                for j in range(2):
                    tick(2 * i + j, j, lambda lag: True)
            for n in range(NTILE, NTILE + DEEPEST):
                tick(n, n % 2, lambda lag: n - lag < NTILE)

        PIECES_AT = {0: (0,), 1: (1,), NTILE - 4: (2,), NTILE - 3: (3,), NTILE - 2: (4, 5), NTILE - 1: (6, 7)}

        def split_pieces(eng, split):
            def f(t, p):
                for piece in PIECES_AT.get(t, ()) if isinstance(t, int) else ():
                    split(eng, 0, 0, piece)
            return f

        DEEPEST = 4
        LOOPED = 6

        def row(t):
            return rows[:, bass.ds(t, 1), :].rearrange("p o d -> p (o d)")

        @block.sync
        def _(sp):
            experts_weights.load(sp, 0, wait=False)

        @block.gpsimd
        def _(pool):
            def keep(t, p):
                need(pool, "xr_l", t)
                for src, dst in ((xr_hi, xt_hi), (xr_lo, xt_lo)):
                    pool.tensor_copy(dst[:, :, bass.ds(t * P, P)], src[:, :, :].bitcast(F32)).then_inc(s["xs"], 1)

            with pool.Fori(0, NTILE) as t:
                keep(t, 0)

        @block.scalar
        def _(act):
            def high(dst, src, name):
                act.activation(dst, src, ACT.Copy).then_inc(s[name], 1)

            def routed(t, p):
                need(act, "xft", t)
                need(act, "xt", t, back=-3)
                need(act, "lg", t, back=1)
                need(act, "xs", t, back=1, per=2)
                high(xr_hi[:, :, :], ps_x[:, D:].rearrange("p (k r) -> p k r", k=DK), "xr_h")

            def transposed(t, p):
                need(act, "xt", t)
                need(act, "q_done", t, back=1)
                high(xa_hi[:, :, :], ps_x[:, 0:D].rearrange("p (k r) -> p k r", k=DK), "xa_h")

            def norm_mixed(t, p):
                need(act, "mv", t)
                need(act, "iv", t, back=1)
                act.activation(std[:, :], mv[:, 1:2], ACT.Sqrt, bias=eps[:, :]).then_inc(s["sd"], 1)

            def projected(i):
                def f(t, p):
                    need(act, f"kv{i}", t)
                    need(act, "sq", t, back=2, per=2)
                    high(kv_hi[p][:, 2 * i:2 * i + 2, :], ps_kv[i][:, :].rearrange("p (j d) -> p j d", d=D), "kv_h")
                return f

            def turned(t, p):
                need(act, "ot", t)
                need(act, "wo", t, back=1)
                high(ot_hi[:, :, :], ps_d[:, 0:D].rearrange("p (k r) -> p k r", k=DK), "ot_h")

            def queries(ks):
                def f(t, p):
                    if 0 in ks:
                        need(act, "q_done", t)
                        need(act, "o", t, back=2)
                        need(act, "x2", t, back=2)
                    for k in ks:
                        g = (weights.G1, weights.G3, weights.G4)[k]
                        for ct in range(DK):
                            act.activation(qv[p][:, k, ct, :], ps_qw[:, ct * P:(ct + 1) * P], ACT.Identity,
                                           scale=cols[:, g, ct:ct + 1], bias=q_bias[:, k, ct:ct + 1])\
                               .then_inc(s["qc"], 1)
                return f

            def norm_out(t, p):
                need(act, "fmv", t)
                need(act, "fiv", t, back=1)
                act.activation(fstd[:, :], fmv[:, 1:2], ACT.Sqrt, bias=eps[:, :]).then_inc(s["fsd"], 1)

            def last_norm(t, p):
                if isinstance(t, int) and t < LOOPED:
                    last = PAIRS - 1
                    if t == 0:
                        norms.act_a(act, last, ps_d)
                    if t == 1:
                        norms.act_b(act, last, ps_d)
                    if t == 2:
                        norms.act_c(act, last)
                    if t == 4:
                        norms.act_e(act, last)

            def last_norm_end(t, p):
                if t == 2:
                    norms.act_d(act, PAIRS - 1, ps_d)

            ticks(act, [(4, routed), (1, transposed), (3, norm_mixed), (1, projected(0)), (3, turned),
                        (4, split_pieces(act, experts_weights.split_high)), (0, last_norm), (1, queries((0,))),
                        (3, norm_out), (1, projected(1)), (1, queries((1, 2)))], last_norm_end)

        @block.vector
        def _(dve):
            def wide(x, shape):
                return x.to_broadcast(shape)

            def low(dst, src, hi, name):
                dve.tensor_tensor(dst, src, hi.bitcast(F32), ALU.subtract).then_inc(s[name], 1)

            def stats(src, st, out, done_st, done, t):
                dve.wait_ge(landed, LANDED)
                dve.bn_stats(st[:, :], src).then_inc(s[done_st], 1)
                dve.wait_ge(landed, LANDED)
                need(dve, done_st, t)
                dve.bn_aggr(out[:, :], st[:, :]).then_inc(s[done], 1)

            def stats_mixed(t, p):
                need(dve, "o", t)
                stats(ps_o[:, 0:D], stat, mv, "st", "mv", t)

            def routed(t, p):
                need(dve, "xr_h", t)
                need(dve, "xa_h", t, back=-3)
                low(xr_lo[:, :, :], ps_x[:, D:].rearrange("p (k r) -> p k r", k=DK), xr_hi[:, :, :], "xr_l")

            def transposed(t, p):
                need(dve, "xa_h", t)
                low(xa_lo[:, :, :], ps_x[:, 0:D].rearrange("p (k r) -> p k r", k=DK), xa_hi[:, :, :], "xa_l")

            def norm_mixed(t, p):
                need(dve, "sd", t)
                dve.reciprocal(inv[:, :], std[:, :]).then_inc(s["iv"], 1)
                need(dve, "iv", t)
                need(dve, "ot", t, back=1)
                dve.tensor_scalar(on[:, :], ps_o[:, 0:D], mv[:, 0:1], inv[:, :], ALU.subtract, ALU.mult)\
                   .then_inc(s["on"], 1)

            def squares(b):
                def f(t, p):
                    need(dve, "sq", t, per=2, i=b)
                    need(dve, "o", t, back=1)
                    dve.tensor_tensor(sq[:, :, :].rearrange("p w (c d) -> p (w c) d", d=P),
                                      ps_sq[:, :].rearrange("p (w d) -> p w d", d=P),
                                      wide(mask[:, :].rearrange("p (o d) -> p o d", o=1), [P, 4, P]), ALU.mult)\
                       .then_inc(s["sm"], 1)
                    need(dve, "sm", t, per=2, i=b)
                    dve.tensor_tensor(mx[:, b, 2, :], sq[:, 0, :], sq[:, 1, :], ALU.mult).then_inc(s["s12"], 1)
                    dve.tensor_tensor(mx[:, b, 0:2, :], ps_vm[:, :].rearrange("p (w d) -> p w d", w=2), sq[:, :, :],
                                      ALU.mult).then_inc(s["av"], 1)
                return f

            def projected(i):
                def f(t, p):
                    need(dve, "kv_h", t, per=2, i=i)
                    low(kv_lo[p][:, 2 * i:2 * i + 2, :], ps_kv[i][:, :].rearrange("p (j d) -> p j d", d=D),
                        kv_hi[p][:, 2 * i:2 * i + 2, :], "kv_l")
                return f

            def logit(t, p):
                need(dve, "lg", t)
                need(dve, "ot_h", t, back=-1)
                dve.tensor_copy(logits[:, bass.ds(t, 1), :].rearrange("p o e -> p (o e)"), ps_d[:, D:D + E])\
                   .then_inc(s["lgc"], 1)

            def turned(t, p):
                need(dve, "ot_h", t)
                low(ot_lo[:, :, :], ps_d[:, 0:D].rearrange("p (k r) -> p k r", k=DK), ot_hi[:, :, :], "ot_l")

            def norm(t, p):
                need(dve, "xt", t, back=1)
                dve.tensor_scalar(xn[:, :], row(t), mean[:, bass.ds(t, 1)], rstd[:, bass.ds(t, 1)], ALU.subtract,
                                  ALU.mult).then_inc(s["xn"], 1)

            def norm_out(t, p):
                need(dve, "wo", t)
                need(dve, "q_done", t, back=-2)
                dve.tensor_tensor(row(t), row(t), ps_qw[:, D:], ALU.add).then_inc(s["x2"], 1)
                dve.wait_ge(landed, LANDED)
                need(dve, "x2", t)
                stats(row(t), fstat, fmv, "fst", "fmv", t)
                need(dve, "fsd", t)
                dve.reciprocal(finv[:, :], fstd[:, :]).then_inc(s["fiv"], 1)
                need(dve, "fiv", t)
                need(dve, "xft", t, back=1)
                dve.tensor_scalar(xf[:, :], row(t), fmv[:, 0:1], finv[:, :], ALU.subtract, ALU.mult)\
                   .then_inc(s["xf"], 1)

            def last_norm(t, p):
                if isinstance(t, int) and t < LOOPED:
                    last = PAIRS - 1
                    if t == 0:
                        norms.dve_a(dve, last)
                    if t == 1:
                        norms.dve_b(dve, last)
                    if t == 3:
                        norms.dve_c(dve, last)
                    if t == 4:
                        norms.dve_d(dve, last)
                        norms.need(dve, "mu", last)
                        norms.need(dve, "rs", last)

            ticks(dve, [(3, stats_mixed), (4, routed), (1, transposed), (3, norm_mixed), (2, squares(0)),
                        (1, projected(0)), (4, logit), (3, turned),
                        (4, split_pieces(dve, experts_weights.split_low)), (2, squares(1)), (0, norm),
                        (0, last_norm), (3, norm_out), (1, projected(1))], lambda t, p: None)

        @block.tensor
        def _(pe):
            pe.wait_ge(weights.ready, 8)

            def turn(bank, src, name):
                for k in range(DK):
                    mm = pe.transpose(bank[:, k * P:(k + 1) * P], src[:, k * P:(k + 1) * P], ident[:, :])
                mm.then_inc(s[name], 1)

            def product(out, lhs, rhs, bias=None):
                i, n = 0, 3 * DK + (bias is not None)
                for k in range(DK):
                    for a, b in hi_lo_products(*lhs, *rhs):
                        mm = pe.matmul(out, a(k), b(k), start=i == 0, stop=i == n - 1)
                        i += 1
                if bias is not None:
                    mm = pe.matmul(out, ones[:, :], bias, start=False, stop=True)
                return mm

            def tiles(x):
                return lambda k: x[:, k, :]

            xa = (tiles(xa_hi), tiles(xa_lo))

            def columns(at):
                return [lambda k, w=w: w[:, k, at] for w in (w_hi, w_lo)]

            def routed(t, p):
                need(pe, "xf", t)
                need(pe, "xr_l", t, back=1)
                need(pe, "xa_l", t, back=-2)
                turn(ps_x[:, D:], xf, "xft")

            def transposed(t, p):
                need(pe, "xn", t)
                need(pe, "xr_l", t, back=4)
                need(pe, "xa_l", t, back=1)
                turn(ps_x[:, 0:D], xn, "xt")

            def squares(b):
                def f(t, p):
                    need(pe, "kv_l", t, per=2)
                    if b:
                        need(pe, "av", t, per=2, i=0)
                    else:
                        need(pe, "av", t, back=1, per=2)
                    r = slice(b * S, (b + 1) * S)
                    for j in range(2):
                        for ct in range(DK):
                            c = slice(ct * P, (ct + 1) * P)
                            o = (2 * j + ct) * P
                            for i, (x, y) in enumerate(hi_lo_products(kv_hi[p], kv_lo[p], kv_hi[p], kv_lo[p])):
                                mm = pe.matmul(ps_sq[:, o:o + P], x[r, 2 - 2 * j, c], y[r, 3 - 2 * j, c],
                                               start=i == 0, stop=i == 2)
                    for i, x in enumerate((kv_hi[p], kv_lo[p])):
                        mm = pe.matmul(ps_vm[:, :], mean_of[r, :],
                                       x[r, :, :].rearrange("r (w o) d -> r w o d", o=2)[:, :, 1, :],
                                       start=i == 0, stop=i == 1)
                    mm.then_inc(s["sq"], 1)
                return f

            def projected(i):
                def f(t, p):
                    need(pe, "xa_l", t)
                    need(pe, "kv_l", t, back=1, per=2, i=i)
                    at = slice(2 * i * D, 2 * (i + 1) * D)
                    product(ps_kv[i][:, :], xa, columns(at), bias_row[:, at]).then_inc(s[f"kv{i}"], 1)
                return f

            def logit(t, p):
                need(pe, "xr_l", t)
                need(pe, "lgc", t, back=1)
                need(pe, "ot_l", t)
                product(ps_d[:, D:D + E], (tiles(xr_hi), tiles(xr_lo)), (tiles(wr_hi), tiles(wr_lo)),
                        bias_row[:, 5 * D:]).then_inc(s["lg"], 1)

            def turned(t, p):
                need(pe, "on", t)
                if isinstance(t, int) and t == 0:
                    norms.need(pe, "sd2", PAIRS - 1)
                need(pe, "ot_l", t, back=1)
                need(pe, "lgc", t, back=2)
                turn(ps_d[:, 0:D], on, "ot")

            def output(t, p):
                need(pe, "ot_l", t)
                need(pe, "x2", t, back=1)
                need(pe, "qc", t, back=-1, per=6)
                product(ps_qw[:, D:], (tiles(ot_hi), tiles(ot_lo)), columns(slice(5 * D, 6 * D)),
                        bias_row[:, 4 * D:5 * D]).then_inc(s["wo"], 1)

            def queries(t, p):
                need(pe, "qc", t, back=1, per=6)
                need(pe, "x2", t, back=3)
                for ct in range(DK):
                    mm = product(ps_qw[:, ct * P:(ct + 1) * P], columns(slice(4 * D + ct * P, 4 * D + (ct + 1) * P)),
                                 xa)
                mm.then_inc(s["q_done"], 1)

            def mix(t, p):
                need(pe, "av", t, per=2)
                need(pe, "qc", t, per=6)
                need(pe, "on", t, back=1)
                for b in range(2):
                    r = slice(b * S, (b + 1) * S)
                    for ct in range(DK):
                        c = slice(ct * P, (ct + 1) * P)
                        for k in range(3):
                            mm = pe.matmul(ps_o[r, c], qv[p][:, k, ct, r], mx[:, b, k, c], start=k == 0,
                                           stop=k == 2)
                mm.then_inc(s["o"], 1)

            def last_norm_end(t, p):
                if t == 0:
                    norms.pe_sum(pe, PAIRS - 1, 0, ps_d)

            def last_norm(t, p):
                if isinstance(t, int) and t == 2:
                    norms.pe_sum(pe, PAIRS - 1, 1, ps_d)

            ticks(pe, [(4, routed), (1, transposed), (2, squares(0)), (1, projected(0)), (4, logit), (3, turned),
                       (2, squares(1)), (3, output), (1, queries), (1, projected(1)), (0, last_norm),
                       (2, mix)], last_norm_end)


I = 512
TOP = 4
ALPHA, LIMIT = 1.702, 7.0
TC = 512
NQ = ROWS // TC
NI = I // P


class ExpertWeights:
    PIECES = 2 * NI

    def __init__(self, nc, outer, io):
        def sb(name, shape, dt=F32):
            return outer.enter_context(nc.sbuf_tensor("e_" + name, shape, dt))

        def sem(name):
            return outer.enter_context(nc.semaphore("e_" + name))

        self.io = io
        self.gu = sb("gu_raw", [P, DK, 2 * I])
        self.dn = sb("dn_raw", [P, NI, D])
        self.gu_hi, self.gu_lo = [sb("gu_hi0", [P, DK, 2 * I], F32R)], [sb("gu_lo0", [P, DK, 2 * I], F32R)]
        self.dn_hi, self.dn_lo = [sb("dn_hi0", [P, NI, D], F32R)], [sb("dn_lo0", [P, NI, D], F32R)]
        self.gu_landed = sem("gu_landed")
        self.dn_landed = sem("dn_landed")
        self.high = sem("wh")
        self.low = sem("wl")

    def load(self, sp, e, wait=True):
        if wait:
            sp.wait_ge(self.low, self.PIECES * e + (NI - self.PIECES))
        sp.dma_start(self.gu[:, :, :], self.io["gu"][bass.ds(e, 1)].rearrange("o (k p) j -> p (o k) j", p=P))\
          .then_inc(self.gu_landed, 16)
        if wait:
            sp.wait_ge(self.low, self.PIECES * e)
        sp.dma_start(self.dn[:, :, :], self.io["dn"][bass.ds(e, 1)].rearrange("o (k p) d -> p (o k) d", p=P))\
          .then_inc(self.dn_landed, 16)

    def piece(self, gu, dn, piece):
        w = 2 * I // NI
        return gu[:, :, piece * w:(piece + 1) * w] if piece < NI else dn[:, piece - NI, :]

    def split_high(self, act, e, p, piece):
        if piece == 0:
            act.wait_ge(self.gu_landed, 16 * e + 16)
        if piece == NI:
            act.wait_ge(self.dn_landed, 16 * e + 16)
        act.activation(self.piece(self.gu_hi[p], self.dn_hi[p], piece), self.piece(self.gu, self.dn, piece), ACT.Copy)\
           .then_inc(self.high, 1)

    def split_low(self, dve, e, p, piece):
        dve.wait_ge(self.high, self.PIECES * e + (piece + 1))
        dve.tensor_tensor(self.piece(self.gu_lo[p], self.dn_lo[p], piece), self.piece(self.gu, self.dn, piece),
                          self.piece(self.gu_hi[p], self.dn_hi[p], piece).bitcast(F32), ALU.subtract)\
           .then_inc(self.low, 1)


def experts(nc, io, rows, xt_hi, xt_lo, logits, ident, weights, stage, out):
    ctx = ExitStack()

    def sb(name, shape, dt=F32):
        return ctx.enter_context(nc.sbuf_tensor("e_" + name, shape, dt))

    def two(name, shape, dt=F32):
        return [sb(f"{name}{i}", shape, dt) for i in range(2)]

    def pb(name):
        return ctx.enter_context(nc.psum_tensor("e_" + name, [P, 512], F32))

    def sem(name):
        return ctx.enter_context(nc.semaphore("e_" + name))

    NTILE = ROWS // P
    TQ = TC // P
    SHIFTED = 2

    with ctx:
        weights.gu_hi.append(sb("gu_hi1", [P, DK, 2 * I], F32R))
        weights.gu_lo.append(sb("gu_lo1", [P, DK, 2 * I], F32R))
        weights.dn_hi.append(sb("dn_hi1", [P, NI, D], F32R))
        weights.dn_lo.append(sb("dn_lo1", [P, NI, D], F32R))
        gu_hi, gu_lo, dn_hi, dn_lo = weights.gu_hi, weights.gu_lo, weights.dn_hi, weights.dn_lo
        PIECES = weights.PIECES
        gub = two("gub", [P, 2 * NI])
        dnb = sb("dnb", [E, D])
        free = stage[:, :, :, :].rearrange("p s c n -> p (s c n)")
        gate, up, silu = [[free[:, (2 * j + i) * TC:(2 * j + i + 1) * TC] for i in range(2)] for j in range(3)]
        prod = two("prod", [P, TC])
        a_hi = two("a_hi", [P, NI, TC], F32R)
        a_lo = two("a_lo", [P, NI, TC], F32R)
        beats = sb("beats", [P, NTILE, E])
        rank = sb("rank", [P, NTILE, E])
        best = sb("best", [P, NTILE])
        comb = sb("comb", [P, NTILE, E])
        total = sb("total", [P, NTILE])
        comb_t = sb("comb_t", [E, TC])

        ps_g = [pb("ps_g0"), pb("ps_g1")]
        ps_u = [pb("ps_u0"), pb("ps_u1")]
        ps_d = [pb("ps_d0"), pb("ps_d1")]
        ps_c = pb("ps_c")
        ps_b = pb("ps_b")

        LAST_DOWN = ps_d + ps_g

        gub_landed = [sem("gub_landed0"), sem("gub_landed1")]
        dnb_landed = sem("dnb_landed")
        stored = sem("stored")
        ranked = sem("ranked")
        exp_done = sem("exp_done")
        combined = sem("combined")
        ct_done = sem("ct_done")
        ct_copied = sem("ct_copied")
        bias_done = sem("bias_done")
        biased = sem("biased")
        s = {n: sem(n) for n in (
            "gu_g gu_u "
            "gate up clip silu h a_hi a_lo "
            "down y").split()}
        block = ctx.enter_context(nc.Block())
        WS = NQ * NI

        def need(eng, name, t, back=0, per=1, i=None):
            if not (isinstance(t, int) and t < back):
                eng.wait_ge(s[name], per * t + (per if i is None else i + 1) - per * back)

        def schedule(eng, chunk, split=None):
            def body(e, p):
                ahead = split and (lambda piece: split(e, p, piece))
                chunk(e - 1, 1 - p, 2, ahead)
                chunk(e - 1, 1 - p, 3, ahead)
                chunk(e, p, 0)
                chunk(e, p, 1)

            chunk(0, 0, 0)
            chunk(0, 0, 1)
            body(1, 1)
            with eng.Fori(1, E // 2) as i:
                for j in range(2):
                    body(2 * i + j, j)
            chunk(E - 1, 1, 2)
            chunk(E - 1, 1, 3)

        def bias_group(e, q):
            u = NQ * e + q - 2 if isinstance(e, int) else None
            return u if u is not None and 0 <= u < NQ else None

        def bias_there(eng, e, p):
            eng.wait_ge(gub_landed[p], 8 * e + (16 - 8 * p))

        @block.sync
        def _(sp):
            def load(e, p):
                if not (isinstance(e, int) and e == 0):
                    weights.load(sp, e)
                need(sp, "gate", e, back=2, per=WS)
                need(sp, "up", e, back=2, per=WS)
                sp.dma_start(gub[p][:, :], io["gub"][bass.ds(e, 1)].rearrange("o p j -> p (o j)"))\
                  .then_inc(gub_landed[p], 16)

            sp.dma_start(dnb[:, :], io["dnb"]).then_inc(dnb_landed, 16)
            load(0, 0)
            load(1, 1)
            with sp.Fori(1, E // 2) as i:
                for j in range(2):
                    load(2 * i + j, j)
            o = out.rearrange("(t b) s d -> (b s) t d", b=2)
            stores = [(TQ * q, TQ * (q + 1)) for q in range(NQ - 1)] + [(t, t + 1) for t in range(NTILE - TQ, NTILE)]
            for first, end in stores:
                sp.wait_ge(s["y"], NTILE * (E - 1) + end)
                sp.dma_start(o[:, first:end, :], rows[:, first:end, :]).then_inc(stored, 16)
            sp.wait_ge(stored, 16 * len(stores))

        @block.scalar
        def _(act):
            def split(e, p, piece):
                if piece == 0:
                    need(act, "gu_u", e, back=2, per=WS)
                if piece == NI:
                    need(act, "down", e, back=2, per=2 * NQ)
                weights.split_high(act, e, p, piece)

            def high(e, q, it):
                need(act, "h", WS * e + NI * q + it)
                if it == 0:
                    need(act, "down", NQ * e + q, back=2, per=2)
                act.activation(a_hi[q % 2][:, it, :], prod[it % 2][:, :], ACT.Copy, scale=1 / ALPHA)\
                   .then_inc(s["a_hi"], 1)

            def chunk(e, p, q, ahead=None):
                start = isinstance(e, int) and e == 0 and q == 0
                g = bias_group(e, q)
                if q == 0:
                    bias_there(act, e, p)
                for it in range(NI):
                    w, v = WS * e + (NI * q + it), it % 2
                    need(act, "gu_u", w)
                    need(act, "h", w, back=2)
                    act.activation(up[v][:, :], ps_u[v][:, :], ACT.Identity, bias=gub[p][:, NI + it:NI + it + 1])\
                       .then_inc(s["up"], 1)
                    need(act, "gate", w)
                    act.activation(silu[v][:, :], gate[v][:, :], ACT.Silu, scale=ALPHA).then_inc(s["silu"], 1)
                    if it:
                        high(e, q, it - 1)
                    elif not start:
                        high(e, q - 1, NI - 1)
                    if ahead:
                        ahead(NI * (q - 2) + it)
                    if start and it == 1:
                        act.wait_ge(ranked, SHIFTED)
                        act.activation(comb[:, :, :], comb[:, :, :], ACT.Exp).then_inc(exp_done, 1)
                    if g is not None and it == 1:
                        act.wait_ge(ct_done, g + 1)
                        if g:
                            act.wait_ge(bias_done, g)
                        act.activation(comb_t[:, :], ps_c[0:E, :], ACT.Copy).then_inc(ct_copied, 1)

            schedule(act, chunk, split)
            high(E - 1, NQ - 1, NI - 1)

        @block.vector
        def _(dve):
            def over(x, shape=(P, NTILE, E)):
                return x.rearrange("p (t o) -> p t o", o=1).to_broadcast(list(shape))

            routing = [0]

            def step(ins):
                routing[0] += 1
                ins.then_inc(ranked, 1)
                dve.wait_ge(ranked, routing[0])

            def route_start():
                step(dve.tensor_reduce(best[:, :], logits[:, :, :], AX.X, ALU.max))
                step(dve.tensor_tensor(comb[:, :, :], logits[:, :, :], over(best[:, :]), ALU.subtract))
                assert routing[0] == SHIFTED
                step(dve.memset(rank[:, :, :], 0.0))

            def route_rank(j):
                for op, at in ((ALU.is_gt, slice(0, j)), (ALU.is_ge, slice(j + 1, E))):
                    k = at.stop - at.start
                    if k:
                        step(dve.tensor_tensor(beats[:, :, at], over(logits[:, :, j], (P, NTILE, k)),
                                               logits[:, :, at], op))
                        step(dve.tensor_tensor(rank[:, :, at], rank[:, :, at], beats[:, :, at], ALU.add))

            def route_end():
                step(dve.tensor_scalar(rank[:, :, :], rank[:, :, :], float(TOP), None, ALU.is_lt))
                dve.wait_ge(exp_done, 1)
                step(dve.tensor_tensor(comb[:, :, :], comb[:, :, :], rank[:, :, :], ALU.mult))
                step(dve.tensor_reduce(total[:, :], comb[:, :, :], AX.X, ALU.add))
                step(dve.reciprocal(total[:, :], total[:, :]))
                dve.tensor_tensor(comb[:, :, :], comb[:, :, :], over(total[:, :]), ALU.mult).then_inc(combined, 1)
                dve.wait_ge(combined, 1)

            def route(step):
                if step == 0:
                    route_start()
                if 1 <= step <= E // 2 + 1:
                    for j in (2 * step - 2, 2 * step - 1):
                        if j < E:
                            route_rank(j)
                if step == E // 2 + 1:
                    route_end()

            def low(e, q, it):
                need(dve, "a_hi", WS * e + (NI * q + it))
                dve.scalar_tensor_tensor(a_lo[q % 2][:, it, :], prod[it % 2][:, :], 1 / ALPHA,
                                         a_hi[q % 2][:, it, :].bitcast(F32), ALU.mult, ALU.subtract)\
                   .then_inc(s["a_lo"], 1)

            def activate(e, q, it):
                w, v = WS * e + (NI * q + it), it % 2
                need(dve, "up", w)
                dve.tensor_scalar(up[v][:, :], up[v][:, :], LIMIT, -LIMIT, ALU.min, ALU.max).then_inc(s["clip"], 1)
                need(dve, "clip", w)
                need(dve, "a_lo", w, back=2)
                need(dve, "silu", w)
                dve.scalar_tensor_tensor(prod[v][:, :], up[v][:, :], 1.0, silu[v][:, :], ALU.add, ALU.mult)\
                   .then_inc(s["h"], 1)

            def add(e, q, d):
                need(dve, "down", NQ * e + q, per=2, i=d)
                for i in range(2):
                    t = TQ * q + 2 * d + i
                    dve.scalar_tensor_tensor(rows[:, t, :], ps_d[d][:, i * D:(i + 1) * D], comb[:, t, bass.ds(e, 1)],
                                             rows[:, t, :], ALU.mult, ALU.add).then_inc(s["y"], 1)

            def chunk(e, p, q, ahead=None):
                start = isinstance(e, int) and e == 0 and q == 0
                second = isinstance(e, int) and e == 0 and q == 1
                g = bias_group(e, q)
                u = NQ * e + q
                if q == 0:
                    bias_there(dve, e, p)
                before = (e, q - 1) if q else (e - 1, NQ - 1)
                twice = (e, q - 2) if q >= 2 else (e - 1, q + 2)
                for it in range(NI):
                    w, v = WS * e + (NI * q + it), it % 2
                    if it >= 2:
                        low(e, q, it - 2)
                    elif not start:
                        low(*before, NI - 2 + it)
                    need(dve, "gu_g", w)
                    need(dve, "silu", w, back=2)
                    dve.tensor_scalar(gate[v][:, :], ps_g[v][:, :], gub[p][:, it:it + 1], LIMIT, ALU.add, ALU.min)\
                       .then_inc(s["gate"], 1)
                    if it:
                        activate(e, q, it - 1)
                    elif not start:
                        activate(*before, NI - 1)
                    if it == 0 and not start and not second:
                        add(*twice, 1)
                    if start or second:
                        route(NI * q + it)
                    if it == NI - 1 and not start:
                        add(*before, 0)
                        if g is not None:
                            add_bias(g, u)
                    if ahead:
                        ahead(NI * (q - 2) + it)
            def add_bias(g, u):
                dve.wait_ge(bias_done, g + 1)
                dve.wait_ge(s["y"], TQ * (u - 1) + 2)
                for h, bank in enumerate((ps_b, ps_c)):
                    t = 4 * g + 2 * h
                    dve.tensor_tensor(rows[:, t:t + 2, :], rows[:, t:t + 2, :],
                                      bank[:, :].rearrange("p (t d) -> p t d", d=D), ALU.add).then_inc(biased, 1)
                dve.wait_ge(biased, 2 * (g + 1))

            schedule(dve, chunk, lambda e, p, piece: weights.split_low(dve, e, p, piece))
            low(E - 1, NQ - 1, NI - 2)
            activate(E - 1, NQ - 1, NI - 1)
            add(E - 1, NQ - 2, 1)
            low(E - 1, NQ - 1, NI - 1)
            for t in range(TQ):
                dve.wait_ge(s["down"], 2 * (NQ * E - 1) + t + 1)
                n = TQ * (NQ - 1) + t
                dve.scalar_tensor_tensor(rows[:, n, :], LAST_DOWN[t][:, 0:D], comb[:, n, E - 1:E], rows[:, n, :],
                                         ALU.mult, ALU.add).then_inc(s["y"], 1)

        @block.tensor
        def _(pe):
            def down(e, p, q, d):
                u = NQ * e + q
                if d == 0:
                    need(pe, "a_lo", u, per=NI)
                pe.wait_ge(weights.low, PIECES * e + PIECES)
                need(pe, "y", u, back=1, per=TQ, i=2 * d + 1)
                for i in range(2):
                    r = slice((2 * d + i) * P, (2 * d + i + 1) * P)
                    for k in range(NI):
                        for n, (x, y) in enumerate(hi_lo_products(a_hi[q % 2], a_lo[q % 2], dn_hi[p], dn_lo[p])):
                            mm = pe.matmul(ps_d[d][:, i * D:(i + 1) * D], x[:, k, r], y[:, k, :],
                                           start=k == 0 and n == 0, stop=k == NI - 1 and n == 2)
                mm.then_inc(s["down"], 1)

            def chunk(e, p, q, ahead=None):
                start = isinstance(e, int) and e == 0 and q == 0
                before = (e, p, q - 1) if q else (e - 1, 1 - p, NQ - 1)
                g = bias_group(e, q)
                if q == 0:
                    pe.wait_ge(weights.low, PIECES * e + NI)
                r = slice(q * TC, (q + 1) * TC)
                for it in range(NI):
                    w, v = WS * e + (NI * q + it), it % 2
                    for bank, made, free, o in ((ps_g, "gu_g", "gate", 0), (ps_u, "gu_u", "up", I)):
                        need(pe, free, w, back=2)
                        c = slice(o + it * P, o + (it + 1) * P)
                        i = 0
                        for k in range(DK):
                            for x, y in hi_lo_products(gu_hi[p], gu_lo[p], xt_hi, xt_lo):
                                mm = pe.matmul(bank[v][:, :], x[:, k, c], y[:, k, r], start=i == 0, stop=i == 5)
                                i += 1
                        mm.then_inc(s[made], 1)
                    if it >= 2 and not start:
                        down(*before, it - 2)
                    if g is not None and it == 0:
                        turn_weights(g)
                    if g is not None and it == 2:
                        biases(g)

            def turn_weights(g):
                if g == 0:
                    pe.wait_ge(combined, 1)
                else:
                    pe.wait_ge(biased, 2 * g)
                for t in range(4):
                    mm = pe.transpose(ps_c[0:E, t * P:(t + 1) * P], comb[:, 4 * g + t, :], ident[:, :])
                mm.then_inc(ct_done, 1)

            def biases(g):
                if g == 0:
                    pe.wait_ge(dnb_landed, 16)
                pe.wait_ge(ct_copied, g + 1)
                for t in range(4):
                    mm = pe.matmul((ps_b, ps_c)[t // 2][:, t % 2 * D:(t % 2 + 1) * D], comb_t[:, t * P:(t + 1) * P],
                                   dnb[:, :], start=True, stop=True)
                mm.then_inc(bias_done, 1)

            schedule(pe, chunk)
            u = NQ * E - 1
            need(pe, "y", u, back=1, per=TQ)
            need(pe, "gate", u, per=NI)
            need(pe, "up", u, per=NI)
            v = (NQ - 1) % 2
            for k in range(NI):
                need(pe, "a_lo", u, per=NI, i=k)
                for t in range(TQ):
                    for n, (x, y) in enumerate(hi_lo_products(a_hi[v], a_lo[v], dn_hi[1], dn_lo[1])):
                        mm = pe.matmul(LAST_DOWN[t][:, 0:D], x[:, k, t * P:(t + 1) * P], y[:, k, :],
                                       start=k == 0 and n == 0, stop=k == NI - 1 and n == 2)
                    if k == NI - 1:
                        mm.then_inc(s["down"], 1)


def program(nc, io, out):
    NTILE = ROWS // P
    with ExitStack() as outer:
        def sb(name, shape, dt=F32):
            return outer.enter_context(nc.sbuf_tensor(name, shape, dt))

        ident = sb("ident", [P, P])
        rows = sb("rows", [P, NTILE, D])
        mean = sb("mean", [P, NTILE])
        rstd = sb("rstd", [P, NTILE])
        stage = sb("stage", [P, 2, CT, 2 * NT])
        halves = sb("halves", [P, 4, CT, 2 * NT], F32R)
        attention_weights = AttentionWeights(nc, outer, io, stage, halves, ident)
        norms = RowNorms(nc, outer, rows, mean, rstd)
        cross_attention(nc, io, rows, mean, rstd, ident, stage, halves, attention_weights, norms)
        xt_hi = sb("xt_hi", [P, DK, ROWS], F32R)
        xt_lo = sb("xt_lo", [P, DK, ROWS], F32R)
        logits = sb("logits", [P, NTILE, E])
        weights = ExpertWeights(nc, outer, io)
        latent_attention(nc, io, rows, mean, rstd, ident, attention_weights, norms, xt_hi, xt_lo, logits, weights)
        experts(nc, io, rows, xt_hi, xt_lo, logits, ident, weights, stage, out)


def lay_out(inputs):
    import numpy as np
    a = {k: np.asarray(v) for k, v in inputs.items()}
    xa, la, ff = "L0_xattn_", "L0_attn_", "L0_ffn_"
    ctx = np.zeros((B, NBLK, BF), np.float32)
    ctx.reshape(B, NBLK * STRIDE, D)[:, :CTX] = a["ctx_1024"]
    t = ctx[:, :NT].reshape(PAIRS, 2, NT, CH, CT, P).transpose(0, 3, 5, 4, 1, 2).reshape(PAIRS, CH, P, CT, 2 * NT)
    col = [a[la + "bq"]] + [np.repeat(a[la + f"g{i}"], HD) for i in (1, 3, 4, 2)] + [a[la + "ln_g"], a[la + "ln_b"]]
    io = {"x": a["x"], "ctxN": ctx, "ctxT": t, "qa_qT": a[xa + "qa_q"].T, "qa_wk": a[xa + "qa_wk"],
          "qa_wvT": a[xa + "qa_wv"].T, "ws_w": a[xa + "ws_w"], "mn_w": a[xa + "mn_w"], "hn_w": a[xa + "hn_w"],
          "bias": np.concatenate([a[la + n] for n in ("bk2", "bv2", "bk1", "bv1", "bo")]
                                 + [a[ff + "router_bias"]])[None],
          "cols": np.stack(col).reshape(7, DK, P).transpose(2, 0, 1), "router_w": a[ff + "router_weight"].T}
    io |= {"W" + n: a[la + "W" + n].T for n in ("q", "k1", "v1", "k2", "v2", "o")}
    io |= {"gu": a[ff + "gate_up_proj"].transpose(0, 2, 1), "dn": a[ff + "down_proj"].transpose(0, 2, 1),
           "gub": a[ff + "gate_up_proj_bias"].reshape(E, 2 * I // P, P).transpose(0, 2, 1),
           "dnb": a[ff + "down_proj_bias"]}
    return {k: np.ascontiguousarray(v) for k, v in io.items()}


def kernel(**inputs):
    import concourse.bacc as bacc
    from concourse.bass_utils import run_bass_kernel_spmd

    arrays = lay_out(inputs)
    nc = bacc.Bacc("TRN2", target_bir_lowering=False, num_devices=1)
    io = {k: nc.dram_tensor(k, v.shape, F32, kind="ExternalInput").ap() for k, v in arrays.items()}
    out = nc.dram_tensor("out", (B, S, D), F32, kind="ExternalOutput").ap()
    program(nc, io, out)
    return run_bass_kernel_spmd(nc, [arrays], core_ids=[0]).results[0]["out"]
```
